# Optimizing a Trainium2 kernel written in Bass

```python
import numpy as np
import jax
import jax.numpy as jnp

def _softmax(x, axis=-1):
    return jax.nn.softmax(x, axis=axis)

def _gelu(x):
    return jax.nn.gelu(x, approximate=True)

def _silu(x):
    return jax.nn.silu(x)

def _sigmoid(x):
    return jax.nn.sigmoid(x)

def _layernorm(x, axis=-1, eps=1e-05):
    m = jnp.mean(x, axis=axis, keepdims=True)
    v = jnp.var(x, axis=axis, keepdims=True)
    return (x - m) / jnp.sqrt(v + eps)

def _scatter_add(tgt, idx, src, axis=0):
    return tgt.at[idx].add(src)

def _segment_sum(src, seg, n):
    return jax.ops.segment_sum(src, seg, n)
kernel_name = 'mk_xattn_ffn_d2_seqx_r8_c9b1b0'

def setup_inputs(seed: int=0):
    np.random.seed(seed)
    _w = jnp.asarray

    def _rec_inputs():
        import jax
        import jax.numpy as jnp
        _rk = jax.random.key(seed)
        x = 7.22e-05 + 1 * jax.random.normal(jax.random.fold_in(_rk, 1), (4, 512, 128), jnp.float32)
        _lenS = 512 - jax.random.randint(jax.random.fold_in(_rk, 7), (4,), 0, max(1, 512 // 4) + 1, jnp.int32)
        _lenS2 = 77 - jax.random.randint(jax.random.fold_in(_rk, 8), (4,), 0, max(1, 77 // 4) + 1, jnp.int32)
        _ctx_768P = jax.random.normal(jax.random.fold_in(_rk, 11), (4, 16, 96), jnp.float32)
        _ctx_768c = jax.random.dirichlet(jax.random.fold_in(_rk, 511), 0.3 * jnp.ones((16,), jnp.float32), (4, 77))
        _ctx_768t = jnp.einsum('bsk,bkd->bsd', _ctx_768c, _ctx_768P)
        _ctx_768t = _ctx_768t * jax.lax.rsqrt(jnp.mean(jnp.square(_ctx_768t)) + 1e-12) * 0.953939
        ctx_768 = -0.000191848 + 0.999787 * (_ctx_768t + 0.3 * jax.random.normal(jax.random.fold_in(_rk, 611), (4, 77, 96), jnp.float32))
        return (x, ctx_768)
    x, ctx_768 = _rec_inputs()

    def _L0_xattn_setup():
        import jax, jax.numpy as jnp
        import numpy as np
        NUM_HEADS = 16
        CLAMP = 10000.0
        key = jax.random.key(seed)
        ks = jax.random.split(key, 8)
        B, Nq, Nkv, Cq, Ckv = (4, 256, 256, 128, 96)
        s_q = 1.0 / np.sqrt(Cq)
        s_kv = 1.0 / np.sqrt(Ckv)
        return {'query': jax.random.normal(ks[0], (B, Nq, Cq), jnp.float32), 'key_value': jax.random.normal(ks[1], (B, Nkv, Ckv), jnp.float32), 'Wq': jax.random.normal(ks[2], (Cq, Cq), jnp.float32) * s_q, 'bq': jnp.zeros((Cq,), jnp.float32), 'Wk': jax.random.normal(ks[3], (Ckv, Cq), jnp.float32) * s_kv, 'bk': jnp.zeros((Cq,), jnp.float32), 'Wv': jax.random.normal(ks[4], (Ckv, Cq), jnp.float32) * s_kv, 'bv': jnp.zeros((Cq,), jnp.float32), 'Wo': jax.random.normal(ks[5], (Cq, Cq), jnp.float32) * s_q, 'bo': jnp.zeros((Cq,), jnp.float32)}
    _L0_xattn_all = _L0_xattn_setup()
    _L0_xattn_in = {k: v for k, v in _L0_xattn_all.items() if k in ('Wq', 'bq', 'Wk', 'bk', 'Wv', 'bv', 'Wo', 'bo')}
    del _L0_xattn_all

    def _L0_ffn_setup():
        import jax, jax.numpy as jnp
        import numpy as np
        D_MODEL = 128
        EXPERT_DIM = 64
        N_EXPERTS = 8
        TOP_K = 2

        def _sq_relu(h):
            return jnp.square(jax.nn.relu(h))
        key = jax.random.key(seed)
        ks = jax.random.split(key, 6)
        s = 0.02
        x = jax.random.normal(ks[0], (2, 256, D_MODEL), dtype=jnp.float32)
        Ws1 = jax.random.normal(ks[1], (D_MODEL, EXPERT_DIM), dtype=jnp.float32) * s
        Ws2 = jax.random.normal(ks[2], (EXPERT_DIM, D_MODEL), dtype=jnp.float32) * s
        W1 = jax.random.normal(ks[3], (N_EXPERTS, D_MODEL, EXPERT_DIM), dtype=jnp.float32) * s
        W2 = jax.random.normal(ks[4], (N_EXPERTS, EXPERT_DIM, D_MODEL), dtype=jnp.float32) * s
        Wr = jax.random.normal(ks[5], (D_MODEL, N_EXPERTS), dtype=jnp.float32) * s
        return {'x': x, 'Ws1': Ws1, 'Ws2': Ws2, 'W1': W1, 'W2': W2, 'Wr': Wr}
    _L0_ffn_all = _L0_ffn_setup()
    _L0_ffn_in = {k: v for k, v in _L0_ffn_all.items() if k in ('Ws1', 'Ws2', 'W1', 'W2', 'Wr')}
    del _L0_ffn_all

    def _L1_xattn_setup():
        import jax, jax.numpy as jnp
        import numpy as np
        B, LQ, LK = (4, 256, 256)
        D1, D2, H = (128, 96, 128)
        key = jax.random.key(seed)
        ks = jax.random.split(key, 9)
        s1, s2, sh = (1.0 / np.sqrt(D1), 1.0 / np.sqrt(D2), 1.0 / np.sqrt(H))
        return {'query': jax.random.normal(ks[0], (B, LQ, D1), jnp.float32), 'key': jax.random.normal(ks[1], (B, LK, D2), jnp.float32), 'value': jax.random.normal(ks[2], (B, LK, D2), jnp.float32), 'Wq': jax.random.normal(ks[3], (D1, H), jnp.float32) * s1, 'bq': jax.random.normal(ks[4], (H,), jnp.float32) * s1, 'Wk': jax.random.normal(ks[5], (D2, H), jnp.float32) * s2, 'bk': jax.random.normal(ks[6], (H,), jnp.float32) * s2, 'Wv': jax.random.normal(ks[7], (D2, H), jnp.float32) * s2, 'bv': jax.random.normal(ks[8], (H,), jnp.float32) * s2}
    _L1_xattn_all = _L1_xattn_setup()
    _L1_xattn_in = {k: v for k, v in _L1_xattn_all.items() if k in ('Wq', 'bq', 'Wk', 'bk', 'Wv', 'bv')}
    del _L1_xattn_all

    def _L1_ffn_setup():
        import jax, jax.numpy as jnp
        import numpy as np
        CAPACITY_FACTOR = 1.0
        key = jax.random.key(seed)
        ks = jax.random.split(key, 5)
        B, S, D, E, F = (2, 256, 128, 8, 512)
        x = jax.random.normal(ks[0], (B, S, D), dtype=jnp.float32)
        Ws = jax.random.normal(ks[1], (D, E), dtype=jnp.float32) * (1.0 / np.sqrt(D))
        bs = jnp.zeros((E,), dtype=jnp.float32)
        W1 = jax.random.normal(ks[2], (E, D, F), dtype=jnp.float32) * (1.0 / np.sqrt(D))
        b1 = jnp.zeros((E, F), dtype=jnp.float32)
        W2 = jax.random.normal(ks[3], (E, F, D), dtype=jnp.float32) * (1.0 / np.sqrt(F))
        b2 = jnp.zeros((E, D), dtype=jnp.float32)
        return {'x': x, 'Ws': Ws, 'bs': bs, 'W1': W1, 'b1': b1, 'W2': W2, 'b2': b2}
    _L1_ffn_all = _L1_ffn_setup()
    _L1_ffn_in = {k: v for k, v in _L1_ffn_all.items() if k in ('Ws', 'bs', 'W1', 'b1', 'W2', 'b2')}
    del _L1_ffn_all
    return {'x': x, 'ctx_768': ctx_768, 'L0_xattn_Wq': _L0_xattn_in['Wq'], 'L0_xattn_bq': _L0_xattn_in['bq'], 'L0_xattn_Wk': _L0_xattn_in['Wk'], 'L0_xattn_bk': _L0_xattn_in['bk'], 'L0_xattn_Wv': _L0_xattn_in['Wv'], 'L0_xattn_bv': _L0_xattn_in['bv'], 'L0_xattn_Wo': _L0_xattn_in['Wo'], 'L0_xattn_bo': _L0_xattn_in['bo'], 'L0_ffn_Ws1': _L0_ffn_in['Ws1'], 'L0_ffn_Ws2': _L0_ffn_in['Ws2'], 'L0_ffn_W1': _L0_ffn_in['W1'], 'L0_ffn_W2': _L0_ffn_in['W2'], 'L0_ffn_Wr': _L0_ffn_in['Wr'], 'L1_xattn_Wq': _L1_xattn_in['Wq'], 'L1_xattn_bq': _L1_xattn_in['bq'], 'L1_xattn_Wk': _L1_xattn_in['Wk'], 'L1_xattn_bk': _L1_xattn_in['bk'], 'L1_xattn_Wv': _L1_xattn_in['Wv'], 'L1_xattn_bv': _L1_xattn_in['bv'], 'L1_ffn_Ws': _L1_ffn_in['Ws'], 'L1_ffn_bs': _L1_ffn_in['bs'], 'L1_ffn_W1': _L1_ffn_in['W1'], 'L1_ffn_b1': _L1_ffn_in['b1'], 'L1_ffn_W2': _L1_ffn_in['W2'], 'L1_ffn_b2': _L1_ffn_in['b2']}

def reference(x, ctx_768, L0_xattn_Wq, L0_xattn_bq, L0_xattn_Wk, L0_xattn_bk, L0_xattn_Wv, L0_xattn_bv, L0_xattn_Wo, L0_xattn_bo, L0_ffn_Ws1, L0_ffn_Ws2, L0_ffn_W1, L0_ffn_W2, L0_ffn_Wr, L1_xattn_Wq, L1_xattn_bq, L1_xattn_Wk, L1_xattn_bk, L1_xattn_Wv, L1_xattn_bv, L1_ffn_Ws, L1_ffn_bs, L1_ffn_W1, L1_ffn_b1, L1_ffn_W2, L1_ffn_b2):
    import jax
    import jax.numpy as jnp

    def _L0_xattn_ref(query, key_value, Wq, bq, Wk, bk, Wv, bv, Wo, bo):
        import jax, jax.numpy as jnp
        import numpy as np
        NUM_HEADS = 16
        CLAMP = 10000.0
        B, Nq, Cq = query.shape
        Nkv = key_value.shape[1]
        H = NUM_HEADS
        D = Cq // H
        scale = D ** (-0.5)
        q = (query @ Wq + bq).reshape(B, Nq, H, D).transpose(0, 2, 1, 3)
        k = (key_value @ Wk + bk).reshape(B, Nkv, H, D).transpose(0, 2, 1, 3)
        v = (key_value @ Wv + bv).reshape(B, Nkv, H, D).transpose(0, 2, 1, 3)
        attn = jnp.einsum('bhqd,bhkd->bhqk', q, k) * scale
        attn = jnp.clip(attn, -CLAMP, CLAMP)
        attn = jax.nn.softmax(attn, axis=-1)
        attn = jnp.where(jnp.any(jnp.isnan(attn)), jnp.asarray(1.0 / Nkv, attn.dtype), attn)
        x = jnp.einsum('bhqk,bhkd->bqhd', attn, v).reshape(B, Nq, Cq)
        return x @ Wo + bo

    def _L0_ffn_ref(x, Ws1, Ws2, W1, W2, Wr):
        import jax, jax.numpy as jnp
        import numpy as np
        D_MODEL = 128
        EXPERT_DIM = 64
        N_EXPERTS = 8
        TOP_K = 2

        def _sq_relu(h):
            return jnp.square(jax.nn.relu(h))
        shape = x.shape
        xf = x.reshape(-1, D_MODEL)
        out_shared = _sq_relu(xf @ Ws1) @ Ws2
        logits = xf @ Wr
        top_vals, top_idx = jax.lax.top_k(logits, TOP_K)
        rw = jax.nn.softmax(top_vals.astype(jnp.float32), axis=-1).astype(x.dtype)
        onehot = jax.nn.one_hot(top_idx, N_EXPERTS, dtype=x.dtype)
        prob = jnp.einsum('tk,tke->te', rw, onehot)
        prob = jnp.trunc(prob)
        h = _sq_relu(jnp.einsum('td,edf->tef', xf, W1))
        y = jnp.einsum('tef,efd->ted', h, W2)
        out_routed = jnp.einsum('ted,te->td', y, prob)
        return (out_shared + out_routed).reshape(shape)

    def _L1_xattn_ref(query, key, value, Wq, bq, Wk, bk, Wv, bv):
        import jax, jax.numpy as jnp
        import numpy as np
        B, LQ, LK = (4, 256, 256)
        D1, D2, H = (128, 96, 128)
        q = jnp.einsum('bqd,dh->bqh', query, Wq) + bq
        k = jnp.einsum('bkd,dh->bkh', key, Wk) + bk
        v = jnp.einsum('bkd,dh->bkh', value, Wv) + bv
        scores = jnp.einsum('bqh,bkh->bqk', q, k)
        weights = jax.nn.softmax(scores, axis=-1)
        return jnp.einsum('bqk,bkh->bqh', weights, v)

    def _L1_ffn_ref(x, Ws, bs, W1, b1, W2, b2):
        import jax, jax.numpy as jnp
        import numpy as np
        CAPACITY_FACTOR = 1.0
        B, S, D = x.shape
        E = Ws.shape[1]
        N = B * S
        k = int(CAPACITY_FACTOR * N / E)
        xf = x.reshape(N, D)
        route_prob = jax.nn.softmax(xf @ Ws + bs, axis=-1).T
        route_vals, routes = jax.lax.top_k(route_prob, k)
        xin = xf[routes]
        h = jax.nn.gelu(jnp.einsum('ekd,edf->ekf', xin, W1) + b1[:, None, :])
        out = jnp.einsum('ekf,efd->ekd', h, W2) + b2[:, None, :]
        out = out * route_vals[..., None]
        final = jnp.zeros((N, D), dtype=x.dtype).at[routes.reshape(-1)].add(out.reshape(-1, D))
        return final.reshape(B, S, D)
    x = x + _L0_xattn_ref(_layernorm(x, axis=-1), ctx_768, L0_xattn_Wq, L0_xattn_bq, L0_xattn_Wk, L0_xattn_bk, L0_xattn_Wv, L0_xattn_bv, L0_xattn_Wo, L0_xattn_bo)
    x = x + _L0_ffn_ref(_layernorm(x, axis=-1), L0_ffn_Ws1, L0_ffn_Ws2, L0_ffn_W1, L0_ffn_W2, L0_ffn_Wr)
    x = x + _L1_xattn_ref(_layernorm(x, axis=-1), ctx_768, ctx_768, L1_xattn_Wq, L1_xattn_bq, L1_xattn_Wk, L1_xattn_bk, L1_xattn_Wv, L1_xattn_bv)
    x = x + _L1_ffn_ref(_layernorm(x, axis=-1), L1_ffn_Ws, L1_ffn_bs, L1_ffn_W1, L1_ffn_b1, L1_ffn_W2, L1_ffn_b2)
    return x

_drawn_inputs = setup_inputs


def setup_inputs(seed=0):
    import zlib

    import numpy as np

    out = dict(_drawn_inputs(seed))
    spreads = {'L0_xattn_bq': (0.0, 0.1),
     'L0_xattn_bk': (0.0, 0.8),
     'L0_xattn_bv': (0.0, 0.1),
     'L0_xattn_bo': (0.0, 0.1),
     'L1_ffn_bs': (0.0, 0.328),
     'L1_ffn_b1': (0.0, 0.458),
     'L1_ffn_b2': (0.0, 0.301)}
    factors = {'L0_ffn_Ws1': 3.21, 'L0_ffn_Ws2': 3.133, 'L1_xattn_bk': 8.0}
    for name, (base, spread) in spreads.items():
        noise = np.random.default_rng([zlib.crc32(name.encode()), seed]).standard_normal(out[name].shape)
        drawn = base * np.exp(spread * noise) if base else spread * noise
        out[name] = jnp.asarray(drawn.astype(out[name].dtype))
    for name, factor in factors.items():
        out[name] = (out[name] * factor).astype(out[name].dtype)
    return out
```

```python
from contextlib import ExitStack

import numpy as np

import concourse.bass as bass
from concourse import mybir

F32 = mybir.dt.float32
BF16 = mybir.dt.bfloat16
F16 = mybir.dt.float16
I32 = mybir.dt.int32
U16 = mybir.dt.uint16
ALU = mybir.AluOpType
ACT = mybir.ActivationFunctionType
X = mybir.AxisListType.X

P = 128
B, T, D = 4, 512, 128
J = T // P
NT = B * J
NK, DC = 77, 96
H = 16
HD = D // H
HK = H * NK
CH = -(-HK // P)
HC = 3
E, F = 8, 512
FC = F // P
CAP = B * T // E
SH = CAP // P
F0 = 64
EPS = 1e-5
CLAMP = 1e4
ROW = D + E
BITS = 30
HEAD_GROUPS = ((0, 6), (6, 6), (12, 4))
FAST, SLOTS = 2, 10


def chunk_rows(i):
    return min(P, HK - i * P)


def chunk_head(i):
    return min(i * P // NK, H - HC)


def constants():
    r = np.arange(P)
    ident = np.eye(P, dtype=np.float32)
    head_mask = (r[:, None] // HD == np.arange(H)[None]).astype(np.float32)
    rows = np.arange(CH)[None, :, None] * P + r[:, None, None]
    heads = np.array([[chunk_head(i) + l for l in range(HC)] for i in range(CH)])
    value_mask = ((rows // NK == heads[None]) & (rows < HK)).astype(np.float32).reshape(P, CH * HC)
    slot = np.stack([r + P * s for s in range(SH)], 1).astype(np.float32)
    c32 = np.concatenate([ident, head_mask, value_mask, slot], 1)
    prefix = (r[:, None] <= r[None]).astype(np.float32)
    same = r[:, None] // NT == r[None] // NT
    before = (same & (r[:, None] % NT < r[None] % NT)).astype(np.float32)
    ones = np.ones((P, P), np.float32)
    slots = np.broadcast_to(np.arange(CAP, dtype=np.float32), (P, CAP))
    neg = np.zeros((P, HK), np.float32)
    neg[:H] = -1.0 * (np.arange(HK)[None] // NK == np.arange(H)[:, None])
    c16 = np.ascontiguousarray(np.concatenate([ident, prefix, before, ones, slots, neg], 1).view(np.uint16)[:, 1::2])
    tau = r % NT
    tile_row = ((tau // J) * T + tau % J).astype(np.float32)
    own = (r[:, None] // NT == np.arange(E)[None]).astype(np.float32)
    crow = (own * tile_row[:, None]).astype(np.float16)
    step = 1 << FAST
    bits = np.array([[k << b for k in range(1, step)] for b in range(BITS - FAST, -1, -FAST)], np.int32)
    cbits = np.broadcast_to(bits.reshape(1, -1), (P, bits.size))
    return {"c_f32": np.concatenate([c32, own], 1).copy(), "c_bf16": c16, "c_rows": crow,
            "c_bits": np.ascontiguousarray(cbits)}


def program(nc, a, out):
    NSTEP = BITS // FAST
    K = (1 << FAST) - 1
    with ExitStack() as ctx:
        def sb(name, shape, dt=F32):
            return ctx.enter_context(nc.sbuf_tensor(name, shape, dt))

        def sem(name):
            return ctx.enter_context(nc.semaphore(name))

        gather_rows = nc.dram_tensor("gather_rows", (B * T, ROW), F32).ap()
        bank = [ctx.enter_context(nc.psum_tensor(f"bank{i}", [P, 512], F32)) for i in range(8)]

        c32 = sb("c32", [P, P + H + CH * HC + SH + E])
        ident = c32[:, 0:P]
        head_mask = c32[:, P:P + H]
        value_mask = c32[:, P + H:P + H + CH * HC]
        slot_no = c32[:, P + H + CH * HC:P + H + CH * HC + SH]
        own = c32[:, P + H + CH * HC + SH:]
        c16 = sb("c16", [P, 4 * P + CAP + HK], BF16)
        ident16, prefix, before, ones16 = (c16[:, i * P:(i + 1) * P] for i in range(4))
        slots16 = c16[:, 4 * P:4 * P + CAP]
        neg_head = c16[0:H, 4 * P + CAP:]
        tile_rows = sb("tile_rows", [P, E], F16)
        bit_steps = sb("bit_steps", [P, NSTEP * K], I32)
        w_kv = sb("w_kv", [DC + 1, 4, D])
        w_q = sb("w_q", [P, 3, D])
        b_q = sb("b_q", [P, 2])
        bo_rows = sb("bo_rows", [P, D])
        w_s1 = sb("w_s1", [P, F0])
        w_s2 = sb("w_s2", [F0, D])
        w_r = sb("w_r", [P, 2, E])
        bs_rows = sb("bs_rows", [P, E])
        w1 = sb("w1", [P, E, F])
        w2 = sb("w2", [P, E, FC, D])
        b1_rows = sb("b1_rows", [E * FC, P])
        b1 = sb("b1", [P, E * FC])
        b2_rows = sb("b2_rows", [P, E, D])

        x = sb("x", [P, NT, D])
        res = sb("res", [P, NT, D])
        ctx_in = sb("ctx_in", [NK, B, DC])
        ctxT = sb("ctxT", [DC + 1, B, 3 * NK])
        kT = sb("kT", [P, B, NK])
        k1T = sb("k1T", [P, B, NK])
        v1 = sb("v1", [NK, B, D])
        kbd = sb("kbd", [P, 2, H, NK])
        v9 = sb("v9", [P, B, CH, HC, HD + 1])
        qT = sb("qT", [P, B, T])
        mrow = sb("mrow", [P, 2, J, H], BF16)
        mT = sb("mT", [H, 2, T], BF16)
        pT = sb("pT", [P, 2, CH, T])
        stats = sb("stats", [P, 4, J, 6])
        mv = sb("mv", [P, 4, J, 2])
        ve = sb("ve", [P, 4, J])
        rstd = sb("rstd", [P, 4, J])
        half_neg = sb("half_neg", [P, J])
        xn = sb("xn", [P, 3, 2, J, D])
        xnT = sb("xnT", [P, 4, 2, T])
        rden = sb("rden", [P, B, J, H])
        reach = sb("reach", [P, B])
        att = sb("att", [P, 2, J, D])
        attT = sb("attT", [P, 2, T])
        hid = sb("hid", [F0, 2, T])
        hid2 = sb("hid2", [F0, 2, T])
        top0 = sb("top0", [P, NT, E])
        q1T = sb("q1T", [P, 2, T])
        p1 = sb("p1", [P, 2, J, NK])
        m1 = sb("m1", [P, 2, J])
        den1 = sb("den1", [P, 2, J])
        r1 = sb("r1", [P, 2, J])
        p1T = sb("p1T", [NK, 2, T])
        xrow = sb("xrow", [P, 2, J, ROW])
        lg = sb("lg", [P, 2, J, E])
        lm = sb("lm", [P, 2, J])
        prob = sb("prob", [P, E, NT])
        zt = sb("zt", [P, 2, K + 1, E])
        cand = sb("cand", [P, K, E])
        ge = sb("ge", [P, K, E, NT], BF16)
        chosen = sb("chosen", [P, E, NT], BF16)
        tot16 = sb("tot16", [P, 1], BF16)
        base = sb("base", [P, 2])
        past = sb("past", [P, CAP], BF16)
        onehot = sb("onehot", [P, CAP], BF16)
        cum = sb("cum", [P, P], BF16)
        cumx = sb("cumx", [P, E, P], BF16)
        le = sb("le", [P, E, P], BF16)
        pcount = sb("pcount", [P, SH, E])
        idx = sb("idx", [P, SH, E], I32)
        xin = pT[:, 0, 0:5, :].rearrange("p a t -> p (a t)")[:, 0:E * SH * ROW].rearrange("p (e s n) -> p e s n", e=E, s=SH)
        xinT = sb("xinT", [P, 2, CAP])
        suspect = sb("suspect", [P, 5])
        scratch = xnT[:, 0, 0, 0:B * J * H]
        suspect16 = sb("suspect16", [P, 1], BF16)
        flag = sb("flag", [1, 1], I32)
        hg = pT[:, 1, 0:4, :].rearrange("p a t -> p (a t)").rearrange("p (u c n) -> p u c n", u=2, c=FC)
        y = pT[:, 1, 4:8, :].rearrange("p a t -> p (a t)").rearrange("p (e s n) -> p e s n", e=E, s=SH)

        S_ps, ST_ps = bank[0:2], bank[2:4]
        tail2_ps, tail1_ps, prep_ps = bank[4], bank[5:7], bank[7]
        logits0 = tail1_ps[0][:, 0:J * E].rearrange("p (j e) -> p j e", j=J)
        logits1 = tail2_ps[:, 0:J * E].rearrange("p (j e) -> p j e", j=J)
        v_ps = prep_ps[:, 0:CH * HC * HD]
        mT_ps = prep_ps[0:H, 0:256].bitcast(BF16)
        O_ps = [t[:, 0:2 * H * (HD + 1)] for t in tail1_ps]

        ld_x = [sem(f"ld_x{b}") for b in range(B)]
        ld_ctx, ld_c32, ld_c16, ld_kv, ld_q, ld_bo = (sem(n) for n in ("ld_ctx", "ld_c32", "ld_c16", "ld_kv", "ld_q", "ld_bo"))
        ld_ffn, ld_rt, ld_rc, ld_b1, ld_b2 = (sem(n) for n in ("ld_ffn", "ld_rt", "ld_rc", "ld_b1", "ld_b2"))
        ld_w = [sem(f"ld_w{e}") for e in range(E)]
        out_base, out_add = sem("out_base"), sem("out_add")
        rows_out = [sem(f"rows_out{b}") for b in range(B)]
        got = [sem(f"got{e}") for e in range(E)]
        ones_set, ctxT_ps_done, ctxT_done = sem("ones_set"), sem("ctxT_ps_done"), sem("ctxT_done")
        kT_ps_done, kT_done, kbd_done = sem("kT_ps_done"), sem("kT_done"), sem("kbd_done")
        v_ps_done, v9_done = sem("v_ps_done"), sem("v9_done")
        k1_ps_done, k1_done, v1_ps_done, v1_done = sem("k1_ps_done"), sem("k1_done"), sem("v1_ps_done"), sem("v1_done")
        b1_ps_done, b1_done = sem("b1_ps_done"), sem("b1_done")
        var_done = [sem(f"var_done{n}") for n in range(4)]
        rstd_done = [sem(f"rstd_done{n}") for n in range(4)]
        xn_done = [sem(f"xn_done{n}") for n in range(4)]
        xnT_ps_done = [sem(f"xnT_ps_done{n}") for n in range(4)]
        xnT_done = [sem(f"xnT_done{n}") for n in range(4)]
        q_ps_done, q_done = sem("q_ps_done"), sem("q_done")
        s_ps_done, max_done, mT_ps_done, mT_done = sem("s_ps_done"), sem("max_done"), sem("mT_ps_done"), sem("mT_done")
        st_ps_done, exp_done = sem("st_ps_done"), sem("exp_done")
        o_ps_done, att_done, attT_ps_done, attT_done = sem("o_ps_done"), sem("att_done"), sem("attT_ps_done"), sem("attT_done")
        wo_ps_done, res1_done, res0_done = sem("wo_ps_done"), sem("res1_done"), sem("res0_done")
        lg0_ps_done, top0_done, hid_ps_done, hid_done, hid2_done = (sem(n) for n in ("lg0_ps_done", "top0_done", "hid_ps_done", "hid_done", "hid2_done"))
        ffn_ps_done, res2_done = sem("ffn_ps_done"), sem("res2_done")
        q1_ps_done, q1_done, s1_ps_done, sub1_done, exp1_done = (sem(n) for n in ("q1_ps_done", "q1_done", "s1_ps_done", "sub1_done", "exp1_done"))
        p1T_ps_done, p1T_done, o1_ps_done, res3_done, r1_done = (sem(n) for n in ("p1T_ps_done", "p1T_done", "o1_ps_done", "res3_done", "r1_done"))
        lg1_ps_done, sub2_done, exp2_done, prob_done = sem("lg1_ps_done"), sem("sub2_done"), sem("exp2_done"), sem("prob_done")
        ge_done, cnt_ps_done = sem("ge_done"), sem("cnt_ps_done")
        chosen_done, pre_ps_done, tot_done, base_ps_done, cumx_done, idx_ps_done, idx_done = (
            sem(n) for n in ("chosen_done", "pre_ps_done", "tot_done", "base_ps_done", "cumx_done", "idx_ps_done", "idx_done"))
        xinT_ps_done, xinT_done, h_ps_done, gelu_done, y_ps_done, y_done = (
            sem(n) for n in ("xinT_ps_done", "xinT_done", "h_ps_done", "gelu_done", "y_ps_done", "y_done"))
        half_set, settled = sem("half_set"), sem("settled")
        suspect_done, flag_ps_done, flag_done, turn = sem("suspect_done"), sem("flag_ps_done"), sem("flag_done"), sem("turn")
        eq_done, rank_ps_done, ld_g = sem("eq_done"), sem("rank_ps_done"), sem("ld_g")
        dve_chain, pool_chain = sem("dve_chain"), sem("pool_chain")

        def tokens(dram, b):
            return dram[b].rearrange("(p j) d -> p j d", j=J)

        PREFIX = (("fetch", 4), ("rstd0", 2), ("norm0", 1), ("turn0", 1), ("turned0", 1), ("query", 1), ("queried", 1), ("score", 3))
        NAN = PREFIX + (("nan", 6),)
        TILE = PREFIX + (
            ("clip", 6), ("exp", 1), ("weigh", 4), ("weights_T", CH), ("weights_copy", 4), ("attend", CH), ("attended", 4),
            ("att_T", 1), ("att_copy", 1), ("project", 1), ("add_att", 3), ("rstd1", 2), ("norm1", 1), ("turn1", 1), ("turned1", 1),
            ("route", 1), ("top", 3), ("route_exp", 1), ("route_weights", 4))
        for n in range(E + 1):
            TILE += ((f"up{n}", 1), (f"relu{n}", 1), (f"square{n}", 1), (f"down{n}", 1), (f"add{n}", 1))
        TILE += (
            ("stats2", 2), ("rstd2", 2), ("norm2", 1), ("turn2", 1), ("turned2", 1), ("query1", 1), ("queried1", 1), ("score1", 1),
            ("shift1", 3), ("exp1", 1), ("weigh1", 3), ("weights1_T", 1), ("weights1_copy", 1), ("attend1", 1), ("add_att1", 3),
            ("rstd3", 2), ("norm3", 1), ("turn3", 1), ("turned3", 1), ("route1", 1), ("shift2", 3), ("exp2", 1), ("share", 8),
            ("store", 32))
        LOADS = 32
        NAN_N, TILE_N = sum(n for _, n in NAN), sum(n for _, n in TILE)
        AFTER_NAN = LOADS + NT * NAN_N
        FLAGGED = 5
        TURNS_ALL = AFTER_NAN + FLAGGED + NT * TILE_N

        class Turns:

            def __init__(self, eng, stages, name, at):
                self.eng, self.at, self.k = eng, at + sum(n for _, n in stages[:[m for m, _ in stages].index(name)]), 0

            def __call__(self, held=True):
                self.eng.wait_ge(turn, self.at + self.k)
                if not held and self.eng is nc.vector:
                    self.eng.memset(idle[:, 0:1], 0.0)
                if not held and self.eng is nc.gpsimd:
                    self.eng.tensor_tensor(idle[:, 1:2], half_neg[:, 0:1], half_neg[:, 0:1], ALU.add)
                self.k += 1

            def end(self, ins):
                ins.then_inc(turn, 1)

        arena0, arena1 = (pT[:, u].rearrange("p c t -> p (c t)") for u in range(2))
        spans = {}
        at = 0
        for name, n in (("w", HK), ("wT", CH * P), ("x", D), ("n", D), ("nT", D), ("q", D), ("att", D), ("h", D),
                        ("v9", CH * HC * (HD + 1)), ("v1", D), ("k1", NK + 1), ("row", ROW), ("stats", 6), ("mv", 2), ("ve", 1),
                        ("rstd", 1), ("m", H), ("den", H), ("lg", E), ("top", E), ("sel", E), ("a", E), ("b", E), ("one", 4)):
            spans[name] = arena0[:, at:at + n]
            at += n
        nan_seen, keep, uniform, finite = (arena1[:, 3000 + n:3001 + n] for n in range(4))
        g_w1 = arena1[:, 0:E * F0]
        g_w2 = arena1[0:F0, E * F0:E * F0 + E * D].rearrange("p (e d) -> p e d", e=E)
        eqb, gtb = (c[:] for c in (sb("eqb", [P, E * B], BF16), sb("gtb", [P, E], BF16)))
        need = sb("need", [P, E])
        idle = sb("idle", [P, 2])
        rank = xnT[:, 1, 0, 0:E * NT].rearrange("p (e t) -> p e t", e=E)

        def start_general(eng):
            if eng is nc.vector:
                eng.wait_ge(out_add, 16 * SH * E)
                eng.memset(finite, 1.0).then_inc(half_set, 1)
                eng.wait_ge(half_set, 2)
            if eng is nc.sync:
                eng.wait_ge(y_done, E)
                eng.wait_ge(out_add, 16 * SH * E)
                eng.dma_start(g_w1.rearrange("p (e f) -> p e f", e=E), a["L0_ffn_W1"].rearrange("e d f -> d e f")).then_inc(turn, 16)
                eng.dma_start(g_w2, a["L0_ffn_W2"].rearrange("e f d -> f e d")).then_inc(ld_g, 16)
                eng.dma_start(bit_steps[:], a["c_bits"]).then_inc(ld_g, 16)
                eng.wait_ge(ld_g, 32)
                eng.wait_ge(turn, 16)
                for _ in range(16):
                    eng.sem_inc(turn, 1)

        def prefix_stages(eng, stages, at, i):
            G = spans
            if eng is nc.vector:
                go = Turns(eng, stages, "fetch", at)
                go(); go.end(eng.tensor_copy(G["x"], x[:, bass.ds(i, 1), :].rearrange("p o d -> p (o d)")))
                go(); go.end(eng.tensor_tensor(kbd[:, 0], kT[:, bass.ds(i // J, 1), :].broadcast_to([P, H, NK]),
                                               head_mask.unsqueeze(2).broadcast_to([P, H, NK]), ALU.mult))
                layer_stats(eng, go)
                go = Turns(eng, stages, "norm0", at)
                normalised(eng, go, G["n"])
                go = Turns(eng, stages, "queried", at)
                go(); go.end(eng.tensor_scalar(G["q"], bank[1][:, 0:P], b_q[:, 0:1], float(HD) ** -0.5, ALU.add, ALU.mult))
            if eng is nc.gpsimd:
                layer_rstd(eng, Turns(eng, stages, "rstd0", at))
            if eng is nc.tensor:
                go = Turns(eng, stages, "turn0", at)
                go(); go.end(eng.transpose(bank[0][:, 0:P], G["n"], ident))
                go = Turns(eng, stages, "query", at)
                go(); go.end(eng.matmul(bank[1][:, 0:P], w_q[:, 0, :], G["nT"], start=True, stop=True))
                go = Turns(eng, stages, "score", at)
                for g, (h0, n) in enumerate(HEAD_GROUPS):
                    go(); go.end(eng.matmul(bank[2 + g][:, 0:n * NK], G["q"], kbd[:, 0, h0:h0 + n, :].rearrange("p h k -> p (h k)"),
                                            start=True, stop=True))
            if eng is nc.scalar:
                go = Turns(eng, stages, "turned0", at)
                go(); go.end(eng.copy(G["nT"], bank[0][:, 0:P]))

        def layer_stats(eng, go):
            go(); go.end(eng.bn_stats(spans["stats"], spans["x"]))
            go(held=False); go.end(eng.bn_aggr(spans["mv"], spans["stats"]))

        def layer_rstd(eng, go):
            go(held=False); go.end(eng.tensor_scalar(spans["ve"], spans["mv"][:, 1:2], EPS, None, ALU.add))
            go(); go.end(eng.tensor_tensor(spans["rstd"], spans["ve"], half_neg[:, 0:1], ALU.pow))

        def normalised(eng, go, to):
            go(); go.end(eng.tensor_scalar(to, spans["x"], spans["mv"][:, 0:1], spans["rstd"], ALU.subtract, ALU.mult))

        def find_nan(eng, i):
            at = LOADS + i * NAN_N
            prefix_stages(eng, NAN, at, i)
            if eng is nc.vector:
                go = Turns(eng, NAN, "nan", at)
                w = spans["w"]
                for g, (h0, n) in enumerate(HEAD_GROUPS):
                    go(); go.end(eng.tensor_copy(w[:, h0 * NK:(h0 + n) * NK], bank[2 + g][:, 0:n * NK]))
                go(); go.end(eng.tensor_tensor(w, w, w, ALU.is_equal))
                go(); go.end(eng.tensor_reduce(spans["one"][:, 0:1], w, X, ALU.min))
                go(); go.end(eng.tensor_tensor(finite, finite, spans["one"][:, 0:1], ALU.min))

        def count_nan(eng):
            if eng is nc.vector:
                eng.wait_ge(turn, AFTER_NAN)
                eng.tensor_scalar(suspect16[:], finite, -1.0, 1.0, ALU.mult, ALU.add).then_inc(turn, 1)
                eng.wait_ge(turn, AFTER_NAN + 2)
                eng.tensor_scalar(nan_seen, bank[0][:, 0:1], 0.5, None, ALU.is_gt).then_inc(turn, 1)
                eng.wait_ge(turn, AFTER_NAN + 3)
                eng.tensor_scalar(keep, nan_seen, -1.0, 1.0, ALU.mult, ALU.add).then_inc(turn, 1)
                eng.wait_ge(turn, AFTER_NAN + 4)
                eng.tensor_scalar(uniform, nan_seen, 1.0 / NK, None, ALU.mult).then_inc(turn, 1)
            if eng is nc.tensor:
                eng.wait_ge(turn, AFTER_NAN + 1)
                eng.matmul(bank[0][:, 0:1], ones16, suspect16[:], start=True, stop=True).then_inc(turn, 1)

        def run_tile(eng, i):
            G = spans
            at = AFTER_NAN + FLAGGED + i * TILE_N
            prefix_stages(eng, TILE, at, i)

            def stage(name):
                return Turns(eng, TILE, name, at)

            if eng is nc.vector:
                heads = G["w"].rearrange("p (h k) -> p h k", h=H)
                go = stage("clip")
                go(); go.end(eng.tensor_copy(G["v9"], v9[:, bass.ds(i // J, 1)].rearrange("p o c l d -> p (o c l d)")))
                for g, (h0, n) in enumerate(HEAD_GROUPS):
                    go(); go.end(eng.tensor_scalar(G["w"][:, h0 * NK:(h0 + n) * NK], bank[2 + g][:, 0:n * NK], -CLAMP, CLAMP, ALU.max, ALU.min))
                go(); go.end(eng.tensor_reduce(G["m"], heads, X, ALU.max))
                go(); go.end(eng.tensor_tensor(heads, heads, G["m"].unsqueeze(2).broadcast_to([P, H, NK]), ALU.subtract))
                go = stage("weigh")
                go(); go.end(eng.tensor_reduce(G["den"], heads, X, ALU.add))
                go(); go.end(eng.reciprocal(G["den"], G["den"]))
                go(); go.end(eng.tensor_tensor(heads, heads, G["den"].unsqueeze(2).broadcast_to([P, H, NK]), ALU.mult))
                go(); go.end(eng.tensor_scalar(G["w"], G["w"], keep, uniform, ALU.mult, ALU.add))
                go = stage("attended")
                go(); go.end(eng.tensor_copy(G["att"].rearrange("p (h d) -> p h d", h=H),
                                             bank[0][:, 0:H * (HD + 1)].rearrange("p (h d) -> p h d", h=H)[:, :, 0:HD]))
                go(); go.end(eng.tensor_copy(G["k1"][:, 0:NK], k1T[:, bass.ds(i // J, 1), :].rearrange("p o k -> p (o k)")))
                go(); go.end(eng.tensor_copy(G["v1"][0:NK, :], v1[:, bass.ds(i // J, 1), :].rearrange("p o k -> p (o k)")))
                go(); go.end(eng.tensor_tensor(G["x"], G["x"], bo_rows[:], ALU.add))
                go = stage("add_att")
                go(); go.end(eng.tensor_tensor(G["x"], bank[0][:, 0:D], G["x"], ALU.add))
                layer_stats(eng, go)
                normalised(eng, stage("norm1"), G["n"])
                go = stage("top")
                go(); go.end(eng.tensor_copy(G["lg"], bank[1][:, 0:E]))
                go(held=False); go.end(eng.max(G["top"], G["lg"]))
                go(); go.end(eng.tensor_tensor(G["a"][:, 0:1], G["top"][:, 1:2], G["top"][:, 0:1], ALU.subtract))
                go = stage("route_weights")
                go(); go.end(eng.tensor_scalar(G["a"][:, 0:1], G["a"][:, 0:1], 1.0, None, ALU.add))
                go(); go.end(eng.reciprocal(G["a"][:, 0:1], G["a"][:, 0:1]))
                go(); go.end(eng.tensor_scalar(G["a"][:, 0:1], G["a"][:, 0:1], 1.0, None, ALU.is_ge))
                go(); go.end(eng.tensor_scalar(G["sel"], G["lg"], G["top"][:, 0:1], G["a"][:, 0:1], ALU.is_ge, ALU.mult))
                for n in range(E + 1):
                    go = stage(f"square{n}")
                    go(); go.end(eng.tensor_tensor(G["h"][0:F0], G["h"][0:F0], G["h"][0:F0], ALU.mult))
                    go = stage(f"add{n}")
                    scale = G["sel"][:, n:n + 1] if n < E else 1.0
                    go(); go.end(eng.scalar_tensor_tensor(G["x"], bank[3][:, 0:D], scale, G["x"], ALU.mult, ALU.add))
                layer_stats(eng, stage("stats2"))
                normalised(eng, stage("norm2"), G["n"])
                go = stage("shift1")
                w1_ = G["w"][:, 0:NK]
                go(); go.end(eng.tensor_copy(w1_, bank[0][:, 0:NK]))
                go(); go.end(eng.tensor_reduce(G["one"][:, 0:1], w1_, X, ALU.max))
                go(); go.end(eng.tensor_scalar(w1_, w1_, G["one"][:, 0:1], None, ALU.subtract))
                go = stage("weigh1")
                go(); go.end(eng.tensor_reduce(G["one"][:, 0:1], w1_, X, ALU.add))
                go(); go.end(eng.reciprocal(G["one"][:, 0:1], G["one"][:, 0:1]))
                go(); go.end(eng.tensor_scalar(w1_, w1_, G["one"][:, 0:1], None, ALU.mult))
                go = stage("add_att1")
                go(); go.end(eng.tensor_tensor(G["x"], bank[0][:, 0:D], G["x"], ALU.add))
                layer_stats(eng, go)
                normalised(eng, stage("norm3"), G["n"])
                go = stage("shift2")
                go(); go.end(eng.tensor_tensor(G["lg"], bank[1][:, 0:E], bs_rows[:], ALU.add))
                go(); go.end(eng.tensor_reduce(G["one"][:, 0:1], G["lg"], X, ALU.max))
                go(); go.end(eng.tensor_scalar(G["lg"], G["lg"], G["one"][:, 0:1], None, ALU.subtract))
                go = stage("share")
                go(); go.end(eng.tensor_reduce(G["one"][:, 0:1], G["lg"], X, ALU.add))
                go(); go.end(eng.reciprocal(G["one"][:, 0:1], G["one"][:, 0:1]))
                go(); go.end(eng.tensor_scalar(G["row"][:, D:ROW], G["lg"], G["one"][:, 0:1], None, ALU.mult))
                go(); go.end(eng.tensor_copy(G["row"][:, 0:D], G["n"]))
                go(); go.end(eng.tensor_tensor(G["a"], G["row"][:, D:ROW], G["row"][:, D:ROW], ALU.is_equal))
                go(); go.end(eng.tensor_scalar(G["a"], G["a"], -1.5, 1.5, ALU.mult, ALU.add))
                go(); go.end(eng.tensor_scalar(G["b"], G["row"][:, D:ROW], 0.0, None, ALU.max))
                go(); go.end(eng.tensor_tensor(prob[:, :, bass.ds(i, 1)], G["a"].unsqueeze(2), G["b"].unsqueeze(2), ALU.add))
            if eng is nc.gpsimd:
                for n in (1, 2, 3):
                    layer_rstd(eng, stage(f"rstd{n}"))
            if eng is nc.tensor:
                go = stage("weights_T")
                for c in range(CH):
                    n = chunk_rows(c)
                    go(); go.end(eng.transpose(bank[5 + c // 4][0:n, (c % 4) * P:(c % 4 + 1) * P], G["w"][:, c * P:c * P + n], ident))
                go = stage("attend")
                wT = G["wT"].rearrange("p (c t) -> p c t", c=CH)
                for c in range(CH):
                    n, h0 = chunk_rows(c), chunk_head(c)
                    go(); go.end(eng.matmul(bank[0][:, h0 * (HD + 1):(h0 + HC) * (HD + 1)], wT[0:n, c, :],
                                            G["v9"].rearrange("p (c n) -> p c n", c=CH)[0:n, c, :], start=(c == 0), stop=(c == CH - 1),
                                            skip_group_check=True))

                def turned(name, b, src, rows=P):
                    go = stage(name)
                    go(); go.end(eng.transpose(bank[b][0:rows, 0:P], src, ident))

                def product(name, to, lhsT, rhs):
                    go = stage(name)
                    go(); go.end(eng.matmul(to, lhsT, rhs, start=True, stop=True))

                turned("att_T", 1, G["att"])
                product("project", bank[0][:, 0:D], G["nT"], w_q[:, 2, :])
                turned("turn1", 0, G["n"])
                product("route", bank[1][:, 0:E], G["nT"], w_r[:, 0, :])
                for n in range(E + 1):
                    product(f"up{n}", bank[2][0:F0, 0:P], g_w1[:, n * F0:(n + 1) * F0] if n < E else w_s1[:], G["nT"])
                    product(f"down{n}", bank[3][:, 0:D], G["h"][0:F0, :], g_w2[:, n, :] if n < E else w_s2[:])
                turned("turn2", 0, G["n"])
                product("query1", bank[1][:, 0:P], w_q[:, 1, :], G["nT"])
                product("score1", bank[0][:, 0:NK], G["q"], G["k1"][:, 0:NK])
                turned("weights1_T", 1, G["w"][:, 0:NK], NK)
                product("attend1", bank[0][:, 0:D], G["wT"][0:NK, 0:P], G["v1"][0:NK, :])
                turned("turn3", 0, G["n"])
                product("route1", bank[1][:, 0:E], G["nT"], w_r[:, 1, :])
            if eng is nc.scalar:
                def one(name, to, src, func=ACT.Copy, **more):
                    go = stage(name)
                    go(); go.end(eng.activation(to, src, func, **more))

                one("exp", G["w"], G["w"], ACT.Exp)
                go = stage("weights_copy")
                wT = G["wT"].rearrange("p (c t) -> p c t", c=CH)
                for c, n in ((0, 4), (4, 4), (8, 1), (9, 1)):
                    rows = chunk_rows(c + n - 1)
                    go(); go.end(eng.copy(wT[0:rows, c:c + n, :].rearrange("p c t -> p (c t)"),
                                          bank[5 + c // 4][0:rows, (c % 4) * P:(c % 4 + n) * P]))
                one("att_copy", G["nT"], bank[1][:, 0:P])
                one("turned1", G["nT"], bank[0][:, 0:P])
                one("route_exp", G["a"][:, 0:1], G["a"][:, 0:1], ACT.Exp)
                for n in range(E + 1):
                    one(f"relu{n}", G["h"][0:F0, :], bank[2][0:F0, 0:P], ACT.Relu)
                one("turned2", G["nT"], bank[0][:, 0:P])
                one("queried1", G["q"], bank[1][:, 0:P], ACT.Identity, bias=b_q[:, 1:2])
                one("exp1", G["w"][:, 0:NK], G["w"][:, 0:NK], ACT.Exp)
                one("weights1_copy", G["wT"][0:NK, 0:P], bank[1][0:NK, 0:P])
                one("turned3", G["nT"], bank[0][:, 0:P])
                one("exp2", G["lg"], G["lg"], ACT.Exp)
            if eng is nc.sync:
                go = stage("store")
                go()
                eng.dma_start(out.rearrange("b (p j) d -> p b j d", j=J)[:, bass.ds(i // J, 1), bass.ds(i % J, 1), :],
                              G["x"].rearrange("p (a b d) -> p a b d", a=1, b=1)).then_inc(turn, 16)
                eng.dma_start(gather_rows.rearrange("(b p j) n -> p b j n", b=B, j=J)[:, bass.ds(i // J, 1), bass.ds(i % J, 1), :],
                              G["row"].rearrange("p (a b d) -> p a b d", a=1, b=1)).then_inc(turn, 16)
        block = ctx.enter_context(nc.Block())

        @block.sync
        def _(sp):
            sp.dma_start(x[:, 0:J, :], tokens(a["x"], 0)).then_inc(ld_x[0], 16)
            sp.dma_start(c32[:], a["c_f32"]).then_inc(ld_c32, 16)
            for b in range(1, B):
                sp.dma_start(x[:, b * J:(b + 1) * J, :], tokens(a["x"], b)).then_inc(ld_x[b], 16)
            sp.dma_start(bo_rows[:], a["L0_xattn_bo"].rearrange("(o d) -> o d", o=1).broadcast_to([P, D])).then_inc(ld_bo, 16)
            sp.dma_start(w_s1[:], a["L0_ffn_Ws1"]).then_inc(ld_ffn, 16)
            sp.dma_start(w_s2[:], a["L0_ffn_Ws2"]).then_inc(ld_ffn, 16)
            sp.dma_start(w_r[:, 0, :], a["L0_ffn_Wr"]).then_inc(ld_rt, 16)
            sp.dma_start(w_r[:, 1, :], a["L1_ffn_Ws"]).then_inc(ld_rt, 16)
            sp.dma_start(bs_rows[:], a["L1_ffn_bs"].rearrange("(o d) -> o d", o=1).broadcast_to([P, E])).then_inc(ld_rt, 16)
            sp.dma_start(tile_rows[:], a["c_rows"]).then_inc(ld_rc, 16)
            sp.dma_start(bit_steps[:], a["c_bits"]).then_inc(ld_rc, 16)
            sp.dma_start(b1_rows[:], a["L1_ffn_b1"].rearrange("e (c p) -> (e c) p", p=P)).then_inc(ld_b1, 16)
            sp.dma_start(b2_rows[:], a["L1_ffn_b2"].rearrange("(o e) d -> o e d", o=1).broadcast_to([P, E, D])).then_inc(ld_b2, 16)
            for e in range(E):
                sp.dma_start(w1[:, e, :], a["L1_ffn_W1"][e]).then_inc(ld_w[e], 16)
                sp.dma_start(w2[:, e, :, :], a["L1_ffn_W2"][e].rearrange("(c p) d -> p c d", p=P)).then_inc(ld_w[e], 16)
            for b in range(B):
                sp.wait_ge(res3_done, b + 1)
                sp.dma_start(tokens(out, b), res[:, b * J:(b + 1) * J, :]).then_inc(out_base, 16)
                sp.wait_ge(prob_done, b + 1)
                sp.dma_start(gather_rows[b * T:(b + 1) * T, :].rearrange("(p j) n -> p j n", j=J),
                             xrow[:, b % 2, :, :]).then_inc(rows_out[b], 16)
            sp.wait_ge(out_base, 16 * B)
            sp.wait_ge(flag_done, 1)
            with sp.If(sp.value_load(flag[0:1, 0:1], min_val=0, max_val=1) > 0):
                start_general(sp)
                with sp.Fori(0, NT) as i:
                    run_tile(sp, i)
                sp.wait_ge(turn, TURNS_ALL)

        @block.scalar
        def _(act):
            act.dma_start(ctx_in[:], a["ctx_768"].rearrange("b k c -> k b c")).then_inc(ld_ctx, 16)
            for n, (w, bias) in enumerate((("L0_xattn_Wk", "L0_xattn_bk"), ("L0_xattn_Wv", "L0_xattn_bv"),
                                           ("L1_xattn_Wk", "L1_xattn_bk"), ("L1_xattn_Wv", "L1_xattn_bv"))):
                act.dma_start(w_kv[0:DC, n, :], a[w]).then_inc(ld_kv, 16)
                act.dma_start(w_kv[DC:DC + 1, n, :], a[bias].rearrange("(o d) -> o d", o=1)).then_inc(ld_kv, 16)
            for n, w in enumerate(("L0_xattn_Wq", "L1_xattn_Wq", "L0_xattn_Wo")):
                act.dma_start(w_q[:, n, :], a[w]).then_inc(ld_q, 16)
            act.dma_start(b_q[:, 0:1], a["L0_xattn_bq"].rearrange("(d o) -> d o", o=1)).then_inc(ld_q, 16)
            act.dma_start(b_q[:, 1:2], a["L1_xattn_bq"].rearrange("(d o) -> d o", o=1)).then_inc(ld_q, 16)
            act.dma_start(c16[:].bitcast(U16), a["c_bf16"]).then_inc(ld_c16, 16)

            def copy_T(n, b, ps):
                act.wait_ge(xnT_ps_done[n], b + 1)
                nc.scalar.copy(xnT[:, n, b % 2, :], ps[:, :]).then_inc(xnT_done[n], 1)

            act.wait_ge(ctxT_ps_done, 1)
            act.wait_ge(ones_set, 1)
            for r in range(3):
                ins = nc.scalar.copy(ctxT[0:DC, :, r * NK:(r + 1) * NK],
                                     tail1_ps[1][0:DC, 0:B * NK].rearrange("p (b k) -> p b k", b=B))
            ins.then_inc(ctxT_done, 1)
            act.wait_ge(kT_ps_done, 1)
            nc.scalar.copy(kT[:].rearrange("p b k -> p (b k)"), tail1_ps[0][:, 0:B * NK]).then_inc(kT_done, 1)
            copy_T(0, 0, prep_ps)
            for ph in range(B + 2):
                b = ph
                for s in range(SLOTS):
                    if b < B:
                        act.wait_ge(st_ps_done, b * CH + s + 1)
                        if b >= 2 and s == 0:
                            act.wait_ge(o_ps_done, 2 * (b - 1))
                        n = chunk_rows(s)
                        nc.scalar.activation(pT[0:n, b % 2, s, :], ST_ps[s % 2][0:n, :], ACT.Exp).then_inc(exp_done, 1)
                    if b + 1 < B and s == 0:
                        copy_T(0, b + 1, prep_ps)
                    if b == 0 and s == 3:
                        act.wait_ge(k1_ps_done, 1)
                        nc.scalar.copy(k1T[:].rearrange("p b k -> p (b k)"), tail2_ps[:, 0:B * NK]).then_inc(k1_done, 1)
                    if b == 0 and s == 5:
                        act.wait_ge(v1_ps_done, 1)
                        nc.scalar.copy(v1[:].rearrange("p b k -> p (b k)"), tail2_ps[0:NK, :]).then_inc(v1_done, 1)
                    if b == 0 and s == 7:
                        act.wait_ge(b1_ps_done, 1)
                        nc.scalar.copy(b1[:], tail2_ps[:, 0:E * FC]).then_inc(b1_done, 1)
                    t = ph - 1
                    if 0 <= t < B:
                        if s == 2:
                            act.wait_ge(attT_ps_done, t + 1)
                            nc.scalar.copy(attT[:, t % 2, :], tail1_ps[0][:, :]).then_inc(attT_done, 1)
                        if s == 6:
                            copy_T(1, t, tail1_ps[0])
                        if s == 7:
                            act.wait_ge(hid_ps_done, t + 1)
                            nc.scalar.activation(hid[:, t % 2, :], tail1_ps[1][0:F0, :], ACT.Relu).then_inc(hid_done, 1)
                    t = ph - 2
                    if 0 <= t < B:
                        if s == 0:
                            copy_T(2, t, tail2_ps)
                        if s == 1:
                            act.wait_ge(q1_ps_done, t + 1)
                            nc.scalar.activation(q1T[:, t % 2, :], tail2_ps[:, :], ACT.Identity, bias=b_q[:, 1:2]).then_inc(q1_done, 1)
                        if s == 3:
                            act.wait_ge(sub1_done, t + 1)
                            nc.scalar.activation(p1[:, t % 2], p1[:, t % 2], ACT.Exp).then_inc(exp1_done, 1)
                        if s == 4:
                            act.wait_ge(p1T_ps_done, t + 1)
                            nc.scalar.copy(p1T[:, t % 2, :], tail2_ps[0:NK, :]).then_inc(p1T_done, 1)
                        if s == 8:
                            copy_T(3, t, tail2_ps)
                        if s == 9:
                            act.wait_ge(sub2_done, t + 1)
                            nc.scalar.activation(lg[:, t % 2], lg[:, t % 2], ACT.Exp).then_inc(exp2_done, 1)
            def experts(again):
                for e in range(E):
                    n = again * E + e
                    act.wait_ge(xinT_ps_done, n + 1)
                    nc.scalar.copy(xinT[:, e % 2, :], bank[e % 2][:, 0:CAP]).then_inc(xinT_done, 1)
                    if n >= 2:
                        act.wait_ge(y_ps_done, n - 1)
                    for c in range(FC):
                        act.wait_ge(h_ps_done, n * FC + c + 1)
                        nc.scalar.activation(hg[:, e % 2, c, :], bank[2 + c][:, 0:CAP], ACT.Gelu_apprx_tanh,
                                             bias=b1[:, e * FC + c:e * FC + c + 1]).then_inc(gelu_done, 1)

            act.wait_ge(b1_done, 1)
            experts(0)
            act.wait_ge(flag_done, 1)
            with act.If(act.value_load(flag[0:1, 0:1], min_val=0, max_val=1) > 0):
                with act.Fori(0, NT) as i:
                    find_nan(act, i)
                with act.Fori(0, NT) as i:
                    run_tile(act, i)
                experts(1)

        @block.tensor
        def _(pe):
            def transposes(n, b, ps):
                src = xrow[:, b % 2, :, 0:D] if n == 3 else xn[:, n, b % 2]
                for j in range(J):
                    ins = pe.transpose(ps[:, j * P:(j + 1) * P], src[:, j, :], ident)
                ins.then_inc(xnT_ps_done[n], 1)

            def prep_T(b):
                pe.wait_ge(xn_done[0], b + 1)
                if b >= 1:
                    pe.wait_ge(mT_done, b)
                if b >= 2:
                    pe.wait_ge(v9_done, b - 1)
                transposes(0, b, prep_ps)

            def prep_q(b):
                pe.wait_ge(xnT_done[0], b + 1)
                pe.matmul(prep_ps[:, :], w_q[:, 0, :], xnT[:, 0, b % 2, :], start=True, stop=True).then_inc(q_ps_done, 1)

            def scores(b, j):
                if j == 0:
                    pe.wait_ge(q_done, b + 1)
                    pe.wait_ge(kbd_done, b + 1)
                for g, (h0, n) in enumerate(HEAD_GROUPS):
                    u = (b * J + j) * 3 + g
                    if u >= 2:
                        pe.wait_ge(max_done, u - 1)
                    pe.matmul(S_ps[u % 2][:, 0:n * NK], qT[:, b, j * P:(j + 1) * P],
                              kbd[:, b % 2, h0:h0 + n, :].rearrange("p h k -> p (h k)"), start=True,
                              stop=True).then_inc(s_ps_done, 1)

            def maxima_T(b, j):
                pe.wait_ge(max_done, 3 * (b * J + j + 1))
                if j == 0:
                    pe.wait_ge(v9_done, b)
                ins = pe.transpose(mT_ps[:, j * P:(j + 1) * P], mrow[:, b % 2, j, :], ident16)
                if j == J - 1:
                    ins.then_inc(mT_ps_done, 1)

            def values(b):
                for i in range(CH):
                    n = chunk_rows(i)
                    o = i * P % NK
                    h0 = chunk_head(i)
                    ins = pe.matmul(v_ps[:, i * HC * HD:(i + 1) * HC * HD], ctxT[:, b, o:o + P],
                                    w_kv[:, 1, h0 * HD:(h0 + HC) * HD], start=True, stop=True)
                ins.then_inc(v_ps_done, 1)

            def scores_T(b, i):
                if i == 0:
                    pe.wait_ge(mT_done, b + 1)
                if b * CH + i >= 2:
                    pe.wait_ge(exp_done, b * CH + i - 1)
                n = chunk_rows(i)
                kb = kbd[:, b % 2].rearrange("p h k -> p (h k)")
                pe.matmul(ST_ps[i % 2][0:n, :], kb[:, i * P:i * P + n], qT[:, b, :], start=True, stop=False)
                pe.matmul(ST_ps[i % 2][0:n, :], neg_head[:, i * P:i * P + n], mT[:, b % 2, :], start=False,
                          stop=True).then_inc(st_ps_done, 1)

            def attend(b, pair):
                if pair == 0:
                    pe.wait_ge(exp_done, (b + 1) * CH)
                    pe.wait_ge(v9_done, b + 1)
                    if b >= 1:
                        pe.wait_ge(res2_done, b)
                        pe.wait_ge(top0_done, b)
                for j in (2 * pair, 2 * pair + 1):
                    o = O_ps[pair][:, (j % 2) * H * (HD + 1):(j % 2 + 1) * H * (HD + 1)]
                    for i in range(CH):
                        n = chunk_rows(i)
                        h0 = chunk_head(i)
                        ins = pe.matmul(o[:, h0 * (HD + 1):(h0 + HC) * (HD + 1)], pT[0:n, b % 2, i, j * P:(j + 1) * P],
                                        v9[0:n, b, i].rearrange("p l d -> p (l d)"), start=(i == 0), stop=(i == CH - 1),
                                        skip_group_check=True)
                ins.then_inc(o_ps_done, 1)

            pe.wait_ge(ld_ctx, 16)
            pe.wait_ge(ld_c32, 16)
            for b in range(B):
                ins = pe.transpose(tail1_ps[1][0:DC, b * NK:(b + 1) * NK], ctx_in[:, b, :], ident[0:NK, 0:NK])
            ins.then_inc(ctxT_ps_done, 1)
            prep_T(0)
            pe.wait_ge(ctxT_done, 1)
            pe.wait_ge(ld_kv, 128)
            pe.matmul(tail1_ps[0][:, 0:B * NK], w_kv[:, 0, :], ctxT[:, :, 0:NK], start=True, stop=True).then_inc(kT_ps_done, 1)
            pe.wait_ge(ld_q, 80)
            prep_q(0)
            pe.wait_ge(ld_c16, 16)
            for j in range(J):
                scores(0, j)
                if j >= 1:
                    maxima_T(0, j - 1)
            maxima_T(0, J - 1)

            for ph in range(B + 2):
                b = ph
                for s in range(SLOTS):
                    if b < B:
                        scores_T(b, s)
                        if b + 1 < B:
                            if s == 0:
                                prep_T(b + 1)
                            if s == 1:
                                prep_q(b + 1)
                            if s in (2, 4, 6, 8):
                                scores(b + 1, s // 2 - 1)
                            if s in (3, 5, 7, 9):
                                maxima_T(b + 1, s // 2 - 1)
                        if s == 2:
                            pe.wait_ge(q_done, min(b + 2, B))
                            values(b)
                    if b == 0 and s == 3:
                        pe.wait_ge(kT_done, 1)
                        pe.matmul(tail2_ps[:, 0:B * NK], w_kv[:, 2, :], ctxT[:, :, 0:NK], start=True, stop=True).then_inc(k1_ps_done, 1)
                    if b == 0 and s == 5:
                        pe.wait_ge(k1_done, 1)
                        for c in range(B):
                            ins = pe.matmul(tail2_ps[0:NK, c * D:(c + 1) * D], ctxT[:, c, 0:NK], w_kv[:, 3, :], start=True, stop=True)
                        ins.then_inc(v1_ps_done, 1)
                    if b == 0 and s == 7:
                        pe.wait_ge(v1_done, 1)
                        pe.wait_ge(ld_b1, 16)
                        pe.transpose(tail2_ps[:, 0:E * FC], b1_rows[:], ident[0:E * FC, 0:E * FC]).then_inc(b1_ps_done, 1)
                    t = ph - 1
                    if 0 <= t < B:
                        if s == 0:
                            attend(t, 0)
                        if s == 1:
                            attend(t, 1)
                        if s == 2:
                            pe.wait_ge(att_done, (t + 1) * 2)
                            for j in range(J):
                                ins = pe.transpose(tail1_ps[0][:, j * P:(j + 1) * P], att[:, t % 2, j, :], ident)
                            ins.then_inc(attT_ps_done, 1)
                        if s == 3:
                            pe.wait_ge(attT_done, t + 1)
                            for j in range(J):
                                ins = pe.matmul(tail1_ps[1][:, j * P:(j + 1) * P], attT[:, t % 2, j * P:(j + 1) * P], w_q[:, 2, :],
                                                start=True, stop=True)
                            ins.then_inc(wo_ps_done, 1)
                        if s == 6:
                            pe.wait_ge(xn_done[1], t + 1)
                            transposes(1, t, tail1_ps[0])
                        if s == 7:
                            pe.wait_ge(xnT_done[1], t + 1)
                            if t == 0:
                                pe.wait_ge(ld_ffn, 32)
                                pe.wait_ge(ld_rt, 48)
                            pe.matmul(tail1_ps[1][0:F0, :], w_s1[:], xnT[:, 1, t % 2, :], start=True, stop=True).then_inc(hid_ps_done, 1)
                            for j in range(J):
                                ins = pe.matmul(logits0[:, j, :], xnT[:, 1, t % 2, j * P:(j + 1) * P], w_r[:, 0, :], start=True, stop=True)
                            ins.then_inc(lg0_ps_done, 1)
                        if s == 8:
                            pe.wait_ge(hid2_done, t + 1)
                            for j in range(J):
                                ins = pe.matmul(tail1_ps[1][:, j * P:(j + 1) * P], hid2[:, t % 2, j * P:(j + 1) * P], w_s2[:],
                                                start=True, stop=True)
                            ins.then_inc(ffn_ps_done, 1)
                    t = ph - 2
                    if 0 <= t < B:
                        if s == 0:
                            pe.wait_ge(xn_done[2], t + 1)
                            if t == 0:
                                pe.wait_ge(b1_done, 1)
                            else:
                                pe.wait_ge(sub2_done, t)
                            transposes(2, t, tail2_ps)
                        if s == 1:
                            pe.wait_ge(xnT_done[2], t + 1)
                            pe.matmul(tail2_ps[:, :], w_q[:, 1, :], xnT[:, 2, t % 2, :], start=True, stop=True).then_inc(q1_ps_done, 1)
                        if s == 2:
                            pe.wait_ge(q1_done, t + 1)
                            for j in range(J):
                                ins = pe.matmul(tail2_ps[:, j * NK:(j + 1) * NK], q1T[:, t % 2, j * P:(j + 1) * P], k1T[:, t, :],
                                                start=True, stop=True)
                            ins.then_inc(s1_ps_done, 1)
                        if s == 4:
                            pe.wait_ge(exp1_done, t + 1)
                            for j in range(J):
                                ins = pe.transpose(tail2_ps[0:NK, j * P:(j + 1) * P], p1[:, t % 2, j, :], ident)
                            ins.then_inc(p1T_ps_done, 1)
                        if s == 5:
                            pe.wait_ge(p1T_done, t + 1)
                            for j in range(J):
                                ins = pe.matmul(tail2_ps[:, j * P:(j + 1) * P], p1T[:, t % 2, j * P:(j + 1) * P], v1[:, t, :],
                                                start=True, stop=True)
                            ins.then_inc(o1_ps_done, 1)
                        if s == 8:
                            pe.wait_ge(xn_done[3], t + 1)
                            transposes(3, t, tail2_ps)
                        if s == 9:
                            pe.wait_ge(xnT_done[3], t + 1)
                            for j in range(J):
                                ins = pe.matmul(logits1[:, j, :], xnT[:, 3, t % 2, j * P:(j + 1) * P], w_r[:, 1, :], start=True, stop=True)
                            ins.then_inc(lg1_ps_done, 1)

            def threshold(again):
                with pe.Fori(0, NSTEP) as i:
                    pe.wait_ge(ge_done, i + 1 + again * NSTEP)
                    for t in range(NT):
                        ins = pe.matmul(bank[6][:, 0:K * E].rearrange("p (k e) -> p k e", k=K), ones16, ge[:, :, :, t],
                                        start=(t == 0), stop=(t == NT - 1))
                    ins.then_inc(cnt_ps_done, 1)

            def indices(again):
                pe.wait_ge(chosen_done, again + 1)
                pe.matmul(bank[7][:, 0:P], chosen[:].rearrange("p e t -> p (e t)"), prefix, start=True, stop=True).then_inc(pre_ps_done, 1)
                pe.wait_ge(tot_done, again + 1)
                pe.matmul(bank[6][:, 0:1], before, tot16[:], start=True, stop=True).then_inc(base_ps_done, 1)
                pe.wait_ge(cumx_done, again + 1)
                for h in range(SH):
                    oh = onehot[:, h * P:(h + 1) * P]
                    for g in range(2):
                        pe.matmul(bank[2 * h + g][:, :], oh, cumx[:, 4 * g:4 * g + 4, :].rearrange("p e t -> p (e t)"), start=True, stop=True)
                    pe.matmul(bank[4 + h][:, 0:E], oh, tile_rows[:], start=True, stop=True).then_inc(idx_ps_done, 1)

            def experts(again):
                for e in range(E):
                    n = again * E + e
                    pe.wait_ge(got[e], 16 * SH * (again + 1))
                    if e >= 2:
                        pe.wait_ge(xinT_done, n - 1)
                    else:
                        pe.wait_ge(idx_done, again + 1)
                    for h in range(SH):
                        ins = pe.transpose(bank[e % 2][:, h * P:(h + 1) * P], xin[:, e, h, 0:D], ident)
                    ins.then_inc(xinT_ps_done, 1)
                    pe.wait_ge(xinT_done, n + 1)
                    pe.wait_ge(ld_w[e], 32)
                    for c in range(FC):
                        if n >= 1:
                            pe.wait_ge(gelu_done, (n - 1) * FC + c + 1)
                        pe.matmul(bank[2 + c][:, 0:CAP], w1[:, e, c * P:(c + 1) * P], xinT[:, e % 2, :], start=True,
                                  stop=True).then_inc(h_ps_done, 1)
                    if n >= 2:
                        pe.wait_ge(y_done, n - 1)
                    for h in range(SH):
                        for c in range(FC):
                            if h == 0:
                                pe.wait_ge(gelu_done, n * FC + c + 1)
                            ins = pe.matmul(bank[6 + e % 2][:, h * P:(h + 1) * P], hg[:, e % 2, c, h * P:(h + 1) * P], w2[:, e, c, :],
                                            start=(c == 0), stop=(c == FC - 1))
                    ins.then_inc(y_ps_done, 1)

            pe.wait_ge(prob_done, B)
            threshold(0)
            indices(0)
            pe.wait_ge(suspect_done, 1)
            pe.matmul(bank[7][0:1, 0:1], ones16[:, 0:1], suspect16[:], start=True, stop=True).then_inc(flag_ps_done, 1)
            pe.wait_ge(flag_done, 1)
            experts(0)
            with pe.If(pe.value_load(flag[0:1, 0:1], min_val=0, max_val=1) > 0):
                with pe.Fori(0, NT) as i:
                    find_nan(pe, i)
                count_nan(pe)
                with pe.Fori(0, NT) as i:
                    run_tile(pe, i)
                threshold(1)
                pe.wait_ge(eq_done, 1)
                pe.matmul(bank[6][:, 0:E * B], prefix, eqb[:], start=True, stop=True)
                pe.matmul(bank[7][:, 0:E * B], ones16, eqb[:], start=True, stop=True)
                pe.matmul(bank[7][:, E * B:E * B + E], ones16, gtb[:], start=True, stop=True).then_inc(rank_ps_done, 1)
                indices(1)
                experts(1)

        @block.vector
        def _(dve):
            count = [0]

            def settle(ins):
                count[0] += 1
                ins.then_inc(dve_chain, 1)
                dve.wait_ge(dve_chain, count[0])

            def ln_stats(n, src):
                for j in range(J):
                    ins = dve.bn_stats(stats[:, n, j, :], src[:, j, :])
                settle(ins)
                for j in range(J):
                    ins = dve.bn_aggr(mv[:, n, j, :], stats[:, n, j, :])
                ins.then_inc(var_done[n], 1)

            def ln_apply(n, b, src, dst):
                dve.wait_ge(rstd_done[n], b + 1)
                for j in range(J):
                    ins = dve.tensor_scalar(dst[:, j, :], src[:, j, :], mv[:, n, j, 0:1], rstd[:, n, j:j + 1],
                                            ALU.subtract, ALU.mult)
                ins.then_inc(xn_done[n], 1)

            def rtiles(b):
                return res[:, b * J:(b + 1) * J, :]

            def ln0(b):
                src = x[:, b * J:(b + 1) * J, :]
                dve.wait_ge(ld_x[b], 16)
                ln_stats(0, src)
                ln_apply(0, b, src, xn[:, 0, b % 2])

            def q_out(b):
                dve.wait_ge(q_ps_done, b + 1)
                dve.tensor_scalar(qT[:, b, :], prep_ps[:, :], b_q[:, 0:1], float(HD) ** -0.5, ALU.add, ALU.mult).then_inc(q_done, 1)

            def maxima(b, j):
                for g, (h0, n) in enumerate(HEAD_GROUPS):
                    u = (b * J + j) * 3 + g
                    dve.wait_ge(s_ps_done, u + 1)
                    dve.tensor_reduce(mrow[:, b % 2, j, h0:h0 + n], S_ps[u % 2][:, 0:n * NK].rearrange("p (h k) -> p h k", h=n),
                                      X, ALU.max).then_inc(max_done, 1)

            def maxima_out(b):
                dve.wait_ge(mT_ps_done, b + 1)
                dve.tensor_copy(mT[:, b % 2, :], mT_ps).then_inc(mT_done, 1)
                dve.tensor_reduce(reach[:, b:b + 1], mrow[:, b % 2].rearrange("p j h -> p (j h)"), X, ALU.max,
                                  apply_absolute_value=True)

            def values_out(b):
                dve.wait_ge(v_ps_done, b + 1)
                dve.tensor_tensor(v9[:, b, :, :, 0:HD].rearrange("p c l d -> p (c l) d"),
                                  v_ps.rearrange("p (c d) -> p c d", d=HD),
                                  value_mask.unsqueeze(2).broadcast_to([P, CH * HC, HD]), ALU.mult).then_inc(v9_done, 1)

            def normalise(b, pair):
                dve.wait_ge(o_ps_done, 2 * b + pair + 1)
                o = O_ps[pair].rearrange("p (h d) -> p h d", d=HD + 1)
                r = rden[:, b, 2 * pair:2 * pair + 2, :].rearrange("p j h -> p (j h)")
                settle(dve.reciprocal(r, o[:, :, HD]))
                dve.tensor_tensor(att[:, b % 2, 2 * pair:2 * pair + 2, :].rearrange("p j (h d) -> p (j h) d", d=HD), o[:, :, 0:HD],
                                  r.unsqueeze(2).broadcast_to([P, 2 * H, HD]), ALU.mult).then_inc(att_done, 1)

            with nc.allow_low_precision("a shift of the exponent that numerator and denominator share"):
                dve.memset(half_neg[:], -0.5).then_inc(half_set, 1)
                dve.memset(ctxT[DC:DC + 1, :, :], 1.0).then_inc(ones_set, 1)
                ln0(0)
                dve.wait_ge(ld_c32, 16)
                for b in range(B):
                    ins = dve.tensor_copy(v9[:, b, :, :, HD], value_mask.rearrange("p (c l) -> p c l", l=HC))
                dve.wait_ge(ld_q, 80)
                q_out(0)
                ln0(1)
                for j in range(J):
                    maxima(0, j)
                maxima_out(0)
                for ph in range(B + 2):
                    b = ph
                    for s in range(SLOTS):
                        if b + 1 < B:
                            if s == 1:
                                q_out(b + 1)
                            if s in (2, 4, 6, 8):
                                maxima(b + 1, s // 2 - 1)
                            if s == 9:
                                maxima_out(b + 1)
                        if b < B and s == 3:
                            values_out(b)
                        if b + 2 < B and s == 7:
                            ln0(b + 2)
                        t = ph - 1
                        if 0 <= t < B:
                            if s == 0:
                                normalise(t, 0)
                            if s == 1:
                                normalise(t, 1)
                            if s == 3:
                                dve.wait_ge(wo_ps_done, t + 1)
                                dve.wait_ge(res0_done, t + 1)
                                settle(dve.tensor_tensor(rtiles(t), tail1_ps[1][:, :].rearrange("p (j d) -> p j d", j=J), rtiles(t), ALU.add))
                                ln_stats(1, rtiles(t))
                            if s == 5:
                                ln_apply(1, t, rtiles(t), xn[:, 1, t % 2])
                            if s == 8:
                                dve.wait_ge(lg0_ps_done, t + 1)
                                for j in range(J):
                                    ins = dve.max(top0[:, t * J + j, :], logits0[:, j, :])
                                ins.then_inc(top0_done, 1)
                                dve.wait_ge(ffn_ps_done, t + 1)
                                ins = dve.tensor_tensor(rtiles(t), tail1_ps[1][:, :].rearrange("p (j d) -> p j d", j=J), rtiles(t), ALU.add)
                                ins.then_inc(res2_done, 1)
                                dve.wait_ge(res2_done, t + 1)
                                ln_stats(2, rtiles(t))
                            if s == 9:
                                ln_apply(2, t, rtiles(t), xn[:, 2, t % 2])
                        t = ph - 2
                        if 0 <= t < B:
                            if s == 2:
                                dve.wait_ge(s1_ps_done, t + 1)
                                sc = tail2_ps[:, 0:J * NK].rearrange("p (j k) -> p j k", j=J)
                                settle(dve.tensor_reduce(m1[:, t % 2, :], sc, X, ALU.max))
                                dve.tensor_tensor(p1[:, t % 2], sc, m1[:, t % 2].unsqueeze(2).broadcast_to([P, J, NK]),
                                                  ALU.subtract).then_inc(sub1_done, 1)
                            if s == 4:
                                dve.wait_ge(exp1_done, t + 1)
                                settle(dve.tensor_reduce(den1[:, t % 2, :], p1[:, t % 2], X, ALU.add))
                                dve.reciprocal(r1[:, t % 2, :], den1[:, t % 2, :]).then_inc(r1_done, 1)
                            if s == 5:
                                dve.wait_ge(o1_ps_done, t + 1)
                                dve.wait_ge(r1_done, t + 1)
                                for j in range(J):
                                    ins = dve.scalar_tensor_tensor(res[:, t * J + j, :], tail2_ps[:, j * P:(j + 1) * P],
                                                                   r1[:, t % 2, j:j + 1], res[:, t * J + j, :], ALU.mult, ALU.add)
                                ins.then_inc(res3_done, 1)
                                dve.wait_ge(res3_done, t + 1)
                                ln_stats(3, rtiles(t))
                            if s == 7:
                                if t >= 2:
                                    dve.wait_ge(rows_out[t - 2], 16)
                                ln_apply(3, t, rtiles(t), xrow[:, t % 2, :, 0:D])
                            if s == 9:
                                dve.wait_ge(lg1_ps_done, t + 1)
                                l = lg[:, t % 2]
                                if t == 0:
                                    dve.wait_ge(ld_rt, 48)
                                settle(dve.tensor_tensor(l, logits1, bs_rows[:].unsqueeze(1).broadcast_to([P, J, E]), ALU.add))
                                settle(dve.tensor_reduce(lm[:, t % 2, :], l, X, ALU.max))
                                dve.tensor_tensor(l, l, lm[:, t % 2].unsqueeze(2).broadcast_to([P, J, E]),
                                                  ALU.subtract).then_inc(sub2_done, 1)
                                dve.wait_ge(exp2_done, t + 1)
                                settle(dve.tensor_reduce(lm[:, t % 2, :], l, X, ALU.add))
                                settle(dve.reciprocal(lm[:, t % 2, :], lm[:, t % 2, :]))
                                settle(dve.tensor_tensor(xrow[:, t % 2, :, D:ROW], l, lm[:, t % 2].unsqueeze(2).broadcast_to([P, J, E]), ALU.mult))
                                dve.tensor_copy(prob[:, :, t * J:(t + 1) * J].rearrange("p e j -> p j e"),
                                                xrow[:, t % 2, :, D:ROW]).then_inc(prob_done, 1)

                def threshold(again):
                    settle(dve.memset(zt[:, 0, :, :], 0.0))
                    z = zt[:, 0]
                    steps_before = count[0]
                    with dve.Fori(0, NSTEP) as i:
                        n = steps_before + 3 * i
                        dve.tensor_tensor(cand[:].bitcast(I32), z[:, 0, :].bitcast(I32).unsqueeze(1).broadcast_to([P, K, E]),
                                          bit_steps[:, 0:K].unsqueeze(2).broadcast_to([P, K, E]), ALU.bitwise_or).then_inc(dve_chain, 1)
                        dve.wait_ge(dve_chain, n + 1)
                        dve.tensor_tensor(ge[:], prob[:].unsqueeze(1).broadcast_to([P, K, E, NT]),
                                          cand[:].unsqueeze(3).broadcast_to([P, K, E, NT]), ALU.is_ge).then_inc(ge_done, 1)
                        dve.tensor_scalar(bit_steps[:, 0:K], bit_steps[:, 0:K], FAST, None, ALU.logical_shift_right)
                        dve.wait_ge(cnt_ps_done, i + 1 + again * NSTEP)
                        dve.scalar_tensor_tensor(z[:, 1:K + 1, :], bank[6][:, 0:K * E].rearrange("p (k e) -> p k e", k=K),
                                                 CAP - 0.5, cand[:], ALU.is_ge, ALU.mult).then_inc(dve_chain, 1)
                        dve.wait_ge(dve_chain, n + 2)
                        dve.tensor_reduce(zt[:, 1, 0, :], z.rearrange("p k e -> p e k"), X, ALU.max).then_inc(dve_chain, 1)
                        dve.wait_ge(dve_chain, n + 3)
                        dve.tensor_copy(z[:, 0, :], zt[:, 1, 0, :]).then_inc(settled, 1)
                        dve.wait_ge(settled, i + 1 + again * NSTEP)
                    count[0] += 3 * NSTEP

                thr = zt[:, 0, 0, :]

                def indices(again):
                    dve.wait_ge(pre_ps_done, again + 1)
                    dve.tensor_copy(tot16[:], bank[7][:, P - 1:P]).then_inc(tot_done, 1)
                    dve.wait_ge(base_ps_done, again + 1)
                    settle(dve.tensor_copy(base[:, 0:1], bank[6][:, 0:1]))
                    dve.tensor_scalar(cum[:], bank[7][:, 0:P], base[:, 0:1], None, ALU.add)
                    settle(dve.tensor_tensor(base[:, 1:2], bank[7][:, P - 1:P], base[:, 0:1], ALU.add))
                    for e in range(E):
                        dve.tensor_scalar(cumx[:, e, :], cum[:], own[:, e:e + 1], None, ALU.mult)
                    settle(dve.tensor_scalar(past[:], slots16, base[:, 1:2], None, ALU.is_ge))
                    dve.scalar_tensor_tensor(onehot[:], slots16, base[:, 0:1], past[:], ALU.is_ge, ALU.subtract).then_inc(cumx_done, 1)
                    for h in range(SH):
                        dve.wait_ge(idx_ps_done, again * SH + h + 1)
                        for g in range(2):
                            ins = dve.tensor_scalar(le[:, 4 * g:4 * g + 4, :], bank[2 * h + g][:, :].rearrange("p (e t) -> p e t", e=4),
                                                    slot_no[:, h:h + 1], None, ALU.is_le)
                        settle(ins)
                        settle(dve.tensor_reduce(pcount[:, h, :], le[:], X, ALU.add))
                        ins = dve.scalar_tensor_tensor(idx[:, h, :], pcount[:, h, :], float(J), bank[4 + h][:, 0:E],
                                                       ALU.mult, ALU.add)
                    ins.then_inc(idx_done, 1)

                def experts(again):
                    for e in range(E):
                        dve.wait_ge(y_ps_done, again * E + e + 1)
                        settle(dve.tensor_tensor(y[:, e], bank[6 + e % 2][:, 0:CAP].rearrange("p (h d) -> p h d", h=SH),
                                                 b2_rows[:, e, :].unsqueeze(1).broadcast_to([P, SH, D]), ALU.add))
                        dve.tensor_tensor(y[:, e], y[:, e], xin[:, e, :, D + e].unsqueeze(2).broadcast_to([P, SH, D]),
                                          ALU.mult).then_inc(y_done, 1)

                dve.wait_ge(ld_rc, 32)
                dve.wait_ge(prob_done, B)
                threshold(0)
                dve.tensor_tensor(chosen[:], prob[:], thr.unsqueeze(2).broadcast_to([P, E, NT]), ALU.is_ge).then_inc(chosen_done, 1)
                indices(0)

                settle(dve.tensor_reduce(suspect[:, 0:1], reach[:], X, ALU.max))
                settle(dve.tensor_scalar(suspect[:, 0:1], suspect[:, 0:1], 0.98 * CLAMP, None, ALU.is_gt))

                def any_false(ok, column):
                    settle(dve.tensor_reduce(suspect[:, column:column + 1], ok, X, ALU.min))
                    settle(dve.tensor_scalar(suspect[:, column:column + 1], suspect[:, column:column + 1], -1.0, 1.0, ALU.mult, ALU.add))

                r = rden[:].rearrange("p b j h -> p (b j h)")
                settle(dve.tensor_tensor(scratch, r, r, ALU.is_equal))
                any_false(scratch, 1)
                pr = prob[:].rearrange("p e t -> p (e t)")
                settle(dve.tensor_tensor(scratch[:, 0:E * NT], pr, pr, ALU.is_equal))
                any_false(scratch[:, 0:E * NT], 2)
                settle(dve.tensor_tensor(scratch[:, 0:NT], top0[:, :, 0], top0[:, :, 1], ALU.subtract))
                settle(dve.tensor_scalar(scratch[:, 0:NT], scratch[:, 0:NT], 16.0, None, ALU.is_lt))
                any_false(scratch[:, 0:NT], 3)
                settle(dve.tensor_scalar(suspect[:, 4:5], base[:, 1:2], CAP + 0.5, None, ALU.is_gt))
                dve.tensor_reduce(suspect16[:], suspect[:], X, ALU.max).then_inc(suspect_done, 1)
                dve.wait_ge(flag_ps_done, 1)
                dve.tensor_scalar(flag[:], bank[7][0:1, 0:1], 0.5, None, ALU.is_gt).then_inc(flag_done, 1)

                dve.wait_ge(ld_b2, 16)
                experts(0)
                dve.wait_ge(flag_done, 1)
                with dve.If(dve.value_load(flag[0:1, 0:1], min_val=0, max_val=1) > 0):
                    dve.wait_ge(y_ps_done, E)
                    start_general(dve)
                    with dve.Fori(0, NT) as i:
                        find_nan(dve, i)
                    count_nan(dve)
                    with dve.Fori(0, NT) as i:
                        run_tile(dve, i)
                    dve.wait_ge(turn, TURNS_ALL)
                    threshold(1)
                    eq = ge[:, 0]
                    gt = ge[:, 1]
                    settle(dve.tensor_tensor(eq, prob[:], thr.unsqueeze(2).broadcast_to([P, E, NT]), ALU.is_equal))
                    settle(dve.tensor_tensor(gt, prob[:], thr.unsqueeze(2).broadcast_to([P, E, NT]), ALU.is_gt))
                    settle(dve.tensor_reduce(eqb[:].rearrange("p (e b) -> p e b", e=E), eq.rearrange("p e (b j) -> p e b j", b=B), X, ALU.add))
                    dve.tensor_reduce(gtb[:], gt, X, ALU.add).then_inc(eq_done, 1)
                    dve.wait_ge(rank_ps_done, 1)
                    settle(dve.tensor_scalar(need[:], bank[7][:, E * B:E * B + E], -1.0, float(CAP), ALU.mult, ALU.add))
                    eb = eqb[:].rearrange("p (e b) -> p e b", e=E)
                    total = bank[7][:, 0:E * B].rearrange("p (e b) -> p e b", e=E)
                    rk = rank[:].rearrange("p e (b j) -> p e b j", b=B)
                    settle(dve.tensor_tensor(rk[:, :, :, 0], bank[6][:, 0:E * B].rearrange("p (e b) -> p e b", e=E), eb, ALU.subtract))
                    for later in range(1, B):
                        for b in range(later):
                            settle(dve.tensor_tensor(rk[:, :, later, 0], rk[:, :, later, 0], total[:, :, b], ALU.add))
                    for j in range(1, J):
                        settle(dve.tensor_tensor(rk[:, :, :, j], rk[:, :, :, j - 1],
                                                 eq.rearrange("p e (b j) -> p e b j", b=B)[:, :, :, j - 1], ALU.add))
                    settle(dve.tensor_tensor(rank[:], rank[:], need[:].unsqueeze(2).broadcast_to([P, E, NT]), ALU.is_lt))
                    settle(dve.tensor_tensor(rank[:], rank[:], eq, ALU.mult))
                    dve.tensor_tensor(chosen[:], rank[:], gt, ALU.add).then_inc(chosen_done, 1)
                    indices(1)
                    experts(1)

        @block.gpsimd
        def _(pool):
            count = [0]

            def settle(ins):
                count[0] += 1
                ins.then_inc(pool_chain, 1)
                pool.wait_ge(pool_chain, count[0])

            def ln_rstd(n, b):
                pool.wait_ge(var_done[n], b + 1)
                settle(nc.gpsimd.tensor_scalar(ve[:, n, :], mv[:, n, :, 1], EPS, None, ALU.add))
                nc.gpsimd.tensor_tensor(rstd[:, n, :], ve[:, n, :], half_neg[:], ALU.pow).then_inc(rstd_done[n], 1)

            def block_keys(b):
                if b >= 2:
                    pool.wait_ge(st_ps_done, CH * (b - 1))
                nc.gpsimd.tensor_tensor(kbd[:, b % 2], kT[:, b, :].unsqueeze(1).broadcast_to([P, H, NK]),
                                        head_mask.unsqueeze(2).broadcast_to([P, H, NK]), ALU.mult).then_inc(kbd_done, 1)

            def residual(b):
                nc.gpsimd.tensor_tensor(res[:, b * J:(b + 1) * J, :], x[:, b * J:(b + 1) * J, :],
                                        bo_rows[:].unsqueeze(1).broadcast_to([P, J, D]), ALU.add).then_inc(res0_done, 1)

            pool.wait_ge(half_set, 1)
            ln_rstd(0, 0)
            pool.wait_ge(kT_done, 1)
            block_keys(0)
            ln_rstd(0, 1)
            block_keys(1)
            pool.wait_ge(ld_bo, 16)
            residual(0)
            for ph in range(B + 2):
                for s in range(SLOTS):
                    if ph + 1 < B and s == 0:
                        residual(ph + 1)
                        if ph >= 1:
                            block_keys(ph + 1)
                    if ph + 2 < B and s == 7:
                        ln_rstd(0, ph + 2)
                    t = ph - 1
                    if 0 <= t < B:
                        if s == 3:
                            ln_rstd(1, t)
                        if s == 7:
                            pool.wait_ge(hid_done, t + 1)
                            nc.gpsimd.tensor_tensor(hid2[:, t % 2, :], hid[:, t % 2, :], hid[:, t % 2, :], ALU.mult).then_inc(hid2_done, 1)
                        if s == 8:
                            ln_rstd(2, t)
                    t = ph - 2
                    if 0 <= t < B:
                        if s == 5:
                            ln_rstd(3, t)
            flat = out.rearrange("b t d -> (b t) d")

            def experts(again):
                pool.wait_ge(idx_done, again + 1)
                for e in range(E):
                    for h in range(SH):
                        nc.gpsimd.indirect_dma_start(xin[:, e, h, :], None, gather_rows, bass.IndirectOffsetOnAxis(idx[:, h, e:e + 1], 0),
                                                     bounds_check=B * T - 1, oob_is_err=False).then_inc(got[e], 16)
                for e in range(E):
                    n = again * E + e
                    pool.wait_ge(y_done, n + 1)
                    if n >= 1:
                        pool.wait_ge(out_add, 16 * SH * n)
                    for h in range(SH):
                        nc.gpsimd.indirect_dma_start(flat, bass.IndirectOffsetOnAxis(idx[:, h, e:e + 1], 0), y[:, e, h, :], None,
                                                     bounds_check=B * T - 1, oob_is_err=True, compute_op=ALU.add).then_inc(out_add, 16)
                pool.wait_ge(out_add, 16 * SH * E * (again + 1))

            for b in range(B):
                pool.wait_ge(rows_out[b], 16)
            pool.wait_ge(out_base, 16 * B)
            pool.wait_ge(o_ps_done, 2 * B)
            experts(0)
            pool.wait_ge(flag_done, 1)
            with pool.If(pool.value_load(flag[0:1, 0:1], min_val=0, max_val=1) > 0):
                start_general(pool)
                with pool.Fori(0, NT) as i:
                    find_nan(pool, i)
                with pool.Fori(0, NT) as i:
                    run_tile(pool, i)
                experts(1)


_INS = ["x", "ctx_768", "L0_xattn_Wq", "L0_xattn_bq", "L0_xattn_Wk", "L0_xattn_bk", "L0_xattn_Wv", "L0_xattn_bv",
        "L0_xattn_Wo", "L0_xattn_bo", "L0_ffn_Ws1", "L0_ffn_Ws2", "L0_ffn_W1", "L0_ffn_W2", "L0_ffn_Wr",
        "L1_xattn_Wq", "L1_xattn_bq", "L1_xattn_Wk", "L1_xattn_bk", "L1_xattn_Wv", "L1_xattn_bv",
        "L1_ffn_Ws", "L1_ffn_bs", "L1_ffn_W1", "L1_ffn_b1", "L1_ffn_W2", "L1_ffn_b2"]


def kernel(**inputs):
    import concourse.bacc as bacc
    from concourse.bass_utils import run_bass_kernel_spmd

    nc = bacc.Bacc("TRN2", target_bir_lowering=False, num_devices=1)
    arrays, args = {}, {}
    for name, v in [(n, np.ascontiguousarray(inputs[n])) for n in _INS] + list(constants().items()):
        arrays[f"in_{name}"] = v
        args[name] = nc.dram_tensor(f"in_{name}", v.shape, mybir.dt.from_np(v.dtype), kind="ExternalInput").ap()
    out = nc.dram_tensor("out_0", (B, T, D), F32, kind="ExternalOutput").ap()
    program(nc, args, out)
    r = run_bass_kernel_spmd(nc, [arrays], core_ids=[0])
    return r.results[0]["out_0"]
```

```python
from contextlib import ExitStack

import numpy as np

import concourse.bass as bass
from concourse import mybir

F32 = mybir.dt.float32
BF16 = mybir.dt.bfloat16
F16 = mybir.dt.float16
I32 = mybir.dt.int32
U16 = mybir.dt.uint16
ALU = mybir.AluOpType
ACT = mybir.ActivationFunctionType
X = mybir.AxisListType.X

P = 128
B, T, D = 4, 512, 128
J = T // P
NT = B * J
NK, DC = 77, 96
H = 16
HD = D // H
HK = H * NK
G = 4
GH = H // G
GK = GH * NK
GC = -(-GK // P)
CW = -(-GK // GC)
CH = G * GC
WINDOW = max(c * CW % NK for c in range(GC)) + CW
GD = GH * HD
E, F = 8, 512
FC = F // P
CAP = B * T // E
SH = CAP // P
F0 = 64
EPS = 1e-5
CLAMP = 1e4
PART_MAX = 256.0
ROW = D + E
BITS = 30
HEAD_GROUPS = ((0, 6), (6, 6), (12, 4))
FAST, SLOTS = 2, CH


def chunk_rows(c):
    return min(CW, GK - c * CW)


def constants():
    r = np.arange(P)
    ident = np.eye(P, dtype=np.float32)
    head_mask = (r[:, None] // HD == np.arange(H)[None]).astype(np.float32)
    part_mask = (r[:, None] % GD // HD == np.arange(GH)[None]).astype(np.float32)
    rows = np.arange(GC)[None, :, None] * CW + r[:, None, None]
    own_head = (rows // NK == np.arange(GD)[None, None] // HD) & (r[:, None, None] < CW) & (rows < GK)
    value_mask = own_head.astype(np.float32).reshape(P, GC * GD)
    slot = np.stack([r + P * s for s in range(SH)], 1).astype(np.float32)
    c32 = np.concatenate([ident, head_mask, value_mask, slot], 1)
    prefix = (r[:, None] <= r[None]).astype(np.float32)
    same = r[:, None] // NT == r[None] // NT
    before = (same & (r[:, None] % NT < r[None] % NT)).astype(np.float32)
    ones = np.ones((P, P), np.float32)
    same = same.astype(np.float32)
    slots = np.broadcast_to(np.arange(CAP, dtype=np.float32), (P, CAP))
    neg = -1.0 * (np.arange(HK)[None] // NK == np.arange(H)[:, None]).astype(np.float32)
    c16 = np.ascontiguousarray(np.concatenate([ident, prefix, before, ones, same, slots], 1).view(np.uint16)[:, 1::2])
    neg16 = np.ascontiguousarray(neg.view(np.uint16)[:, 1::2])
    tau = r % NT
    tile_row = ((tau // J) * T + tau % J).astype(np.float32)
    own = (r[:, None] // NT == np.arange(E)[None]).astype(np.float32)
    crow = (own * tile_row[:, None]).astype(np.float16)
    step = 1 << FAST
    bits = np.array([[k << b for k in range(1, step)] for b in range(BITS - FAST, -1, -FAST)], np.int32)
    cbits = np.broadcast_to(bits.reshape(1, -1), (P, bits.size))
    return {"c_f32": np.concatenate([c32, own, part_mask], 1).copy(), "c_bf16": c16, "c_neg": neg16, "c_rows": crow,
            "c_bits": np.ascontiguousarray(cbits)}


def program(nc, a, out):
    NSTEP = BITS // FAST
    K = (1 << FAST) - 1
    with ExitStack() as ctx:
        def sb(name, shape, dt=F32):
            return ctx.enter_context(nc.sbuf_tensor(name, shape, dt))

        def sem(name):
            return ctx.enter_context(nc.semaphore(name))

        gather_rows = nc.dram_tensor("gather_rows", (B * T, ROW), F32).ap()
        psum = ctx.enter_context(nc.psum_tensor("psum", [P, 8, 512], F32))
        bank = [psum[:, i, :] for i in range(8)]

        NV = GC * GD
        c32 = sb("c32", [P, P + H + NV + SH + E + GH])
        ident = c32[:, 0:P]
        head_mask = c32[:, P:P + H]
        value_mask = c32[:, P + H:P + H + NV].rearrange("p (c d) -> p c d", c=GC)
        slot_no = c32[:, P + H + NV:P + H + NV + SH]
        own = c32[:, P + H + NV + SH:P + H + NV + SH + E]
        part_mask = c32[:, P + H + NV + SH + E:]
        c16 = sb("c16", [P, 5 * P + CAP], BF16)
        neg_head = sb("neg_head", [P, HK], BF16)
        ident16, prefix, before, ones16, same16 = (c16[:, i * P:(i + 1) * P] for i in range(5))
        slots16 = c16[:, 5 * P:5 * P + CAP]
        tile_rows = sb("tile_rows", [P, E], F16)
        bit_steps = sb("bit_steps", [P, NSTEP * K], I32)
        w_kv = sb("w_kv", [DC + 1, 4, D])
        w_q = sb("w_q", [P, 3, D])
        b_q = sb("b_q", [P, 2])
        bo_rows = sb("bo_rows", [P, D])
        w_s1 = sb("w_s1", [P, F0])
        w_s2 = sb("w_s2", [F0, D])
        w_r = sb("w_r", [P, 2, E])
        bs_rows = sb("bs_rows", [P, E])
        w1 = sb("w1", [P, E, F])
        w2 = sb("w2", [P, E, FC, D])
        b1_rows = sb("b1_rows", [E * FC, P])
        b1 = sb("b1", [P, E * FC])
        b2_rows = sb("b2_rows", [P, E, D])

        x = sb("x", [P, NT, D])
        res = sb("res", [P, NT, D])
        ctx_in = sb("ctx_in", [NK, B, DC])
        ctxT = sb("ctxT", [DC + 1, B, WINDOW])
        kT = sb("kT", [P, B, NK])
        k1T = sb("k1T", [P, B, NK])
        v1 = sb("v1", [NK, B, D])
        w_k4 = sb("w_k4", [DC + 1, G, 4, GD])
        w_q4 = sb("w_q4", [P, G, 4, GD])
        b_q4 = sb("b_q4", [P, G])
        k_parts = sb("k_parts", [P, G, B, NK], F16)
        k_stack = sb("k_stack", [P, B, G, GH, NK], F16)
        q_hi = sb("q_hi", [P, 2, T], F16)
        q_lo = sb("q_lo", [P, 2, T], F16)
        q_stack = sb("q_stack", [P, B, G, T], F16)
        v8 = sb("v8", [P, B, GC, G, GD])
        mrow = sb("mrow", [P, 2, J, H], BF16)
        mT = sb("mT", [P, 2, T], BF16)
        pT = sb("pT", [P, 2, CH, T])
        stats = sb("stats", [P, 4, J, 6])
        mv = sb("mv", [P, 4, J, 2])
        ve = sb("ve", [P, 4, J])
        rstd = sb("rstd", [P, 4, J])
        half_neg = sb("half_neg", [P, J])
        xn = sb("xn", [P, 3, J, D])
        xnT = sb("xnT", [P, 4, T])
        rden = sb("rden", [P, T])
        reach = sb("reach", [P, B])
        attT = sb("attT", [P, T])
        hid = sb("hid", [F0, T])
        hid2 = sb("hid2", [F0, T])
        top0 = sb("top0", [P, NT, E])
        q1T = sb("q1T", [P, T])
        p1 = sb("p1", [P, J, NK])
        m1 = sb("m1", [P, 2, J])
        den1 = sb("den1", [P, 2, J])
        r1 = sb("r1", [P, 2, J])
        p1T = sb("p1T", [NK, T])
        xrow = sb("xrow", [P, 2, J, ROW])
        lg = sb("lg", [P, 2, J, E])
        lm = sb("lm", [P, 2, J])
        prob = sb("prob", [P, E, NT])
        probT = sb("probT", [P, P])
        thr = sb("thr", [P, K + 1])
        cand = sb("cand", [P, K])
        ge = sb("ge", [P, 2, E, NT], BF16)
        chosen = sb("chosen", [P, E, NT], BF16)
        chosenT = sb("chosenT", [P, P], BF16)
        passing = sb("passing", [P, K, P], BF16)
        count16 = sb("count16", [P, K], BF16)
        pre = sb("pre", [P, P], BF16)
        base = sb("base", [P, 2])
        past = sb("past", [P, CAP], BF16)
        onehot = sb("onehot", [P, CAP], BF16)
        cum = sb("cum", [P, P], BF16)
        cumx = sb("cumx", [P, E, P], BF16)
        le = sb("le", [P, SH, E // 2, P], BF16)
        pcount = sb("pcount", [P, SH, E])
        idx = sb("idx", [P, SH, E], I32)
        xin = pT[:, 0, 0:5, :].rearrange("p a t -> p (a t)")[:, 0:E * SH * ROW].rearrange("p (e s n) -> p e s n", e=E, s=SH)
        xinT = sb("xinT", [P, 2, CAP])
        suspect = sb("suspect", [P, 6])
        scratch = xnT[:, 0, 0:E * NT]
        suspect16 = sb("suspect16", [P, 1], BF16)
        flag = sb("flag", [1, 1], I32)
        hg = pT[:, 1, 0:4, :].rearrange("p a t -> p (a t)").rearrange("p (u c n) -> p u c n", u=2, c=FC)
        y = pT[:, 1, 4:8, :].rearrange("p a t -> p (a t)").rearrange("p (e s n) -> p e s n", e=E, s=SH)

        S_ps, ST_ps = bank[0:2], bank[2:4]
        tail2_ps, tail1_ps, prep_ps = bank[4], bank[5:7], bank[7]
        logits0 = tail1_ps[0][:, 0:J * E].rearrange("p (j e) -> p j e", j=J)
        logits1 = tail2_ps[:, 0:J * E].rearrange("p (j e) -> p j e", j=J)
        v_ps = prep_ps[0:CW, 0:GC * D]
        mT_ps = prep_ps[0:H, 0:256].bitcast(BF16)
        O_ps, den_ps = tail1_ps
        k4_ps, q4_ps = psum[:, 0:G, 0:B * NK], psum[:, G:2 * G, :]

        ld_x = [sem(f"ld_x{b}") for b in range(B)]
        ld_ctx, ld_c32, ld_c16, ld_kv, ld_q, ld_bo = (sem(n) for n in ("ld_ctx", "ld_c32", "ld_c16", "ld_kv", "ld_q", "ld_bo"))
        ld_neg, ld_k, ld_q0, ld_bq = sem("ld_neg"), sem("ld_k"), sem("ld_q0"), sem("ld_bq")
        ld_ffn, ld_rt, ld_rc, ld_b1, ld_b2 = (sem(n) for n in ("ld_ffn", "ld_rt", "ld_rc", "ld_b1", "ld_b2"))
        ld_w = [sem(f"ld_w{e}") for e in range(E)]
        out_base, out_add = sem("out_base"), sem("out_add")
        rows_out = [sem(f"rows_out{b}") for b in range(B)]
        got = [sem(f"got{e}") for e in range(E)]
        ones_set, ctxT_ps_done, ctxT_done = sem("ones_set"), sem("ctxT_ps_done"), sem("ctxT_done")
        kT_ps_done, kT_done, w_k4_done, w_q4_done = (sem(n) for n in ("kT_ps_done", "kT_done", "w_k4_done", "w_q4_done"))
        k4_ps_done, k_hi_done, k_lo_done, k_stack_done = (sem(n) for n in ("k4_ps_done", "k_hi_done", "k_lo_done", "k_stack_done"))
        q4_ps_done, q4_hi_done, q4_lo_done, b_q4_done = (sem(n) for n in ("q4_ps_done", "q4_hi_done", "q4_lo_done", "b_q4_done"))
        q_hi_done, q_lo_done = sem("q_hi_done"), sem("q_lo_done")
        q_stack_done = [sem(f"q_stack_done{b}") for b in range(B)]
        v_ps_done, v8_done = sem("v_ps_done"), sem("v8_done")
        k1_ps_done, k1_done, v1_ps_done, v1_done = sem("k1_ps_done"), sem("k1_done"), sem("v1_ps_done"), sem("v1_done")
        b1_ps_done, b1_done = sem("b1_ps_done"), sem("b1_done")
        var_done = [sem(f"var_done{n}") for n in range(4)]
        rstd_done = [sem(f"rstd_done{n}") for n in range(4)]
        xn_done = [sem(f"xn_done{n}") for n in range(4)]
        xnT_ps_done = [sem(f"xnT_ps_done{n}") for n in range(4)]
        xnT_done = [sem(f"xnT_done{n}") for n in range(4)]
        q_ps_done = sem("q_ps_done")
        s_ps_done, max_done, mT_ps_done, mT_done = sem("s_ps_done"), sem("max_done"), sem("mT_ps_done"), sem("mT_done")
        st_ps_done, exp_done = sem("st_ps_done"), sem("exp_done")
        o_ps_done, attT_done = sem("o_ps_done"), sem("attT_done")
        wo_ps_done, res1_done, res0_done = sem("wo_ps_done"), sem("res1_done"), sem("res0_done")
        lg0_ps_done, top0_done, hid_ps_done, hid_done, hid2_done = (sem(n) for n in ("lg0_ps_done", "top0_done", "hid_ps_done", "hid_done", "hid2_done"))
        ffn_ps_done, res2_done = sem("ffn_ps_done"), sem("res2_done")
        q1_ps_done, q1_done, s1_ps_done, sub1_done, exp1_done = (sem(n) for n in ("q1_ps_done", "q1_done", "s1_ps_done", "sub1_done", "exp1_done"))
        p1T_ps_done, p1T_done, o1_ps_done, res3_done, r1_done = (sem(n) for n in ("p1T_ps_done", "p1T_done", "o1_ps_done", "res3_done", "r1_done"))
        lg1_ps_done, sub2_done, exp2_done, prob_done = sem("lg1_ps_done"), sem("sub2_done"), sem("exp2_done"), sem("prob_done")
        ge_done, cnt_ps_done = sem("ge_done"), sem("cnt_ps_done")
        probT_ps_done, part_ps_done, chosenT_done = sem("probT_ps_done"), sem("part_ps_done"), sem("chosenT_done")
        chosen_done, chosenT_ps_done, pre_done, base_ps_done, cumx_done, idx_ps_done, idx_done = (
            sem(n) for n in ("chosen_done", "chosenT_ps_done", "pre_done", "base_ps_done", "cumx_done", "idx_ps_done", "idx_done"))
        xinT_ps_done, xinT_done, h_ps_done, gelu_done, y_ps_done, y_done = (
            sem(n) for n in ("xinT_ps_done", "xinT_done", "h_ps_done", "gelu_done", "y_ps_done", "y_done"))
        half_set, zeroed = sem("half_set"), sem("zeroed")
        suspect_done, flag_ps_done, flag_done, turn = sem("suspect_done"), sem("flag_ps_done"), sem("flag_done"), sem("turn")
        eq_done, rank_ps_done, ld_g = sem("eq_done"), sem("rank_ps_done"), sem("ld_g")
        dve_chain, pool_chain = sem("dve_chain"), sem("pool_chain")

        def tokens(dram, b):
            return dram[b].rearrange("(p j) d -> p j d", j=J)

        PREFIX = (("fetch", 4), ("rstd0", 2), ("norm0", 1), ("turn0", 1), ("turned0", 1), ("query", 1), ("queried", 1), ("score", 3))
        NAN = PREFIX + (("nan", 6),)
        TILE = PREFIX + (
            ("clip", 6), ("exp", 1), ("weigh", 4), ("weights_T", CH), ("weights_copy", GC), ("attend", CH), ("attended", 4),
            ("att_T", 1), ("att_copy", 1), ("project", 1), ("add_att", 3), ("rstd1", 2), ("norm1", 1), ("turn1", 1), ("turned1", 1),
            ("route", 1), ("top", 3), ("route_exp", 1), ("route_weights", 4))
        for n in range(E + 1):
            TILE += ((f"up{n}", 1), (f"relu{n}", 1), (f"square{n}", 1), (f"down{n}", 1), (f"add{n}", 1))
        TILE += (
            ("stats2", 2), ("rstd2", 2), ("norm2", 1), ("turn2", 1), ("turned2", 1), ("query1", 1), ("queried1", 1), ("score1", 1),
            ("shift1", 3), ("exp1", 1), ("weigh1", 3), ("weights1_T", 1), ("weights1_copy", 1), ("attend1", 1), ("add_att1", 3),
            ("rstd3", 2), ("norm3", 1), ("turn3", 1), ("turned3", 1), ("route1", 1), ("shift2", 3), ("exp2", 1), ("share", 8),
            ("store", 32))
        LOADS = 32
        NAN_N, TILE_N = sum(n for _, n in NAN), sum(n for _, n in TILE)
        AFTER_NAN = LOADS + NT * NAN_N
        FLAGGED = 5
        TURNS_ALL = AFTER_NAN + FLAGGED + NT * TILE_N

        class Turns:

            def __init__(self, eng, stages, name, at):
                self.eng, self.at, self.k = eng, at + sum(n for _, n in stages[:[m for m, _ in stages].index(name)]), 0

            def __call__(self, held=True):
                self.eng.wait_ge(turn, self.at + self.k)
                if not held and self.eng is nc.vector:
                    self.eng.memset(idle[:, 0:1], 0.0)
                if not held and self.eng is nc.gpsimd:
                    self.eng.tensor_tensor(idle[:, 1:2], half_neg[:, 0:1], half_neg[:, 0:1], ALU.add)
                self.k += 1

            def end(self, ins):
                ins.then_inc(turn, 1)

        arena0, arena1 = (pT[:, u].rearrange("p c t -> p (c t)") for u in range(2))
        spans = {}
        at = 0
        for name, n in (("w", HK + CW), ("kbd", HK), ("wT", CH * P), ("x", D), ("n", D), ("nT", D), ("q", D), ("att", D), ("h", D),
                        ("v8", GC * D), ("v1", D), ("k1", NK + 1), ("row", ROW), ("stats", 6), ("mv", 2), ("ve", 1),
                        ("rstd", 1), ("m", H), ("den", H), ("lg", E), ("top", E), ("sel", E), ("a", E), ("b", E), ("one", 4)):
            spans[name] = arena0[:, at:at + n]
            at += n
        kbd = spans["kbd"].rearrange("p (h k) -> p h k", h=H)
        nan_seen, keep, uniform, finite = (arena1[:, 3000 + n:3001 + n] for n in range(4))
        g_w1 = arena1[:, 0:E * F0]
        g_w2 = arena1[0:F0, E * F0:E * F0 + E * D].rearrange("p (e d) -> p e d", e=E)
        eqb, gtb = (c[:] for c in (sb("eqb", [P, E * B], BF16), sb("gtb", [P, E], BF16)))
        need = sb("need", [P, E])
        idle = sb("idle", [P, 2])
        rank = xnT[:, 1, 0:E * NT].rearrange("p (e t) -> p e t", e=E)

        def start_general(eng):
            if eng is nc.vector:
                eng.wait_ge(out_add, 16 * SH * E)
                eng.memset(spans["w"][:, HK:], 0.0).then_inc(half_set, 1)
                eng.memset(finite, 1.0).then_inc(half_set, 1)
                eng.wait_ge(half_set, 3)
            if eng is nc.sync:
                eng.wait_ge(y_done, E)
                eng.wait_ge(out_add, 16 * SH * E)
                eng.dma_start(g_w1.rearrange("p (e f) -> p e f", e=E), a["L0_ffn_W1"].rearrange("e d f -> d e f")).then_inc(turn, 16)
                eng.dma_start(g_w2, a["L0_ffn_W2"].rearrange("e f d -> f e d")).then_inc(ld_g, 16)
                eng.wait_ge(ld_g, 16)
                eng.wait_ge(turn, 16)
                for _ in range(16):
                    eng.sem_inc(turn, 1)

        def prefix_stages(eng, stages, at, i):
            if eng is nc.vector:
                go = Turns(eng, stages, "fetch", at)
                go(); go.end(eng.tensor_copy(spans["x"], x[:, bass.ds(i, 1), :].rearrange("p o d -> p (o d)")))
                go(); go.end(eng.tensor_tensor(kbd, kT[:, bass.ds(i // J, 1), :].broadcast_to([P, H, NK]),
                                               head_mask.unsqueeze(2).broadcast_to([P, H, NK]), ALU.mult))
                layer_stats(eng, go)
                go = Turns(eng, stages, "norm0", at)
                normalised(eng, go, spans["n"])
                go = Turns(eng, stages, "queried", at)
                go(); go.end(eng.tensor_scalar(spans["q"], bank[1][:, 0:P], b_q[:, 0:1], None, ALU.add))
            if eng is nc.gpsimd:
                layer_rstd(eng, Turns(eng, stages, "rstd0", at))
            if eng is nc.tensor:
                go = Turns(eng, stages, "turn0", at)
                go(); go.end(eng.transpose(bank[0][:, 0:P], spans["n"], ident))
                go = Turns(eng, stages, "query", at)
                go(); go.end(eng.matmul(bank[1][:, 0:P], w_q[:, 0, :], spans["nT"], start=True, stop=True))
                go = Turns(eng, stages, "score", at)
                for g, (h0, n) in enumerate(HEAD_GROUPS):
                    go(); go.end(eng.matmul(bank[2 + g][:, 0:n * NK], spans["q"], kbd[:, h0:h0 + n, :].rearrange("p h k -> p (h k)"),
                                            start=True, stop=True))
            if eng is nc.scalar:
                go = Turns(eng, stages, "turned0", at)
                go(); go.end(eng.copy(spans["nT"], bank[0][:, 0:P]))

        def layer_stats(eng, go):
            go(); go.end(eng.bn_stats(spans["stats"], spans["x"]))
            go(held=False); go.end(eng.bn_aggr(spans["mv"], spans["stats"]))

        def layer_rstd(eng, go):
            go(held=False); go.end(eng.tensor_scalar(spans["ve"], spans["mv"][:, 1:2], EPS, None, ALU.add))
            go(); go.end(eng.tensor_tensor(spans["rstd"], spans["ve"], half_neg[:, 0:1], ALU.pow))

        def normalised(eng, go, to):
            go(); go.end(eng.tensor_scalar(to, spans["x"], spans["mv"][:, 0:1], spans["rstd"], ALU.subtract, ALU.mult))

        def find_nan(eng, i):
            at = LOADS + i * NAN_N
            prefix_stages(eng, NAN, at, i)
            if eng is nc.vector:
                go = Turns(eng, NAN, "nan", at)
                w = spans["w"][:, 0:HK]
                for g, (h0, n) in enumerate(HEAD_GROUPS):
                    go(); go.end(eng.tensor_copy(w[:, h0 * NK:(h0 + n) * NK], bank[2 + g][:, 0:n * NK]))
                go(); go.end(eng.tensor_tensor(w, w, w, ALU.is_equal))
                go(); go.end(eng.tensor_reduce(spans["one"][:, 0:1], w, X, ALU.min))
                go(); go.end(eng.tensor_tensor(finite, finite, spans["one"][:, 0:1], ALU.min))

        def count_nan(eng):
            if eng is nc.vector:
                eng.wait_ge(turn, AFTER_NAN)
                eng.tensor_scalar(suspect16[:], finite, -1.0, 1.0, ALU.mult, ALU.add).then_inc(turn, 1)
                eng.wait_ge(turn, AFTER_NAN + 2)
                eng.tensor_scalar(nan_seen, bank[0][:, 0:1], 0.5, None, ALU.is_gt).then_inc(turn, 1)
                eng.wait_ge(turn, AFTER_NAN + 3)
                eng.tensor_scalar(keep, nan_seen, -1.0, 1.0, ALU.mult, ALU.add).then_inc(turn, 1)
                eng.wait_ge(turn, AFTER_NAN + 4)
                eng.tensor_scalar(uniform, nan_seen, 1.0 / NK, None, ALU.mult).then_inc(turn, 1)
            if eng is nc.tensor:
                eng.wait_ge(turn, AFTER_NAN + 1)
                eng.matmul(bank[0][:, 0:1], ones16, suspect16[:], start=True, stop=True).then_inc(turn, 1)

        def run_tile(eng, i):
            at = AFTER_NAN + FLAGGED + i * TILE_N
            prefix_stages(eng, TILE, at, i)

            def stage(name):
                return Turns(eng, TILE, name, at)

            if eng is nc.vector:
                heads = spans["w"][:, 0:HK].rearrange("p (h k) -> p h k", h=H)
                go = stage("clip")
                go(); go.end(eng.tensor_copy(spans["v8"][0:CW], v8[0:CW, bass.ds(i // J, 1)].rearrange("p o c g d -> p (o c g d)")))
                for g, (h0, n) in enumerate(HEAD_GROUPS):
                    go(); go.end(eng.tensor_scalar(spans["w"][:, h0 * NK:(h0 + n) * NK], bank[2 + g][:, 0:n * NK], -CLAMP, CLAMP, ALU.max, ALU.min))
                go(); go.end(eng.tensor_reduce(spans["m"], heads, X, ALU.max))
                go(); go.end(eng.tensor_tensor(heads, heads, spans["m"].unsqueeze(2).broadcast_to([P, H, NK]), ALU.subtract))
                go = stage("weigh")
                go(); go.end(eng.tensor_reduce(spans["den"], heads, X, ALU.add))
                go(); go.end(eng.reciprocal(spans["den"], spans["den"]))
                go(); go.end(eng.tensor_tensor(heads, heads, spans["den"].unsqueeze(2).broadcast_to([P, H, NK]), ALU.mult))
                go(); go.end(eng.tensor_scalar(spans["w"][:, 0:HK], spans["w"][:, 0:HK], keep, uniform, ALU.mult, ALU.add))
                go = stage("attended")
                go(); go.end(eng.tensor_copy(spans["att"], bank[0][:, 0:D]))
                go(); go.end(eng.tensor_copy(spans["k1"][:, 0:NK], k1T[:, bass.ds(i // J, 1), :].rearrange("p o k -> p (o k)")))
                go(); go.end(eng.tensor_copy(spans["v1"][0:NK, :], v1[:, bass.ds(i // J, 1), :].rearrange("p o k -> p (o k)")))
                go(); go.end(eng.tensor_tensor(spans["x"], spans["x"], bo_rows[:], ALU.add))
                go = stage("add_att")
                go(); go.end(eng.tensor_tensor(spans["x"], bank[0][:, 0:D], spans["x"], ALU.add))
                layer_stats(eng, go)
                normalised(eng, stage("norm1"), spans["n"])
                go = stage("top")
                go(); go.end(eng.tensor_copy(spans["lg"], bank[1][:, 0:E]))
                go(held=False); go.end(eng.max(spans["top"], spans["lg"]))
                go(); go.end(eng.tensor_tensor(spans["a"][:, 0:1], spans["top"][:, 1:2], spans["top"][:, 0:1], ALU.subtract))
                go = stage("route_weights")
                go(); go.end(eng.tensor_scalar(spans["a"][:, 0:1], spans["a"][:, 0:1], 1.0, None, ALU.add))
                go(); go.end(eng.reciprocal(spans["a"][:, 0:1], spans["a"][:, 0:1]))
                go(); go.end(eng.tensor_scalar(spans["a"][:, 0:1], spans["a"][:, 0:1], 1.0, None, ALU.is_ge))
                go(); go.end(eng.tensor_scalar(spans["sel"], spans["lg"], spans["top"][:, 0:1], spans["a"][:, 0:1], ALU.is_ge, ALU.mult))
                for n in range(E + 1):
                    go = stage(f"square{n}")
                    go(); go.end(eng.tensor_tensor(spans["h"][0:F0], spans["h"][0:F0], spans["h"][0:F0], ALU.mult))
                    go = stage(f"add{n}")
                    scale = spans["sel"][:, n:n + 1] if n < E else 1.0
                    go(); go.end(eng.scalar_tensor_tensor(spans["x"], bank[3][:, 0:D], scale, spans["x"], ALU.mult, ALU.add))
                layer_stats(eng, stage("stats2"))
                normalised(eng, stage("norm2"), spans["n"])
                go = stage("shift1")
                w1_ = spans["w"][:, 0:NK]
                go(); go.end(eng.tensor_copy(w1_, bank[0][:, 0:NK]))
                go(); go.end(eng.tensor_reduce(spans["one"][:, 0:1], w1_, X, ALU.max))
                go(); go.end(eng.tensor_scalar(w1_, w1_, spans["one"][:, 0:1], None, ALU.subtract))
                go = stage("weigh1")
                go(); go.end(eng.tensor_reduce(spans["one"][:, 0:1], w1_, X, ALU.add))
                go(); go.end(eng.reciprocal(spans["one"][:, 0:1], spans["one"][:, 0:1]))
                go(); go.end(eng.tensor_scalar(w1_, w1_, spans["one"][:, 0:1], None, ALU.mult))
                go = stage("add_att1")
                go(); go.end(eng.tensor_tensor(spans["x"], bank[0][:, 0:D], spans["x"], ALU.add))
                layer_stats(eng, go)
                normalised(eng, stage("norm3"), spans["n"])
                go = stage("shift2")
                go(); go.end(eng.tensor_tensor(spans["lg"], bank[1][:, 0:E], bs_rows[:], ALU.add))
                go(); go.end(eng.tensor_reduce(spans["one"][:, 0:1], spans["lg"], X, ALU.max))
                go(); go.end(eng.tensor_scalar(spans["lg"], spans["lg"], spans["one"][:, 0:1], None, ALU.subtract))
                go = stage("share")
                go(); go.end(eng.tensor_reduce(spans["one"][:, 0:1], spans["lg"], X, ALU.add))
                go(); go.end(eng.reciprocal(spans["one"][:, 0:1], spans["one"][:, 0:1]))
                go(); go.end(eng.tensor_scalar(spans["row"][:, D:ROW], spans["lg"], spans["one"][:, 0:1], None, ALU.mult))
                go(); go.end(eng.tensor_copy(spans["row"][:, 0:D], spans["n"]))
                go(); go.end(eng.tensor_tensor(spans["a"], spans["row"][:, D:ROW], spans["row"][:, D:ROW], ALU.is_equal))
                go(); go.end(eng.tensor_scalar(spans["a"], spans["a"], -1.5, 1.5, ALU.mult, ALU.add))
                go(); go.end(eng.tensor_scalar(spans["b"], spans["row"][:, D:ROW], 0.0, None, ALU.max))
                go(); go.end(eng.tensor_tensor(prob[:, :, bass.ds(i, 1)], spans["a"].unsqueeze(2), spans["b"].unsqueeze(2), ALU.add))
            if eng is nc.gpsimd:
                for n in (1, 2, 3):
                    layer_rstd(eng, stage(f"rstd{n}"))
            if eng is nc.tensor:
                go = stage("weights_T")
                for c in range(GC):
                    for g in range(G):
                        o = g * GK + c * CW
                        go(); go.end(eng.transpose(bank[5 + c][0:CW, g * P:(g + 1) * P], spans["w"][:, o:o + CW], ident))
                go = stage("attend")
                wT = spans["wT"].rearrange("p (c g t) -> p c g t", c=GC, g=G)
                for g in range(G):
                    for c in range(GC):
                        n, o = chunk_rows(c), c * D + g * GD
                        go(); go.end(eng.matmul(bank[0][:, g * GD:(g + 1) * GD], wT[0:n, c, g, :], spans["v8"][0:n, o:o + GD],
                                                start=(c == 0), stop=(c == GC - 1)))

                def turned(name, b, src, rows=P):
                    go = stage(name)
                    go(); go.end(eng.transpose(bank[b][0:rows, 0:P], src, ident))

                def product(name, to, lhsT, rhs):
                    go = stage(name)
                    go(); go.end(eng.matmul(to, lhsT, rhs, start=True, stop=True))

                turned("att_T", 1, spans["att"])
                product("project", bank[0][:, 0:D], spans["nT"], w_q[:, 2, :])
                turned("turn1", 0, spans["n"])
                product("route", bank[1][:, 0:E], spans["nT"], w_r[:, 0, :])
                for n in range(E + 1):
                    product(f"up{n}", bank[2][0:F0, 0:P], g_w1[:, n * F0:(n + 1) * F0] if n < E else w_s1[:], spans["nT"])
                    product(f"down{n}", bank[3][:, 0:D], spans["h"][0:F0, :], g_w2[:, n, :] if n < E else w_s2[:])
                turned("turn2", 0, spans["n"])
                product("query1", bank[1][:, 0:P], w_q[:, 1, :], spans["nT"])
                product("score1", bank[0][:, 0:NK], spans["q"], spans["k1"][:, 0:NK])
                turned("weights1_T", 1, spans["w"][:, 0:NK], NK)
                product("attend1", bank[0][:, 0:D], spans["wT"][0:NK, 0:P], spans["v1"][0:NK, :])
                turned("turn3", 0, spans["n"])
                product("route1", bank[1][:, 0:E], spans["nT"], w_r[:, 1, :])
            if eng is nc.scalar:
                def one(name, to, src, func=ACT.Copy, **more):
                    go = stage(name)
                    go(); go.end(eng.activation(to, src, func, **more))

                one("exp", spans["w"][:, 0:HK], spans["w"][:, 0:HK], ACT.Exp)
                go = stage("weights_copy")
                wT = spans["wT"].rearrange("p (c t) -> p c t", c=GC)
                for c in range(GC):
                    go(); go.end(eng.copy(wT[0:CW, c, :], bank[5 + c][0:CW, :]))
                one("att_copy", spans["nT"], bank[1][:, 0:P])
                one("turned1", spans["nT"], bank[0][:, 0:P])
                one("route_exp", spans["a"][:, 0:1], spans["a"][:, 0:1], ACT.Exp)
                for n in range(E + 1):
                    one(f"relu{n}", spans["h"][0:F0, :], bank[2][0:F0, 0:P], ACT.Relu)
                one("turned2", spans["nT"], bank[0][:, 0:P])
                one("queried1", spans["q"], bank[1][:, 0:P], ACT.Identity, bias=b_q[:, 1:2])
                one("exp1", spans["w"][:, 0:NK], spans["w"][:, 0:NK], ACT.Exp)
                one("weights1_copy", spans["wT"][0:NK, 0:P], bank[1][0:NK, 0:P])
                one("turned3", spans["nT"], bank[0][:, 0:P])
                one("exp2", spans["lg"], spans["lg"], ACT.Exp)
            if eng is nc.sync:
                go = stage("store")
                go()
                eng.dma_start(out.rearrange("b (p j) d -> p b j d", j=J)[:, bass.ds(i // J, 1), bass.ds(i % J, 1), :],
                              spans["x"].rearrange("p (a b d) -> p a b d", a=1, b=1)).then_inc(turn, 16)
                eng.dma_start(gather_rows.rearrange("(b p j) n -> p b j n", b=B, j=J)[:, bass.ds(i // J, 1), bass.ds(i % J, 1), :],
                              spans["row"].rearrange("p (a b d) -> p a b d", a=1, b=1)).then_inc(turn, 16)
        block = ctx.enter_context(nc.Block())

        @block.sync
        def _(sp):
            sp.dma_start(x[:, 0:J, :], tokens(a["x"], 0)).then_inc(ld_x[0], 16)
            sp.dma_start(w_q[:, 0, :], a["L0_xattn_Wq"]).then_inc(ld_q0, 16)
            sp.dma_start(x[:, J:2 * J, :], tokens(a["x"], 1)).then_inc(ld_x[1], 16)
            sp.dma_start(c16[:].bitcast(U16), a["c_bf16"]).then_inc(ld_c16, 16)
            sp.wait_ge(zeroed, 1)
            sp.dma_start(neg_head[0:H, :].bitcast(U16), a["c_neg"]).then_inc(ld_neg, 16)
            for b in range(2, B):
                sp.dma_start(x[:, b * J:(b + 1) * J, :], tokens(a["x"], b)).then_inc(ld_x[b], 16)
            for n, w in ((1, "L1_xattn_Wq"), (2, "L0_xattn_Wo")):
                sp.dma_start(w_q[:, n, :], a[w]).then_inc(ld_q, 16)
            sp.dma_start(b_q[:, 1:2], a["L1_xattn_bq"].rearrange("(d o) -> d o", o=1)).then_inc(ld_q, 16)
            sp.dma_start(bo_rows[:], a["L0_xattn_bo"].rearrange("(o d) -> o d", o=1).broadcast_to([P, D])).then_inc(ld_bo, 16)
            sp.dma_start(w_s1[:], a["L0_ffn_Ws1"]).then_inc(ld_ffn, 16)
            sp.dma_start(w_s2[:], a["L0_ffn_Ws2"]).then_inc(ld_ffn, 16)
            sp.dma_start(w_r[:, 0, :], a["L0_ffn_Wr"]).then_inc(ld_rt, 16)
            sp.dma_start(w_r[:, 1, :], a["L1_ffn_Ws"]).then_inc(ld_rt, 16)
            sp.dma_start(bs_rows[:], a["L1_ffn_bs"].rearrange("(o d) -> o d", o=1).broadcast_to([P, E])).then_inc(ld_rt, 16)
            sp.dma_start(tile_rows[:], a["c_rows"]).then_inc(ld_rc, 16)
            sp.dma_start(bit_steps[:], a["c_bits"]).then_inc(ld_rc, 16)
            sp.dma_start(b1_rows[:], a["L1_ffn_b1"].rearrange("e (c p) -> (e c) p", p=P)).then_inc(ld_b1, 16)
            sp.dma_start(b2_rows[:], a["L1_ffn_b2"].rearrange("(o e) d -> o e d", o=1).broadcast_to([P, E, D])).then_inc(ld_b2, 16)

            def stack_queries(b):
                for r, (part, split) in enumerate(((q_hi, q_hi_done), (q_hi, q_hi_done), (q_lo, q_lo_done), (q_lo, q_lo_done))):
                    if r % 2 == 0:
                        sp.wait_ge(split, b)
                    for g in range(G):
                        sp.dma_start(q_stack[r * GD:(r + 1) * GD, b, g, :],
                                     part[g * GD:(g + 1) * GD, b % 2, :]).then_inc(q_stack_done[b], 16)

            stack_queries(1)
            for ph in range(B + 3):
                if ph + 2 < B:
                    stack_queries(ph + 2)
                if ph == B - 1:
                    for e in range(E):
                        sp.dma_start(w1[:, e, :], a["L1_ffn_W1"][e]).then_inc(ld_w[e], 16)
                        sp.dma_start(w2[:, e, :, :], a["L1_ffn_W2"][e].rearrange("(c p) d -> p c d", p=P)).then_inc(ld_w[e], 16)
                b = ph - 3
                if 0 <= b:
                    sp.wait_ge(prob_done, b + 1)
                    sp.dma_start(gather_rows[b * T:(b + 1) * T, :].rearrange("(p j) n -> p j n", j=J),
                                 xrow[:, b % 2, :, :]).then_inc(rows_out[b], 16)
                b = ph - 2
                if 0 <= b < B:
                    sp.wait_ge(res3_done, b + 1)
                    sp.dma_start(tokens(out, b), res[:, b * J:(b + 1) * J, :]).then_inc(out_base, 16)
            sp.wait_ge(out_base, 16 * B)
            sp.wait_ge(flag_done, 1)
            with sp.If(sp.value_load(flag[0:1, 0:1], min_val=0, max_val=1) > 0):
                start_general(sp)
                with sp.Fori(0, NT) as i:
                    run_tile(sp, i)
                sp.wait_ge(turn, TURNS_ALL)

        @block.scalar
        def _(act):
            act.dma_start(ctx_in[:], a["ctx_768"].rearrange("b k c -> k b c")).then_inc(ld_ctx, 16)
            act.dma_start(c32[:], a["c_f32"]).then_inc(ld_c32, 16)
            act.dma_start(w_kv[0:DC, 0, :], a["L0_xattn_Wk"]).then_inc(ld_k, 16)
            act.dma_start(w_kv[DC:DC + 1, 0, :], a["L0_xattn_bk"].rearrange("(o d) -> o d", o=1)).then_inc(ld_k, 16)
            act.dma_start(b_q[:, 0:1], a["L0_xattn_bq"].rearrange("(d o) -> d o", o=1)).then_inc(ld_bq, 16)

            def copy_T(n, b, ps):
                act.wait_ge(xnT_ps_done[n], b + 1)
                nc.scalar.copy(xnT[:, n, :], ps[:, :]).then_inc(xnT_done[n], 1)

            act.wait_ge(ctxT_ps_done, 1)
            act.wait_ge(ones_set, 1)
            for o in range(0, WINDOW, NK):
                n = min(NK, WINDOW - o)
                ins = nc.scalar.copy(ctxT[0:DC, :, o:o + n],
                                     tail1_ps[1][0:DC, 0:B * NK].rearrange("p (b k) -> p b k", b=B)[:, :, 0:n])
            ins.then_inc(ctxT_done, 1)
            copy_T(0, 0, prep_ps)
            for u in range(2):
                act.wait_ge(k4_ps_done, u + 1)
                nc.scalar.activation(k_parts[:, 2 * u:2 * u + 2].rearrange("p g b k -> p g (b k)"), k4_ps[:, 2 * u:2 * u + 2, :], ACT.Copy,
                                     scale=float(HD) ** -0.5).then_inc(k_hi_done, 1)
            act.wait_ge(b_q4_done, 1)
            for u in range(2):
                act.wait_ge(q4_ps_done, u + 1)
                for g in (2 * u, 2 * u + 1):
                    ins = nc.scalar.activation(q_stack[:, 0, g, :], q4_ps[:, g, :], ACT.Identity, bias=b_q4[:, g:g + 1])
                ins.then_inc(q4_hi_done, 1)

            def q_high(b):
                act.wait_ge(q_ps_done, b)
                if b >= 3:
                    act.wait_ge(q_stack_done[b - 2], 256)
                nc.scalar.activation(q_hi[:, b % 2, :], prep_ps[:, :], ACT.Identity, bias=b_q[:, 0:1]).then_inc(q_hi_done, 1)

            copy_T(0, 1, prep_ps)
            q_high(1)
            for ph in range(B + 3):
                b = ph
                for s in range(SLOTS):
                    if b < B:
                        act.wait_ge(st_ps_done, b * CH + s + 1)
                        if b >= 2 and s == 0:
                            act.wait_ge(o_ps_done, b - 1)
                        n = chunk_rows(s // G)
                        nc.scalar.activation(pT[0:n, b % 2, s, :], ST_ps[s % 2][0:n, :], ACT.Exp).then_inc(exp_done, 1)
                    if b + 2 < B and s == 1:
                        copy_T(0, b + 2, prep_ps)
                    if b + 2 < B and s == 2:
                        q_high(b + 2)
                    if b == 0 and s == 3:
                        act.wait_ge(k1_ps_done, 1)
                        nc.scalar.copy(k1T[:].rearrange("p b k -> p (b k)"), tail2_ps[:, 0:B * NK]).then_inc(k1_done, 1)
                    if b == 0 and s == 5:
                        act.wait_ge(v1_ps_done, 1)
                        nc.scalar.copy(v1[:].rearrange("p b k -> p (b k)"), tail2_ps[0:NK, :]).then_inc(v1_done, 1)
                    if b == 0 and s == 7:
                        act.wait_ge(kT_ps_done, 1)
                        nc.scalar.activation(kT[:].rearrange("p b k -> p (b k)"), tail2_ps[:, 0:B * NK], ACT.Copy,
                                             scale=float(HD) ** -0.5).then_inc(kT_done, 1)
                    if b == 0 and s == 9:
                        act.wait_ge(b1_ps_done, 1)
                        nc.scalar.copy(b1[:], tail2_ps[:, 0:E * FC]).then_inc(b1_done, 1)
                    t = ph - 1
                    if 0 <= t < B:
                        if s == 7:
                            copy_T(1, t, tail1_ps[0])
                        if s == 8:
                            act.wait_ge(hid_ps_done, t + 1)
                            nc.scalar.activation(hid[:], tail1_ps[1][0:F0, :], ACT.Relu).then_inc(hid_done, 1)
                            act.wait_ge(hid_done, t + 1)
                            nc.scalar.activation(hid2[:], hid[:], ACT.Square).then_inc(hid2_done, 1)
                    t = ph - 2
                    if 0 <= t < B:
                        if s == 2:
                            copy_T(2, t, tail2_ps)
                        if s == 3:
                            act.wait_ge(q1_ps_done, t + 1)
                            nc.scalar.activation(q1T[:], tail2_ps[:, :], ACT.Identity, bias=b_q[:, 1:2]).then_inc(q1_done, 1)
                        if s == 5:
                            act.wait_ge(sub1_done, t + 1)
                            nc.scalar.activation(p1[:], p1[:], ACT.Exp).then_inc(exp1_done, 1)
                        if s == 7:
                            act.wait_ge(p1T_ps_done, t + 1)
                            nc.scalar.copy(p1T[:], tail2_ps[0:NK, :]).then_inc(p1T_done, 1)
                    t = ph - 3
                    if 0 <= t < B:
                        if s == 0:
                            copy_T(3, t, tail2_ps)
                        if s == 1:
                            act.wait_ge(sub2_done, t + 1)
                            nc.scalar.activation(lg[:, t % 2], lg[:, t % 2], ACT.Exp).then_inc(exp2_done, 1)

            def experts(again):
                for e in range(E):
                    n = again * E + e
                    act.wait_ge(xinT_ps_done, n + 1)
                    nc.scalar.copy(xinT[:, e % 2, :], bank[e % 2][:, 0:CAP]).then_inc(xinT_done, 1)
                    if n >= 2:
                        act.wait_ge(y_ps_done, n - 1)
                    for c in range(FC):
                        act.wait_ge(h_ps_done, n * FC + c + 1)
                        nc.scalar.activation(hg[:, e % 2, c, :], bank[2 + c][:, 0:CAP], ACT.Gelu_apprx_tanh,
                                             bias=b1[:, e * FC + c:e * FC + c + 1]).then_inc(gelu_done, 1)

            act.wait_ge(b1_done, 1)
            experts(0)
            act.wait_ge(flag_done, 1)
            with act.If(act.value_load(flag[0:1, 0:1], min_val=0, max_val=1) > 0):
                with act.Fori(0, NT) as i:
                    find_nan(act, i)
                with act.Fori(0, NT) as i:
                    run_tile(act, i)
                experts(1)

        @block.tensor
        def _(pe):
            def transposes(n, b, ps):
                src = xrow[:, b % 2, :, 0:D] if n == 3 else xn[:, n]
                for j in range(J):
                    ins = pe.transpose(ps[:, j * P:(j + 1) * P], src[:, j, :], ident)
                ins.then_inc(xnT_ps_done[n], 1)

            def prep_T(b):
                pe.wait_ge(xn_done[0], b + 1)
                if b == 1:
                    pe.wait_ge(q4_lo_done, 2)
                if b >= 2:
                    pe.wait_ge(mT_done, b - 1)
                if b >= 3:
                    pe.wait_ge(v8_done, b - 2)
                transposes(0, b, prep_ps)

            def prep_q(b):
                pe.wait_ge(xnT_done[0], b + 1)
                pe.matmul(prep_ps[:, :], w_q[:, 0, :], xnT[:, 0, :], start=True, stop=True).then_inc(q_ps_done, 1)

            def scores(b, j, groups=range(G)):
                if j == 0 and groups[0] == 0:
                    if b == 0:
                        pe.wait_ge(q4_lo_done, 2)
                    else:
                        pe.wait_ge(q_stack_done[b], 256)
                    pe.wait_ge(k_stack_done, b + 1)
                for g in groups:
                    u = (b * J + j) * G + g
                    if u >= 2:
                        pe.wait_ge(max_done, u - 1)
                    pe.matmul(S_ps[u % 2][:, 0:GK], q_stack[:, b, g, j * P:(j + 1) * P],
                              k_stack[:, b, g].rearrange("p h k -> p (h k)"), start=True, stop=True).then_inc(s_ps_done, 1)

            def maxima_T(b, j):
                pe.wait_ge(max_done, G * (b * J + j + 1))
                if j == 0:
                    if b == 0:
                        pe.wait_ge(q_lo_done, 1)
                    pe.wait_ge(v8_done, b)
                ins = pe.transpose(mT_ps[:, j * P:(j + 1) * P], mrow[:, b % 2, j, :], ident16)
                if j == J - 1:
                    ins.then_inc(mT_ps_done, 1)

            def values(b):
                for c in range(GC):
                    o = c * CW % NK
                    ins = pe.matmul(v_ps[:, c * D:(c + 1) * D], ctxT[:, b, o:o + CW], w_kv[:, 1, :], start=True, stop=True)
                ins.then_inc(v_ps_done, 1)

            def scores_T(b, s):
                if s == 0:
                    pe.wait_ge(mT_done, b + 1)
                if b * CH + s >= 2:
                    pe.wait_ge(exp_done, b * CH + s - 1)
                c, g = s // G, s % G
                n, o = chunk_rows(c), c * CW
                pe.matmul(ST_ps[s % 2][0:n, :], k_stack[:, b, g].rearrange("p h k -> p (h k)")[:, o:o + n], q_stack[:, b, g, :],
                          start=True, stop=False)
                pe.matmul(ST_ps[s % 2][0:n, :], neg_head[:, g * GK + o:g * GK + o + n], mT[:, b % 2, :], start=False,
                          stop=True).then_inc(st_ps_done, 1)

            def attend(b, c):
                pe.wait_ge(exp_done, b * CH + (c + 1) * G)
                if c == 0:
                    pe.wait_ge(v8_done, b + 1)
                    if b >= 1:
                        pe.wait_ge(res2_done, b)
                        pe.wait_ge(top0_done, b)
                n = chunk_rows(c)
                for to, of in ((O_ps, None), (den_ps, value_mask)):
                    for g in range(G):
                        lhsT = v8[0:n, b, c, g, :] if of is None else of[0:n, c, :]
                        ins = pe.matmul(to[g * GD:(g + 1) * GD, :], lhsT, pT[0:n, b % 2, c * G + g, :], start=(c == 0),
                                        stop=(c == GC - 1), tile_position=(0, g * GD))
                if c == GC - 1:
                    ins.then_inc(o_ps_done, 1)

            pe.wait_ge(ld_ctx, 16)
            pe.wait_ge(ld_c32, 16)
            for b in range(B):
                ins = pe.transpose(tail1_ps[1][0:DC, b * NK:(b + 1) * NK], ctx_in[:, b, :], ident[0:NK, 0:NK])
            ins.then_inc(ctxT_ps_done, 1)
            prep_T(0)
            pe.wait_ge(ctxT_done, 1)
            pe.wait_ge(w_k4_done, 1)
            for g in range(G):
                ins = pe.matmul(k4_ps[:, g, :], w_k4[:, g].rearrange("p r d -> p (r d)"), ctxT[:, :, 0:NK], start=True, stop=True)
                if g % 2:
                    ins.then_inc(k4_ps_done, 1)
            pe.wait_ge(xnT_done[0], 1)
            pe.wait_ge(w_q4_done, 1)
            for g in range(G):
                ins = pe.matmul(q4_ps[:, g, :], w_q4[:, g].rearrange("p r d -> p (r d)"), xnT[:, 0, :], start=True, stop=True)
                if g % 2:
                    ins.then_inc(q4_ps_done, 1)
            for j in range(J):
                scores(0, j)
                if j == 0:
                    prep_T(1)
                if j == 1:
                    prep_q(1)
                if j == 2:
                    pe.wait_ge(ld_c16, 16)
                if j >= 2:
                    maxima_T(0, j - 2)
            maxima_T(0, J - 2)
            pe.wait_ge(ld_neg, 16)

            for ph in range(B + 3):
                b = ph
                for s in range(SLOTS):
                    t = ph - 1
                    if b < B and s == 0:
                        maxima_T(b, J - 1)
                    if 0 <= t < B and s < GC - 1:
                        attend(t, s + 1)
                    if b < B:
                        scores_T(b, s)
                        if b + 2 < B and s == 1:
                            prep_T(b + 2)
                        if b + 2 < B and s == 2:
                            prep_q(b + 2)
                        if b + 1 < B:
                            if s >= 4:
                                scores(b + 1, (s - 4) // 2, range((s % 2) * 2, (s % 2) * 2 + 2))
                            if s in (6, 8, 10):
                                maxima_T(b + 1, s // 2 - 3)
                        if s == 3:
                            pe.wait_ge(q_lo_done, min(b + 2, B - 1))
                            if b == 0:
                                pe.wait_ge(ld_kv, 96)
                            values(b)
                    if b == 0 and s == 3:
                        pe.matmul(tail2_ps[:, 0:B * NK], w_kv[:, 2, :], ctxT[:, :, 0:NK], start=True, stop=True).then_inc(k1_ps_done, 1)
                    if b == 0 and s == 5:
                        pe.wait_ge(k1_done, 1)
                        for c in range(B):
                            ins = pe.matmul(tail2_ps[0:NK, c * D:(c + 1) * D], ctxT[:, c, 0:NK], w_kv[:, 3, :], start=True, stop=True)
                        ins.then_inc(v1_ps_done, 1)
                    if b == 0 and s == 7:
                        pe.wait_ge(v1_done, 1)
                        pe.matmul(tail2_ps[:, 0:B * NK], w_kv[:, 0, :], ctxT[:, :, 0:NK], start=True, stop=True).then_inc(kT_ps_done, 1)
                    if b == 0 and s == 9:
                        pe.wait_ge(kT_done, 1)
                        pe.wait_ge(ld_b1, 16)
                        pe.transpose(tail2_ps[:, 0:E * FC], b1_rows[:], ident[0:E * FC, 0:E * FC]).then_inc(b1_ps_done, 1)
                    if 0 <= t < B:
                        if s == 4:
                            pe.wait_ge(attT_done, t + 1)
                            if t == 0:
                                pe.wait_ge(ld_q, 48)
                            for j in range(J):
                                ins = pe.matmul(tail1_ps[1][:, j * P:(j + 1) * P], attT[:, j * P:(j + 1) * P], w_q[:, 2, :],
                                                start=True, stop=True)
                            ins.then_inc(wo_ps_done, 1)
                        if s == 7:
                            pe.wait_ge(xn_done[1], t + 1)
                            transposes(1, t, tail1_ps[0])
                        if s == 8:
                            pe.wait_ge(xnT_done[1], t + 1)
                            if t == 0:
                                pe.wait_ge(ld_ffn, 32)
                                pe.wait_ge(ld_rt, 48)
                            pe.matmul(tail1_ps[1][0:F0, :], w_s1[:], xnT[:, 1, :], start=True, stop=True).then_inc(hid_ps_done, 1)
                            for j in range(J):
                                ins = pe.matmul(logits0[:, j, :], xnT[:, 1, j * P:(j + 1) * P], w_r[:, 0, :], start=True, stop=True)
                            ins.then_inc(lg0_ps_done, 1)
                        if s == 10:
                            pe.wait_ge(hid2_done, t + 1)
                            for j in range(J):
                                ins = pe.matmul(tail1_ps[1][:, j * P:(j + 1) * P], hid2[:, j * P:(j + 1) * P], w_s2[:],
                                                start=True, stop=True)
                            ins.then_inc(ffn_ps_done, 1)
                    if b < B and s == 11:
                        attend(b, 0)
                    t = ph - 3
                    if 0 <= t < B:
                        if s == 0:
                            pe.wait_ge(xn_done[3], t + 1)
                            transposes(3, t, tail2_ps)
                        if s == 1:
                            pe.wait_ge(xnT_done[3], t + 1)
                            for j in range(J):
                                ins = pe.matmul(logits1[:, j, :], xnT[:, 3, j * P:(j + 1) * P], w_r[:, 1, :], start=True, stop=True)
                            ins.then_inc(lg1_ps_done, 1)
                    t = ph - 2
                    if 0 <= t < B:
                        if s == 2:
                            pe.wait_ge(xn_done[2], t + 1)
                            if t == 0:
                                pe.wait_ge(b1_done, 1)
                            else:
                                pe.wait_ge(sub2_done, t)
                            transposes(2, t, tail2_ps)
                        if s == 3:
                            pe.wait_ge(xnT_done[2], t + 1)
                            pe.matmul(tail2_ps[:, :], w_q[:, 1, :], xnT[:, 2, :], start=True, stop=True).then_inc(q1_ps_done, 1)
                        if s == 4:
                            pe.wait_ge(q1_done, t + 1)
                            for j in range(J):
                                ins = pe.matmul(tail2_ps[:, j * NK:(j + 1) * NK], q1T[:, j * P:(j + 1) * P], k1T[:, t, :],
                                                start=True, stop=True)
                            ins.then_inc(s1_ps_done, 1)
                        if s == 7:
                            pe.wait_ge(exp1_done, t + 1)
                            for j in range(J):
                                ins = pe.transpose(tail2_ps[0:NK, j * P:(j + 1) * P], p1[:, j, :], ident)
                            ins.then_inc(p1T_ps_done, 1)
                        if s == 8:
                            pe.wait_ge(p1T_done, t + 1)
                            for j in range(J):
                                ins = pe.matmul(tail2_ps[:, j * P:(j + 1) * P], p1T[:, j * P:(j + 1) * P], v1[:, t, :],
                                                start=True, stop=True)
                            ins.then_inc(o1_ps_done, 1)

            def threshold(again):
                pe.transpose(bank[7][:, 0:P], prob[:].rearrange("p e t -> p (e t)"), ident).then_inc(probT_ps_done, 1)
                for i in range(NSTEP):
                    pe.wait_ge(ge_done, i + 1 + again * NSTEP)
                    pe.matmul(bank[6][:, 0:K], same16, count16[:], start=True, stop=True).then_inc(cnt_ps_done, 1)

            def indices(again):
                pe.wait_ge(pre_done, again + 1)
                pe.matmul(bank[6][:, 0:1], before, pre[:, P - 1:P], start=True, stop=True).then_inc(base_ps_done, 1)
                for g in range(2):
                    pe.wait_ge(cumx_done, 2 * again + g + 1)
                    for h in range(SH):
                        oh = onehot[:, h * P:(h + 1) * P]
                        if g == 0:
                            pe.matmul(bank[4 + h][:, 0:E], oh, tile_rows[:], start=True, stop=True)
                        pe.matmul(bank[2 * h + g][:, :], oh, cumx[:, 4 * g:4 * g + 4, :].rearrange("p e t -> p (e t)"), start=True,
                                  stop=True).then_inc(idx_ps_done, 1)

            def rows_T(again, e):
                n = again * E + e
                pe.wait_ge(got[e], 16 * SH * (again + 1))
                if e >= 2:
                    pe.wait_ge(xinT_done, n - 1)
                else:
                    pe.wait_ge(idx_done, 2 * again + 2)
                for h in range(SH):
                    ins = pe.transpose(bank[e % 2][:, h * P:(h + 1) * P], xin[:, e, h, 0:D], ident)
                ins.then_inc(xinT_ps_done, 1)

            def experts(again):
                rows_T(again, 0)
                for e in range(E):
                    n = again * E + e
                    pe.wait_ge(xinT_done, n + 1)
                    pe.wait_ge(ld_w[e], 32)
                    for c in range(FC):
                        if n >= 1:
                            pe.wait_ge(gelu_done, (n - 1) * FC + c + 1)
                        pe.matmul(bank[2 + c][:, 0:CAP], w1[:, e, c * P:(c + 1) * P], xinT[:, e % 2, :], start=True,
                                  stop=True).then_inc(h_ps_done, 1)
                    if e + 1 < E:
                        rows_T(again, e + 1)
                    if n >= 2:
                        pe.wait_ge(y_done, n - 1)
                    for h in range(SH):
                        for c in range(FC):
                            if h == 0:
                                pe.wait_ge(gelu_done, n * FC + c + 1)
                            ins = pe.matmul(bank[6 + e % 2][:, h * P:(h + 1) * P], hg[:, e % 2, c, h * P:(h + 1) * P], w2[:, e, c, :],
                                            start=(c == 0), stop=(c == FC - 1))
                    ins.then_inc(y_ps_done, 1)

            pe.wait_ge(prob_done, B)
            threshold(0)
            indices(0)
            experts(0)
            pe.wait_ge(suspect_done, 1)
            pe.matmul(bank[0][0:1, 0:1], ones16[:, 0:1], suspect16[:], start=True, stop=True).then_inc(flag_ps_done, 1)
            pe.wait_ge(flag_done, 1)
            with pe.If(pe.value_load(flag[0:1, 0:1], min_val=0, max_val=1) > 0):
                with pe.Fori(0, NT) as i:
                    find_nan(pe, i)
                count_nan(pe)
                with pe.Fori(0, NT) as i:
                    run_tile(pe, i)
                pe.wait_ge(turn, TURNS_ALL)
                threshold(1)
                pe.wait_ge(chosenT_done, 1)
                pe.transpose(bank[6][:, 0:P // 2].bitcast(BF16), chosenT[:], ident16)
                pe.transpose(bank[7][:, 0:P // 2].bitcast(BF16), passing[:, 0, :], ident16).then_inc(part_ps_done, 1)
                pe.wait_ge(eq_done, 1)
                pe.matmul(bank[6][:, 0:E * B], prefix, eqb[:], start=True, stop=True)
                pe.matmul(bank[7][:, 0:E * B], ones16, eqb[:], start=True, stop=True)
                pe.matmul(bank[7][:, E * B:E * B + E], ones16, gtb[:], start=True, stop=True).then_inc(rank_ps_done, 1)
                pe.wait_ge(chosen_done, 1)
                pe.transpose(bank[6][:, 0:P // 2].bitcast(BF16), chosen[:].rearrange("p e t -> p (e t)"), ident16).then_inc(chosenT_ps_done, 1)
                indices(1)
                experts(1)

        @block.vector
        def _(dve):
            count = [0]

            def settle(ins):
                count[0] += 1
                ins.then_inc(dve_chain, 1)
                dve.wait_ge(dve_chain, count[0])

            def ln_stats(n, src):
                for j in range(J):
                    ins = dve.bn_stats(stats[:, n, j, :], src[:, j, :])
                settle(ins)
                for j in range(J):
                    ins = dve.bn_aggr(mv[:, n, j, :], stats[:, n, j, :])
                ins.then_inc(var_done[n], 1)

            def ln_apply(n, b, src, dst):
                dve.wait_ge(rstd_done[n], b + 1)
                for j in range(J):
                    ins = dve.tensor_scalar(dst[:, j, :], src[:, j, :], mv[:, n, j, 0:1], rstd[:, n, j:j + 1],
                                            ALU.subtract, ALU.mult)
                ins.then_inc(xn_done[n], 1)

            def rtiles(b):
                return res[:, b * J:(b + 1) * J, :]

            def ln0(b):
                ln0_stats(b)
                ln0_apply(b)

            def ln0_stats(b):
                dve.wait_ge(ld_x[b], 16)
                ln_stats(0, x[:, b * J:(b + 1) * J, :])

            def ln0_apply(b):
                src = x[:, b * J:(b + 1) * J, :]
                if b >= 1:
                    dve.wait_ge(xnT_ps_done[0], b)
                ln_apply(0, b, src, xn[:, 0])

            def q_low(b):
                dve.wait_ge(q_hi_done, b)
                if b >= 3:
                    dve.wait_ge(q_stack_done[b - 2], 256)
                dve.scalar_tensor_tensor(q_lo[:, b % 2, :], prep_ps[:, :], b_q[:, 0:1], q_hi[:, b % 2, :], ALU.add,
                                         ALU.subtract).then_inc(q_lo_done, 1)

            def maxima(b, j, groups=range(G)):
                for g in groups:
                    u = (b * J + j) * G + g
                    dve.wait_ge(s_ps_done, u + 1)
                    dve.tensor_reduce(mrow[:, b % 2, j, g * GH:(g + 1) * GH], S_ps[u % 2][:, 0:GK].rearrange("p (h k) -> p h k", h=GH),
                                      X, ALU.max).then_inc(max_done, 1)

            def maxima_out(b):
                dve.wait_ge(mT_ps_done, b + 1)
                dve.tensor_copy(mT[0:H, b % 2, :], mT_ps).then_inc(mT_done, 1)
                dve.tensor_reduce(reach[:, b:b + 1], mrow[:, b % 2].rearrange("p j h -> p (j h)"), X, ALU.max,
                                  apply_absolute_value=True)

            def values_out(b):
                dve.wait_ge(v_ps_done, b + 1)
                for c in range(GC):
                    ins = dve.tensor_tensor(v8[0:CW, b, c], v_ps[:, c * D:(c + 1) * D].rearrange("p (g d) -> p g d", g=G),
                                            value_mask[0:CW, c, :].unsqueeze(1).broadcast_to([CW, G, GD]), ALU.mult)
                ins.then_inc(v8_done, 1)

            def normalise(b):
                dve.wait_ge(o_ps_done, b + 1)
                settle(dve.reciprocal(rden[:], den_ps[:, :]))
                dve.tensor_tensor(attT[:], O_ps[:, :], rden[:], ALU.mult).then_inc(attT_done, 1)

            with nc.allow_low_precision("a shift of the exponent that numerator and denominator share"):
                dve.memset(half_neg[:], -0.5).then_inc(half_set, 1)
                dve.memset(ctxT[DC:DC + 1, :, :], 1.0).then_inc(ones_set, 1)
                dve.memset(mT[:], 0.0)
                dve.memset(neg_head[:], 0.0).then_inc(zeroed, 1)
                ln0(0)
                ln0_stats(1)
                dve.wait_ge(ld_bq, 16)
                for g in range(G):
                    for r in range(4):
                        ins = dve.tensor_copy(b_q4[r * GD:(r + 1) * GD, g:g + 1], b_q[g * GD:(g + 1) * GD, 0:1])
                ins.then_inc(b_q4_done, 1)
                ln0_apply(1)
                for u in range(2):
                    dve.wait_ge(k_hi_done, u + 1)
                    for r in (1, 3):
                        part = k_parts[r * GD:(r + 1) * GD, 2 * u:2 * u + 2].rearrange("p g b k -> p g (b k)")
                        ins = dve.scalar_tensor_tensor(part, k4_ps[r * GD:(r + 1) * GD, 2 * u:2 * u + 2, :], float(HD) ** -0.5, part,
                                                       ALU.mult, ALU.subtract)
                    ins.then_inc(k_lo_done, 1)
                for u in range(2):
                    dve.wait_ge(q4_hi_done, u + 1)
                    for g in (2 * u, 2 * u + 1):
                        part = q_stack[2 * GD:, 0, g, :]
                        ins = dve.scalar_tensor_tensor(part, q4_ps[2 * GD:, g, :], b_q4[2 * GD:, g:g + 1], part, ALU.add, ALU.subtract)
                    ins.then_inc(q4_lo_done, 1)
                dve.wait_ge(ld_c32, 16)
                maxima(0, 0)
                ln0_stats(2)
                maxima(0, 1)
                q_low(1)
                maxima(0, 2)
                ln0_apply(2)
                maxima(0, 3)
                for ph in range(B + 3):
                    b = ph
                    for s in range(SLOTS):
                        if b < B and s == 0:
                            maxima_out(b)
                        if b + 1 < B and s >= 4:
                            maxima(b + 1, (s - 4) // 2, range((s % 2) * 2, (s % 2) * 2 + 2))
                        if b + 2 < B and s == 2:
                            q_low(b + 2)
                        if b < B and s == 4:
                            values_out(b)
                        if b + 3 < B and s == 7:
                            ln0_stats(b + 3)
                        if b + 3 < B and s == 10:
                            ln0_apply(b + 3)
                        t = ph - 3
                        if 0 <= t < B and s == 1:
                            dve.wait_ge(lg1_ps_done, t + 1)
                            l = lg[:, t % 2]
                            settle(dve.tensor_tensor(l, logits1, bs_rows[:].unsqueeze(1).broadcast_to([P, J, E]), ALU.add))
                            settle(dve.tensor_reduce(lm[:, t % 2, :], l, X, ALU.max))
                            dve.tensor_tensor(l, l, lm[:, t % 2].unsqueeze(2).broadcast_to([P, J, E]),
                                              ALU.subtract).then_inc(sub2_done, 1)
                        if 0 <= t < B and s == 3:
                            l = lg[:, t % 2]
                            dve.wait_ge(exp2_done, t + 1)
                            settle(dve.tensor_reduce(lm[:, t % 2, :], l, X, ALU.add))
                            settle(dve.reciprocal(lm[:, t % 2, :], lm[:, t % 2, :]))
                            settle(dve.tensor_tensor(xrow[:, t % 2, :, D:ROW], l, lm[:, t % 2].unsqueeze(2).broadcast_to([P, J, E]), ALU.mult))
                            dve.tensor_copy(prob[:, :, t * J:(t + 1) * J].rearrange("p e j -> p j e"),
                                            xrow[:, t % 2, :, D:ROW]).then_inc(prob_done, 1)
                        t = ph - 2
                        if 0 <= t < B:
                            if s == 0:
                                ln_apply(2, t, rtiles(t), xn[:, 2])
                            if s == 5:
                                dve.wait_ge(s1_ps_done, t + 1)
                                sc = tail2_ps[:, 0:J * NK].rearrange("p (j k) -> p j k", j=J)
                                settle(dve.tensor_reduce(m1[:, t % 2, :], sc, X, ALU.max))
                                dve.tensor_tensor(p1[:], sc, m1[:, t % 2].unsqueeze(2).broadcast_to([P, J, NK]),
                                                  ALU.subtract).then_inc(sub1_done, 1)
                            if s == 7:
                                dve.wait_ge(exp1_done, t + 1)
                                settle(dve.tensor_reduce(den1[:, t % 2, :], p1[:], X, ALU.add))
                                dve.reciprocal(r1[:, t % 2, :], den1[:, t % 2, :]).then_inc(r1_done, 1)
                        t = ph - 1
                        if 0 <= t < B:
                            if s == 3:
                                normalise(t)
                            if s == 5:
                                dve.wait_ge(wo_ps_done, t + 1)
                                dve.wait_ge(res0_done, t + 1)
                                settle(dve.tensor_tensor(rtiles(t), tail1_ps[1][:, :].rearrange("p (j d) -> p j d", j=J), rtiles(t), ALU.add))
                                ln_stats(1, rtiles(t))
                            if s == 6:
                                ln_apply(1, t, rtiles(t), xn[:, 1])
                            if s == 9:
                                dve.wait_ge(lg0_ps_done, t + 1)
                                for j in range(J):
                                    ins = dve.max(top0[:, t * J + j, :], logits0[:, j, :])
                                ins.then_inc(top0_done, 1)
                            if s == 10:
                                dve.wait_ge(ffn_ps_done, t + 1)
                                ins = dve.tensor_tensor(rtiles(t), tail1_ps[1][:, :].rearrange("p (j d) -> p j d", j=J), rtiles(t), ALU.add)
                                ins.then_inc(res2_done, 1)
                                dve.wait_ge(res2_done, t + 1)
                                ln_stats(2, rtiles(t))
                        t = ph - 2
                        if 0 <= t < B:
                            if s == 8:
                                dve.wait_ge(o1_ps_done, t + 1)
                                dve.wait_ge(r1_done, t + 1)
                                for j in range(J):
                                    ins = dve.scalar_tensor_tensor(res[:, t * J + j, :], tail2_ps[:, j * P:(j + 1) * P],
                                                                   r1[:, t % 2, j:j + 1], res[:, t * J + j, :], ALU.mult, ALU.add)
                                ins.then_inc(res3_done, 1)
                                dve.wait_ge(res3_done, t + 1)
                                ln_stats(3, rtiles(t))
                            if s == 10:
                                if t >= 2:
                                    dve.wait_ge(rows_out[t - 2], 16)
                                ln_apply(3, t, rtiles(t), xrow[:, t % 2, :, 0:D])

                def threshold(again):
                    dve.memset(thr[:], 0.0)
                    dve.wait_ge(probT_ps_done, again + 1)
                    settle(dve.tensor_copy(probT[:], bank[7][:, 0:P]))
                    for i in range(NSTEP):
                        settle(dve.tensor_tensor(cand[:].bitcast(I32), thr[:, 0:1].bitcast(I32).broadcast_to([P, K]),
                                                 bit_steps[:, i * K:(i + 1) * K], ALU.bitwise_or))
                        for k in range(K):
                            ins = dve.tensor_scalar(passing[:, k, :], probT[:], cand[:, k:k + 1], None, ALU.is_ge, ALU.add,
                                                    accum_out=count16[:, k:k + 1])
                        ins.then_inc(ge_done, 1)
                        dve.wait_ge(cnt_ps_done, i + 1 + again * NSTEP)
                        settle(dve.scalar_tensor_tensor(thr[:, 1:K + 1], bank[6][:, 0:K], CAP - 0.5, cand[:], ALU.is_ge, ALU.mult))
                        settle(dve.tensor_reduce(thr[:, 0:1], thr[:], X, ALU.max))

                def indices(again):
                    dve.tensor_tensor_scan(pre[:], ones16, chosenT[:], 0.0, ALU.mult, ALU.add).then_inc(pre_done, 1)
                    dve.wait_ge(base_ps_done, again + 1)
                    settle(dve.tensor_copy(base[:, 0:1], bank[6][:, 0:1]))
                    settle(dve.tensor_tensor(base[:, 1:2], pre[:, P - 1:P], base[:, 0:1], ALU.add))
                    dve.tensor_scalar(cum[:], pre[:], base[:, 0:1], None, ALU.add)
                    settle(dve.tensor_scalar(past[:], slots16, base[:, 1:2], None, ALU.is_ge))
                    dve.scalar_tensor_tensor(onehot[:], slots16, base[:, 0:1], past[:], ALU.is_ge, ALU.subtract)
                    for e in range(E):
                        ins = dve.tensor_scalar(cumx[:, e, :], cum[:], own[:, e:e + 1], None, ALU.mult)
                        if e % 4 == 3:
                            ins.then_inc(cumx_done, 1)
                    for g in range(2):
                        es = slice(4 * g, 4 * g + 4)
                        for h in range(SH):
                            dve.wait_ge(idx_ps_done, (2 * again + g) * SH + h + 1)
                            ins = dve.tensor_scalar(le[:, h, :, :], bank[2 * h + g][:, :].rearrange("p (e t) -> p e t", e=4),
                                                    slot_no[:, h:h + 1], None, ALU.is_le)
                        settle(ins)
                        settle(dve.tensor_reduce(pcount[:, :, es], le[:], X, ALU.add))
                        for h in range(SH):
                            ins = dve.scalar_tensor_tensor(idx[:, h, es], pcount[:, h, es], float(J), bank[4 + h][:, es],
                                                           ALU.mult, ALU.add)
                        ins.then_inc(idx_done, 1)

                def experts(again):
                    for e in range(E):
                        dve.wait_ge(y_ps_done, again * E + e + 1)
                        settle(dve.tensor_tensor(y[:, e], bank[6 + e % 2][:, 0:CAP].rearrange("p (h d) -> p h d", h=SH),
                                                 b2_rows[:, e, :].unsqueeze(1).broadcast_to([P, SH, D]), ALU.add))
                        dve.tensor_tensor(y[:, e], y[:, e], xin[:, e, :, D + e].unsqueeze(2).broadcast_to([P, SH, D]),
                                          ALU.mult).then_inc(y_done, 1)

                dve.wait_ge(ld_rc, 32)
                dve.wait_ge(prob_done, B)
                threshold(0)
                settle(dve.tensor_scalar(chosenT[:], probT[:], thr[:, 0:1], None, ALU.is_ge))
                indices(0)

                settle(dve.tensor_reduce(suspect[:, 0:1], reach[:], X, ALU.max))
                settle(dve.tensor_scalar(suspect[:, 0:1], suspect[:, 0:1], 0.98 * CLAMP, None, ALU.is_gt))

                def any_false(ok, column):
                    settle(dve.tensor_reduce(suspect[:, column:column + 1], ok, X, ALU.min))
                    settle(dve.tensor_scalar(suspect[:, column:column + 1], suspect[:, column:column + 1], -1.0, 1.0, ALU.mult, ALU.add))

                settle(dve.tensor_reduce(suspect[:, 1:2], kT[:].rearrange("p b k -> p (b k)"), X, ALU.max, apply_absolute_value=True))
                settle(dve.tensor_reduce(suspect[:, 5:6], w_q[:, 0, :], X, ALU.max, apply_absolute_value=True))
                settle(dve.tensor_scalar(suspect[:, 5:6], suspect[:, 5:6], float(D), None, ALU.mult))
                settle(dve.tensor_tensor(suspect[:, 1:2], suspect[:, 1:2], suspect[:, 5:6], ALU.max))
                settle(dve.tensor_tensor(suspect[:, 1:2], suspect[:, 1:2], b_q[:, 0:1], ALU.max))
                settle(dve.tensor_scalar(suspect[:, 5:6], b_q[:, 0:1], -1.0, None, ALU.mult))
                settle(dve.tensor_tensor(suspect[:, 1:2], suspect[:, 1:2], suspect[:, 5:6], ALU.max))
                settle(dve.tensor_scalar(suspect[:, 1:2], suspect[:, 1:2], PART_MAX, None, ALU.is_gt))
                pr = prob[:].rearrange("p e t -> p (e t)")
                settle(dve.tensor_tensor(scratch, pr, pr, ALU.is_equal))
                any_false(scratch, 2)
                settle(dve.tensor_tensor(scratch[:, 0:NT], top0[:, :, 0], top0[:, :, 1], ALU.subtract))
                settle(dve.tensor_scalar(scratch[:, 0:NT], scratch[:, 0:NT], 16.0, None, ALU.is_lt))
                any_false(scratch[:, 0:NT], 3)
                settle(dve.tensor_scalar(suspect[:, 4:5], base[:, 1:2], CAP + 0.5, None, ALU.is_gt))
                dve.tensor_reduce(suspect16[:], suspect[:, 0:5], X, ALU.max).then_inc(suspect_done, 1)
                dve.wait_ge(ld_b2, 16)
                experts(0)
                dve.wait_ge(flag_ps_done, 1)
                dve.tensor_scalar(flag[:], bank[0][0:1, 0:1], 0.5, None, ALU.is_gt).then_inc(flag_done, 1)
                dve.wait_ge(flag_done, 1)
                with dve.If(dve.value_load(flag[0:1, 0:1], min_val=0, max_val=1) > 0):
                    dve.wait_ge(y_ps_done, E)
                    start_general(dve)
                    with dve.Fori(0, NT) as i:
                        find_nan(dve, i)
                    count_nan(dve)
                    with dve.Fori(0, NT) as i:
                        run_tile(dve, i)
                    dve.wait_ge(turn, TURNS_ALL)
                    threshold(1)
                    eq = ge[:, 0]
                    gt = ge[:, 1]
                    settle(dve.tensor_scalar(chosenT[:], probT[:], thr[:, 0:1], None, ALU.is_equal))
                    dve.tensor_scalar(passing[:, 0, :], probT[:], thr[:, 0:1], None, ALU.is_gt).then_inc(chosenT_done, 1)
                    dve.wait_ge(part_ps_done, 1)
                    settle(dve.tensor_copy(eq.rearrange("p e t -> p (e t)"), bank[6][:, 0:P // 2].bitcast(BF16)))
                    settle(dve.tensor_copy(gt.rearrange("p e t -> p (e t)"), bank[7][:, 0:P // 2].bitcast(BF16)))
                    settle(dve.tensor_reduce(eqb[:].rearrange("p (e b) -> p e b", e=E), eq.rearrange("p e (b j) -> p e b j", b=B), X, ALU.add))
                    dve.tensor_reduce(gtb[:], gt, X, ALU.add).then_inc(eq_done, 1)
                    dve.wait_ge(rank_ps_done, 1)
                    settle(dve.tensor_scalar(need[:], bank[7][:, E * B:E * B + E], -1.0, float(CAP), ALU.mult, ALU.add))
                    eb = eqb[:].rearrange("p (e b) -> p e b", e=E)
                    total = bank[7][:, 0:E * B].rearrange("p (e b) -> p e b", e=E)
                    rk = rank[:].rearrange("p e (b j) -> p e b j", b=B)
                    settle(dve.tensor_tensor(rk[:, :, :, 0], bank[6][:, 0:E * B].rearrange("p (e b) -> p e b", e=E), eb, ALU.subtract))
                    for later in range(1, B):
                        for b in range(later):
                            settle(dve.tensor_tensor(rk[:, :, later, 0], rk[:, :, later, 0], total[:, :, b], ALU.add))
                    for j in range(1, J):
                        settle(dve.tensor_tensor(rk[:, :, :, j], rk[:, :, :, j - 1],
                                                 eq.rearrange("p e (b j) -> p e b j", b=B)[:, :, :, j - 1], ALU.add))
                    settle(dve.tensor_tensor(rank[:], rank[:], need[:].unsqueeze(2).broadcast_to([P, E, NT]), ALU.is_lt))
                    settle(dve.tensor_tensor(rank[:], rank[:], eq, ALU.mult))
                    dve.tensor_tensor(chosen[:], rank[:], gt, ALU.add).then_inc(chosen_done, 1)
                    dve.wait_ge(chosenT_ps_done, 1)
                    settle(dve.tensor_copy(chosenT[:], bank[6][:, 0:P // 2].bitcast(BF16)))
                    indices(1)
                    experts(1)

        @block.gpsimd
        def _(pool):
            count = [0]

            def settle(ins):
                count[0] += 1
                ins.then_inc(pool_chain, 1)
                pool.wait_ge(pool_chain, count[0])

            def ln_rstd(n, b):
                pool.wait_ge(var_done[n], b + 1)
                settle(nc.gpsimd.tensor_scalar(ve[:, n, :], mv[:, n, :, 1], EPS, None, ALU.add))
                nc.gpsimd.tensor_tensor(rstd[:, n, :], ve[:, n, :], half_neg[:], ALU.pow).then_inc(rstd_done[n], 1)

            def stack_keys(b):
                nc.gpsimd.tensor_tensor(k_stack[:, b], k_parts[:, :, b, :].unsqueeze(2).broadcast_to([P, G, GH, NK]),
                                        part_mask.unsqueeze(1).unsqueeze(3).broadcast_to([P, G, GH, NK]), ALU.mult).then_inc(k_stack_done, 1)

            def residual(b):
                nc.gpsimd.tensor_tensor(res[:, b * J:(b + 1) * J, :], x[:, b * J:(b + 1) * J, :],
                                        bo_rows[:].unsqueeze(1).broadcast_to([P, J, D]), ALU.add).then_inc(res0_done, 1)

            pool.wait_ge(ld_k, 32)
            nc.gpsimd.tensor_copy(w_k4[:], w_kv[:, 0, :].rearrange("p (g d) -> p g d", g=G).unsqueeze(2).broadcast_to([DC + 1, G, 4, GD])
                                  ).then_inc(w_k4_done, 1)
            pool.wait_ge(half_set, 1)
            ln_rstd(0, 0)
            pool.wait_ge(ld_q0, 16)
            nc.gpsimd.tensor_copy(w_q4[:], w_q[:, 0, :].rearrange("p (g d) -> p g d", g=G).unsqueeze(2).broadcast_to([P, G, 4, GD])
                                  ).then_inc(w_q4_done, 1)
            ln_rstd(0, 1)
            pool.wait_ge(k_lo_done, 2)
            pool.wait_ge(ld_c32, 16)
            stack_keys(0)
            for n, (w, bias) in enumerate((("L0_xattn_Wv", "L0_xattn_bv"), ("L1_xattn_Wk", "L1_xattn_bk"), ("L1_xattn_Wv", "L1_xattn_bv"))):
                pool.dma_start(w_kv[0:DC, n + 1, :], a[w]).then_inc(ld_kv, 16)
                pool.dma_start(w_kv[DC:DC + 1, n + 1, :], a[bias].rearrange("(o d) -> o d", o=1)).then_inc(ld_kv, 16)
            ln_rstd(0, 2)
            stack_keys(1)
            pool.wait_ge(ld_bo, 16)
            residual(0)
            for ph in range(B + 2):
                if ph + 1 < B:
                    residual(ph + 1)
                    if ph >= 1:
                        stack_keys(ph + 1)
                if 0 <= ph - 1 < B:
                    ln_rstd(1, ph - 1)
                if ph + 3 < B:
                    ln_rstd(0, ph + 3)
                if 0 <= ph - 2 < B:
                    ln_rstd(3, ph - 2)
                if 0 <= ph - 1 < B:
                    ln_rstd(2, ph - 1)
            flat = out.rearrange("b t d -> (b t) d")

            def experts(again):
                for e in range(E):
                    pool.wait_ge(idx_done, 2 * again + e // 4 + 1)
                    for h in range(SH):
                        nc.gpsimd.indirect_dma_start(xin[:, e, h, :], None, gather_rows, bass.IndirectOffsetOnAxis(idx[:, h, e:e + 1], 0),
                                                     bounds_check=B * T - 1, oob_is_err=False).then_inc(got[e], 16)
                for e in range(E):
                    n = again * E + e
                    pool.wait_ge(y_done, n + 1)
                    if n >= 1:
                        pool.wait_ge(out_add, 16 * SH * n)
                    for h in range(SH):
                        nc.gpsimd.indirect_dma_start(flat, bass.IndirectOffsetOnAxis(idx[:, h, e:e + 1], 0), y[:, e, h, :], None,
                                                     bounds_check=B * T - 1, oob_is_err=True, compute_op=ALU.add).then_inc(out_add, 16)
                pool.wait_ge(out_add, 16 * SH * E * (again + 1))

            for b in range(B):
                pool.wait_ge(rows_out[b], 16)
            pool.wait_ge(out_base, 16 * B)
            pool.wait_ge(o_ps_done, B)
            experts(0)
            pool.wait_ge(flag_done, 1)
            with pool.If(pool.value_load(flag[0:1, 0:1], min_val=0, max_val=1) > 0):
                start_general(pool)
                with pool.Fori(0, NT) as i:
                    find_nan(pool, i)
                with pool.Fori(0, NT) as i:
                    run_tile(pool, i)
                experts(1)


_INS = ["x", "ctx_768", "L0_xattn_Wq", "L0_xattn_bq", "L0_xattn_Wk", "L0_xattn_bk", "L0_xattn_Wv", "L0_xattn_bv",
        "L0_xattn_Wo", "L0_xattn_bo", "L0_ffn_Ws1", "L0_ffn_Ws2", "L0_ffn_W1", "L0_ffn_W2", "L0_ffn_Wr",
        "L1_xattn_Wq", "L1_xattn_bq", "L1_xattn_Wk", "L1_xattn_bk", "L1_xattn_Wv", "L1_xattn_bv",
        "L1_ffn_Ws", "L1_ffn_bs", "L1_ffn_W1", "L1_ffn_b1", "L1_ffn_W2", "L1_ffn_b2"]


def kernel(**inputs):
    import concourse.bacc as bacc
    from concourse.bass_utils import run_bass_kernel_spmd

    nc = bacc.Bacc("TRN2", target_bir_lowering=False, num_devices=1)
    arrays, args = {}, {}
    for name, v in [(n, np.ascontiguousarray(inputs[n])) for n in _INS] + list(constants().items()):
        arrays[f"in_{name}"] = v
        args[name] = nc.dram_tensor(f"in_{name}", v.shape, mybir.dt.from_np(v.dtype), kind="ExternalInput").ap()
    out = nc.dram_tensor("out_0", (B, T, D), F32, kind="ExternalOutput").ap()
    program(nc, args, out)
    r = run_bass_kernel_spmd(nc, [arrays], core_ids=[0])
    return r.results[0]["out_0"]
```

```python
from contextlib import ExitStack

import numpy as np

import concourse.bass as bass
from concourse import mybir

F32 = mybir.dt.float32
BF16 = mybir.dt.bfloat16
F16 = mybir.dt.float16
I32 = mybir.dt.int32
U16 = mybir.dt.uint16
ALU = mybir.AluOpType
ACT = mybir.ActivationFunctionType
X = mybir.AxisListType.X

P = 128
B, T, D = 4, 512, 128
J = T // P
NT = B * J
NK, DC = 77, 96
H = 16
HD = D // H
HK = H * NK
G = 4
GH = H // G
GK = GH * NK
GC = -(-GK // P)
CW = -(-GK // GC)
CH = G * GC
WINDOW = max(c * CW % NK for c in range(GC)) + CW
GD = GH * HD
E, F = 8, 512
FC = F // P
CAP = B * T // E
SH = CAP // P
F0 = 64
EPS = 1e-5
CLAMP = 1e4
PART_MAX = 256.0
ROW = D + E
BITS = 30
HEAD_GROUPS = ((0, 6), (6, 6), (12, 4))
FAST, SLOTS = 2, CH
SKIP = 2
FIRST = float(np.array([((1 << FAST * SKIP) - 1) << (BITS - FAST * SKIP)], np.int32).view(np.float32)[0])


def chunk_rows(c):
    return min(CW, GK - c * CW)


def constants():
    r = np.arange(P)
    ident = np.eye(P, dtype=np.float32)
    head_mask = (r[:, None] // HD == np.arange(H)[None]).astype(np.float32)
    part_mask = (r[:, None] % GD // HD == np.arange(GH)[None]).astype(np.float32)
    rows = np.arange(GC)[None, :, None] * CW + r[:, None, None]
    own_head = (rows // NK == np.arange(GD)[None, None] // HD) & (r[:, None, None] < CW) & (rows < GK)
    value_mask = own_head.astype(np.float32).reshape(P, GC * GD)
    slot = np.stack([r + P * s for s in range(SH)], 1).astype(np.float32)
    c32 = np.concatenate([ident, head_mask, value_mask, slot], 1)
    prefix = (r[:, None] <= r[None]).astype(np.float32)
    same = r[:, None] // NT == r[None] // NT
    before = (same & (r[:, None] % NT < r[None] % NT)).astype(np.float32)
    ones = np.ones((P, P), np.float32)
    same = same.astype(np.float32)
    slots = np.broadcast_to(np.arange(CAP, dtype=np.float32), (P, CAP))
    neg = -1.0 * (np.arange(HK)[None] // NK == np.arange(H)[:, None]).astype(np.float32)
    c16 = np.ascontiguousarray(np.concatenate([ident, prefix, before, ones, same, slots], 1).view(np.uint16)[:, 1::2])
    neg16 = np.ascontiguousarray(neg.view(np.uint16)[:, 1::2])
    tau = r % NT
    tile_row = ((tau // J) * T + tau % J).astype(np.float32)
    own = (r[:, None] // NT == np.arange(E)[None]).astype(np.float32)
    crow = (own * tile_row[:, None]).astype(np.float16)
    bits = np.array([[k << b for k in range(1 << FAST)] for b in range(BITS - FAST, -1, -FAST)] + [[0] * (1 << FAST)], np.int32)
    cbits = np.broadcast_to(bits.reshape(1, -1), (P, bits.size))
    return {"c_f32": np.concatenate([c32, own, part_mask], 1).copy(), "c_bf16": c16, "c_neg": neg16, "c_rows": crow,
            "c_bits": np.ascontiguousarray(cbits)}


def program(nc, a, out):
    NSTEP = BITS // FAST
    K = 1 << FAST
    with ExitStack() as ctx:
        def sb(name, shape, dt=F32):
            return ctx.enter_context(nc.sbuf_tensor(name, shape, dt))

        def sem(name):
            return ctx.enter_context(nc.semaphore(name))

        gather_rows = nc.dram_tensor("gather_rows", (B * T, ROW), F32).ap()
        psum = ctx.enter_context(nc.psum_tensor("psum", [P, 8, 512], F32))
        bank = [psum[:, i, :] for i in range(8)]

        NV = GC * GD
        c32 = sb("c32", [P, P + H + NV + SH + E + GH])
        ident = c32[:, 0:P]
        head_mask = c32[:, P:P + H]
        value_mask = c32[:, P + H:P + H + NV].rearrange("p (c d) -> p c d", c=GC)
        slot_no = c32[:, P + H + NV:P + H + NV + SH]
        own = c32[:, P + H + NV + SH:P + H + NV + SH + E]
        part_mask = c32[:, P + H + NV + SH + E:]
        c16 = sb("c16", [P, 5 * P + CAP], BF16)
        neg_head = sb("neg_head", [P, HK], BF16)
        ident16, prefix, before, ones16, same16 = (c16[:, i * P:(i + 1) * P] for i in range(5))
        slots16 = c16[:, 5 * P:5 * P + CAP]
        tile_rows = sb("tile_rows", [P, E], F16)
        bit_steps = sb("bit_steps", [P, (NSTEP + 1) * K], I32)
        w_kv = sb("w_kv", [DC + 1, 4, D])
        w_q = sb("w_q", [P, 3, D])
        b_q = sb("b_q", [P, 2])
        bo_rows = sb("bo_rows", [P, D])
        w_s1 = sb("w_s1", [P, F0])
        w_s2 = sb("w_s2", [F0, D])
        w_r = sb("w_r", [P, 2, E])
        bs_rows = sb("bs_rows", [P, E])
        w1 = sb("w1", [P, E, F])
        w2 = sb("w2", [P, E, FC, D])
        b1_rows = sb("b1_rows", [E * FC, P])
        b1 = sb("b1", [P, E * FC])
        b2_rows = sb("b2_rows", [P, E, D])

        x = sb("x", [P, NT, D])
        res = sb("res", [P, NT, D])
        ctx_in = sb("ctx_in", [NK, B, DC])
        ctxT = sb("ctxT", [DC + 1, B, WINDOW])
        kT = sb("kT", [P, B, NK])
        k1T = sb("k1T", [P, B, NK])
        v1 = sb("v1", [NK, B, D])
        w_k4 = sb("w_k4", [DC + 1, G, 4, GD])
        w_q4 = sb("w_q4", [P, G, 4, GD])
        b_q4 = sb("b_q4", [P, G])
        k_parts = sb("k_parts", [P, G, B, NK], F16)
        k_stack = sb("k_stack", [P, B, G, GH, NK], F16)
        q_hi = sb("q_hi", [P, 2, T], F16)
        q_lo = sb("q_lo", [P, 2, T], F16)
        q_stack = sb("q_stack", [P, B, G, T], F16)
        v8 = sb("v8", [P, B, GC, G, GD])
        mrow = sb("mrow", [P, 2, J, H], BF16)
        mT = sb("mT", [P, 2, T], BF16)
        pT = sb("pT", [P, 2, CH, T])
        stats = sb("stats", [P, 4, J, 6])
        mv = sb("mv", [P, 4, J, 2])
        ve = sb("ve", [P, 4, J])
        rstd = sb("rstd", [P, 4, J])
        half_neg = sb("half_neg", [P, J])
        xn = sb("xn", [P, 3, J, D])
        xnT = sb("xnT", [P, 4, T])
        rden = sb("rden", [P, T])
        reach = sb("reach", [P, B])
        attT = sb("attT", [P, T])
        hid = sb("hid", [F0, T])
        hid2 = sb("hid2", [F0, T])
        top0 = sb("top0", [P, NT, E])
        q1T = sb("q1T", [P, T])
        p1 = sb("p1", [P, J, NK])
        m1 = sb("m1", [P, 2, J])
        den1 = sb("den1", [P, 2, J])
        r1 = sb("r1", [P, 2, J])
        p1T = sb("p1T", [NK, T])
        xrow = sb("xrow", [P, 2, J, ROW])
        lg = sb("lg", [P, 2, J, E])
        lm = sb("lm", [P, 2, J])
        prob = sb("prob", [P, E, NT])
        probT = sb("probT", [P, P])
        cand = sb("cand", [P, K])
        follow = sb("follow", [P, K, K])
        ge = sb("ge", [P, 2, E, NT], BF16)
        chosen = sb("chosen", [P, E, NT], BF16)
        chosenT = sb("chosenT", [P, P], BF16)
        passing = sb("passing", [P, K, P], BF16)
        survivors = sb("survivors", [P, K, K])
        count16 = sb("count16", [P, K], BF16)
        pre = sb("pre", [P, P], BF16)
        base = sb("base", [P, 3])
        past = sb("past", [P, CAP], BF16)
        onehot = sb("onehot", [P, CAP], BF16)
        cum = sb("cum", [P, P], BF16)
        cumx = sb("cumx", [P, E, P], BF16)
        le = sb("le", [P, SH, E // 2, P], BF16)
        pcount = sb("pcount", [P, SH, E])
        idx = sb("idx", [P, SH, E], I32)
        xin = pT[:, 0, 0:5, :].rearrange("p a t -> p (a t)")[:, 0:E * SH * ROW].rearrange("p (e s n) -> p e s n", e=E, s=SH)
        xinT = sb("xinT", [P, 2, CAP])
        suspect = sb("suspect", [P, 6])
        scratch = xnT[:, 0, 0:E * NT]
        suspect16 = sb("suspect16", [P, 1], BF16)
        flag = sb("flag", [1, 1], I32)
        hg = pT[:, 1, 0:4, :].rearrange("p a t -> p (a t)").rearrange("p (u c n) -> p u c n", u=2, c=FC)
        y = pT[:, 1, 4:8, :].rearrange("p a t -> p (a t)").rearrange("p (e s n) -> p e s n", e=E, s=SH)

        S_ps, ST_ps = bank[0:2], bank[2:4]
        tail2_ps, tail1_ps, prep_ps = bank[4], bank[5:7], bank[7]

        def logits(ps):
            return ps[:, 0:J * E].rearrange("p (j e) -> p j e", j=J)

        v_ps = prep_ps[0:CW, 0:GC * D]
        mT_ps = prep_ps[0:H, 0:256].bitcast(BF16)
        O_ps, den_ps = tail1_ps
        k4_ps, q4_ps = psum[:, 0:G, 0:B * NK], psum[:, G:2 * G, :]

        ld_x = [sem(f"ld_x{b}") for b in range(B)]
        ld_ctx, ld_c32, ld_c16, ld_kv, ld_q, ld_bo = (sem(n) for n in ("ld_ctx", "ld_c32", "ld_c16", "ld_kv", "ld_q", "ld_bo"))
        ld_neg, ld_k, ld_q0, ld_bq = sem("ld_neg"), sem("ld_k"), sem("ld_q0"), sem("ld_bq")
        ld_ffn, ld_rt, ld_rc, ld_b1, ld_b2 = (sem(n) for n in ("ld_ffn", "ld_rt", "ld_rc", "ld_b1", "ld_b2"))
        ld_w = [sem(f"ld_w{e}") for e in range(E)]
        out_base, out_add = sem("out_base"), sem("out_add")
        rows_out = [sem(f"rows_out{b}") for b in range(B)]
        got = [sem(f"got{e}") for e in range(E)]
        ones_set, ctxT_ps_done, ctxT_done = sem("ones_set"), sem("ctxT_ps_done"), sem("ctxT_done")
        kT_ps_done, kT_done, w_k4_done, w_q4_done = (sem(n) for n in ("kT_ps_done", "kT_done", "w_k4_done", "w_q4_done"))
        k4_ps_done, k_hi_done, k_lo_done, k_stack_done = (sem(n) for n in ("k4_ps_done", "k_hi_done", "k_lo_done", "k_stack_done"))
        q4_ps_done, q4_hi_done, q4_lo_done, b_q4_done = (sem(n) for n in ("q4_ps_done", "q4_hi_done", "q4_lo_done", "b_q4_done"))
        q_hi_done, q_lo_done = sem("q_hi_done"), sem("q_lo_done")
        q_stack_done = [sem(f"q_stack_done{b}") for b in range(B)]
        v_ps_done, v8_done = sem("v_ps_done"), sem("v8_done")
        k1_ps_done, k1_done, v1_ps_done, v1_done = sem("k1_ps_done"), sem("k1_done"), sem("v1_ps_done"), sem("v1_done")
        b1_ps_done, b1_done = sem("b1_ps_done"), sem("b1_done")
        var_done = [sem(f"var_done{n}") for n in range(4)]
        rstd_done = [sem(f"rstd_done{n}") for n in range(4)]
        xn_done = [sem(f"xn_done{n}") for n in range(4)]
        xnT_ps_done = [sem(f"xnT_ps_done{n}") for n in range(4)]
        xnT_done = [sem(f"xnT_done{n}") for n in range(4)]
        q_ps_done = sem("q_ps_done")
        s_ps_done, max_done, mT_ps_done, mT_done = sem("s_ps_done"), sem("max_done"), sem("mT_ps_done"), sem("mT_done")
        st_ps_done, exp_done = sem("st_ps_done"), sem("exp_done")
        o_ps_done, attT_done = sem("o_ps_done"), sem("attT_done")
        wo_ps_done, res1_done, res0_done = sem("wo_ps_done"), sem("res1_done"), sem("res0_done")
        lg0_ps_done, top0_done, hid_ps_done, hid_done, hid2_done = (sem(n) for n in ("lg0_ps_done", "top0_done", "hid_ps_done", "hid_done", "hid2_done"))
        ffn_ps_done, res2_done = sem("ffn_ps_done"), sem("res2_done")
        q1_ps_done, q1_done, s1_ps_done, sub1_done, exp1_done = (sem(n) for n in ("q1_ps_done", "q1_done", "s1_ps_done", "sub1_done", "exp1_done"))
        p1T_ps_done, p1T_done, o1_ps_done, res3_done, r1_done = (sem(n) for n in ("p1T_ps_done", "p1T_done", "o1_ps_done", "res3_done", "r1_done"))
        lg1_ps_done, sub2_done, exp2_done, prob_done = sem("lg1_ps_done"), sem("sub2_done"), sem("exp2_done"), sem("prob_done")
        ge_done, cnt_ps_done = sem("ge_done"), sem("cnt_ps_done")
        probT_ps_done, part_ps_done, chosenT_done = sem("probT_ps_done"), sem("part_ps_done"), sem("chosenT_done")
        chosen_done, chosenT_ps_done, pre_done, base_ps_done, cumx_done, idx_ps_done, idx_done = (
            sem(n) for n in ("chosen_done", "chosenT_ps_done", "pre_done", "base_ps_done", "cumx_done", "idx_ps_done", "idx_done"))
        xinT_ps_done, xinT_done, h_ps_done, gelu_done, y_ps_done, y_done = (
            sem(n) for n in ("xinT_ps_done", "xinT_done", "h_ps_done", "gelu_done", "y_ps_done", "y_done"))
        half_set, zeroed = sem("half_set"), sem("zeroed")
        suspect_done, flag_ps_done, flag_done, turn = sem("suspect_done"), sem("flag_ps_done"), sem("flag_done"), sem("turn")
        eq_done, rank_ps_done, ld_g = sem("eq_done"), sem("rank_ps_done"), sem("ld_g")
        dve_chain, pool_chain = sem("dve_chain"), sem("pool_chain")

        UNITS = B + 1
        halves = ((0, J // 2, (bank[2], bank[3]), bank[5]), (J // 2, J, (bank[0], bank[1]), bank[7]))

        def units(t):
            return [(t, 0, J, tail1_ps, tail2_ps)] if t < B - 1 else [(t + k, *half) for k, half in enumerate(halves)]

        def layer1_slot(t, s):
            if t == B - 2 and s >= 7:
                return s + 3
            return s if t < B - 1 else s - 2

        def router1_slot(t, s):
            return s + 3 if t == B - 2 else s

        def last_unit(t):
            return t + len(units(t))

        def tokens(dram, b):
            return dram[b].rearrange("(p j) d -> p j d", j=J)

        PREFIX = (("fetch", 4), ("rstd0", 2), ("norm0", 1), ("turn0", 1), ("turned0", 1), ("query", 1), ("queried", 1), ("score", 3))
        NAN = PREFIX + (("nan", 6),)
        TILE = PREFIX + (
            ("clip", 6), ("exp", 1), ("weigh", 4), ("weights_T", CH), ("weights_copy", GC), ("attend", CH), ("attended", 4),
            ("att_T", 1), ("att_copy", 1), ("project", 1), ("add_att", 3), ("rstd1", 2), ("norm1", 1), ("turn1", 1), ("turned1", 1),
            ("route", 1), ("top", 3), ("route_exp", 1), ("route_weights", 4))
        for n in range(E + 1):
            TILE += ((f"up{n}", 1), (f"relu{n}", 1), (f"square{n}", 1), (f"down{n}", 1), (f"add{n}", 1))
        TILE += (
            ("stats2", 2), ("rstd2", 2), ("norm2", 1), ("turn2", 1), ("turned2", 1), ("query1", 1), ("queried1", 1), ("score1", 1),
            ("shift1", 3), ("exp1", 1), ("weigh1", 3), ("weights1_T", 1), ("weights1_copy", 1), ("attend1", 1), ("add_att1", 3),
            ("rstd3", 2), ("norm3", 1), ("turn3", 1), ("turned3", 1), ("route1", 1), ("shift2", 3), ("exp2", 1), ("share", 8),
            ("store", 32))
        LOADS = 32
        NAN_N, TILE_N = sum(n for _, n in NAN), sum(n for _, n in TILE)
        AFTER_NAN = LOADS + NT * NAN_N
        FLAGGED = 5
        TURNS_ALL = AFTER_NAN + FLAGGED + NT * TILE_N

        class Turns:

            def __init__(self, eng, stages, name, at):
                self.eng, self.at, self.k = eng, at + sum(n for _, n in stages[:[m for m, _ in stages].index(name)]), 0

            def __call__(self, held=True):
                self.eng.wait_ge(turn, self.at + self.k)
                if not held and self.eng is nc.vector:
                    self.eng.memset(idle[:, 0:1], 0.0)
                if not held and self.eng is nc.gpsimd:
                    self.eng.tensor_tensor(idle[:, 1:2], half_neg[:, 0:1], half_neg[:, 0:1], ALU.add)
                self.k += 1

            def end(self, ins):
                ins.then_inc(turn, 1)

        arena0, arena1 = (pT[:, u].rearrange("p c t -> p (c t)") for u in range(2))
        spans = {}
        at = 0
        for name, n in (("w", HK + CW), ("kbd", HK), ("wT", CH * P), ("x", D), ("n", D), ("nT", D), ("q", D), ("att", D), ("h", D),
                        ("v8", GC * D), ("v1", D), ("k1", NK + 1), ("row", ROW), ("stats", 6), ("mv", 2), ("ve", 1),
                        ("rstd", 1), ("m", H), ("den", H), ("lg", E), ("top", E), ("sel", E), ("a", E), ("b", E), ("one", 4)):
            spans[name] = arena0[:, at:at + n]
            at += n
        kbd = spans["kbd"].rearrange("p (h k) -> p h k", h=H)
        nan_seen, keep, uniform, finite = (arena1[:, 3000 + n:3001 + n] for n in range(4))
        g_w1 = arena1[:, 0:E * F0]
        g_w2 = arena1[0:F0, E * F0:E * F0 + E * D].rearrange("p (e d) -> p e d", e=E)
        eqb, gtb = (c[:] for c in (sb("eqb", [P, E * B], BF16), sb("gtb", [P, E], BF16)))
        need = sb("need", [P, E])
        idle = sb("idle", [P, 2])
        rank = xnT[:, 1, 0:E * NT].rearrange("p (e t) -> p e t", e=E)

        def start_general(eng):
            if eng is nc.vector:
                eng.wait_ge(out_add, 16 * SH * E)
                eng.memset(spans["w"][:, HK:], 0.0).then_inc(half_set, 1)
                eng.memset(finite, 1.0).then_inc(half_set, 1)
                eng.wait_ge(half_set, 3)
            if eng is nc.sync:
                eng.wait_ge(y_done, E)
                eng.wait_ge(out_add, 16 * SH * E)
                eng.dma_start(g_w1.rearrange("p (e f) -> p e f", e=E), a["L0_ffn_W1"].rearrange("e d f -> d e f")).then_inc(turn, 16)
                eng.dma_start(g_w2, a["L0_ffn_W2"].rearrange("e f d -> f e d")).then_inc(ld_g, 16)
                eng.wait_ge(ld_g, 16)
                eng.wait_ge(turn, 16)
                for _ in range(16):
                    eng.sem_inc(turn, 1)

        def prefix_stages(eng, stages, at, i):
            if eng is nc.vector:
                go = Turns(eng, stages, "fetch", at)
                go(); go.end(eng.tensor_copy(spans["x"], x[:, bass.ds(i, 1), :].rearrange("p o d -> p (o d)")))
                go(); go.end(eng.tensor_tensor(kbd, kT[:, bass.ds(i // J, 1), :].broadcast_to([P, H, NK]),
                                               head_mask.unsqueeze(2).broadcast_to([P, H, NK]), ALU.mult))
                layer_stats(eng, go)
                go = Turns(eng, stages, "norm0", at)
                normalised(eng, go, spans["n"])
                go = Turns(eng, stages, "queried", at)
                go(); go.end(eng.tensor_scalar(spans["q"], bank[1][:, 0:P], b_q[:, 0:1], None, ALU.add))
            if eng is nc.gpsimd:
                layer_rstd(eng, Turns(eng, stages, "rstd0", at))
            if eng is nc.tensor:
                go = Turns(eng, stages, "turn0", at)
                go(); go.end(eng.transpose(bank[0][:, 0:P], spans["n"], ident))
                go = Turns(eng, stages, "query", at)
                go(); go.end(eng.matmul(bank[1][:, 0:P], w_q[:, 0, :], spans["nT"], start=True, stop=True))
                go = Turns(eng, stages, "score", at)
                for g, (h0, n) in enumerate(HEAD_GROUPS):
                    go(); go.end(eng.matmul(bank[2 + g][:, 0:n * NK], spans["q"], kbd[:, h0:h0 + n, :].rearrange("p h k -> p (h k)"),
                                            start=True, stop=True))
            if eng is nc.scalar:
                go = Turns(eng, stages, "turned0", at)
                go(); go.end(eng.copy(spans["nT"], bank[0][:, 0:P]))

        def layer_stats(eng, go):
            go(); go.end(eng.bn_stats(spans["stats"], spans["x"]))
            go(held=False); go.end(eng.bn_aggr(spans["mv"], spans["stats"]))

        def layer_rstd(eng, go):
            go(held=False); go.end(eng.tensor_scalar(spans["ve"], spans["mv"][:, 1:2], EPS, None, ALU.add))
            go(); go.end(eng.tensor_tensor(spans["rstd"], spans["ve"], half_neg[:, 0:1], ALU.pow))

        def normalised(eng, go, to):
            go(); go.end(eng.tensor_scalar(to, spans["x"], spans["mv"][:, 0:1], spans["rstd"], ALU.subtract, ALU.mult))

        def find_nan(eng, i):
            at = LOADS + i * NAN_N
            prefix_stages(eng, NAN, at, i)
            if eng is nc.vector:
                go = Turns(eng, NAN, "nan", at)
                w = spans["w"][:, 0:HK]
                for g, (h0, n) in enumerate(HEAD_GROUPS):
                    go(); go.end(eng.tensor_copy(w[:, h0 * NK:(h0 + n) * NK], bank[2 + g][:, 0:n * NK]))
                go(); go.end(eng.tensor_tensor(w, w, w, ALU.is_equal))
                go(); go.end(eng.tensor_reduce(spans["one"][:, 0:1], w, X, ALU.min))
                go(); go.end(eng.tensor_tensor(finite, finite, spans["one"][:, 0:1], ALU.min))

        def count_nan(eng):
            if eng is nc.vector:
                eng.wait_ge(turn, AFTER_NAN)
                eng.tensor_scalar(suspect16[:], finite, -1.0, 1.0, ALU.mult, ALU.add).then_inc(turn, 1)
                eng.wait_ge(turn, AFTER_NAN + 2)
                eng.tensor_scalar(nan_seen, bank[0][:, 0:1], 0.5, None, ALU.is_gt).then_inc(turn, 1)
                eng.wait_ge(turn, AFTER_NAN + 3)
                eng.tensor_scalar(keep, nan_seen, -1.0, 1.0, ALU.mult, ALU.add).then_inc(turn, 1)
                eng.wait_ge(turn, AFTER_NAN + 4)
                eng.tensor_scalar(uniform, nan_seen, 1.0 / NK, None, ALU.mult).then_inc(turn, 1)
            if eng is nc.tensor:
                eng.wait_ge(turn, AFTER_NAN + 1)
                eng.matmul(bank[0][:, 0:1], ones16, suspect16[:], start=True, stop=True).then_inc(turn, 1)

        def run_tile(eng, i):
            at = AFTER_NAN + FLAGGED + i * TILE_N
            prefix_stages(eng, TILE, at, i)

            def stage(name):
                return Turns(eng, TILE, name, at)

            if eng is nc.vector:
                heads = spans["w"][:, 0:HK].rearrange("p (h k) -> p h k", h=H)
                go = stage("clip")
                go(); go.end(eng.tensor_copy(spans["v8"][0:CW], v8[0:CW, bass.ds(i // J, 1)].rearrange("p o c g d -> p (o c g d)")))
                for g, (h0, n) in enumerate(HEAD_GROUPS):
                    go(); go.end(eng.tensor_scalar(spans["w"][:, h0 * NK:(h0 + n) * NK], bank[2 + g][:, 0:n * NK], -CLAMP, CLAMP, ALU.max, ALU.min))
                go(); go.end(eng.tensor_reduce(spans["m"], heads, X, ALU.max))
                go(); go.end(eng.tensor_tensor(heads, heads, spans["m"].unsqueeze(2).broadcast_to([P, H, NK]), ALU.subtract))
                go = stage("weigh")
                go(); go.end(eng.tensor_reduce(spans["den"], heads, X, ALU.add))
                go(); go.end(eng.reciprocal(spans["den"], spans["den"]))
                go(); go.end(eng.tensor_tensor(heads, heads, spans["den"].unsqueeze(2).broadcast_to([P, H, NK]), ALU.mult))
                go(); go.end(eng.tensor_scalar(spans["w"][:, 0:HK], spans["w"][:, 0:HK], keep, uniform, ALU.mult, ALU.add))
                go = stage("attended")
                go(); go.end(eng.tensor_copy(spans["att"], bank[0][:, 0:D]))
                go(); go.end(eng.tensor_copy(spans["k1"][:, 0:NK], k1T[:, bass.ds(i // J, 1), :].rearrange("p o k -> p (o k)")))
                go(); go.end(eng.tensor_copy(spans["v1"][0:NK, :], v1[:, bass.ds(i // J, 1), :].rearrange("p o k -> p (o k)")))
                go(); go.end(eng.tensor_tensor(spans["x"], spans["x"], bo_rows[:], ALU.add))
                go = stage("add_att")
                go(); go.end(eng.tensor_tensor(spans["x"], bank[0][:, 0:D], spans["x"], ALU.add))
                layer_stats(eng, go)
                normalised(eng, stage("norm1"), spans["n"])
                go = stage("top")
                go(); go.end(eng.tensor_copy(spans["lg"], bank[1][:, 0:E]))
                go(held=False); go.end(eng.max(spans["top"], spans["lg"]))
                go(); go.end(eng.tensor_tensor(spans["a"][:, 0:1], spans["top"][:, 1:2], spans["top"][:, 0:1], ALU.subtract))
                go = stage("route_weights")
                go(); go.end(eng.tensor_scalar(spans["a"][:, 0:1], spans["a"][:, 0:1], 1.0, None, ALU.add))
                go(); go.end(eng.reciprocal(spans["a"][:, 0:1], spans["a"][:, 0:1]))
                go(); go.end(eng.tensor_scalar(spans["a"][:, 0:1], spans["a"][:, 0:1], 1.0, None, ALU.is_ge))
                go(); go.end(eng.tensor_scalar(spans["sel"], spans["lg"], spans["top"][:, 0:1], spans["a"][:, 0:1], ALU.is_ge, ALU.mult))
                for n in range(E + 1):
                    go = stage(f"square{n}")
                    go(); go.end(eng.tensor_tensor(spans["h"][0:F0], spans["h"][0:F0], spans["h"][0:F0], ALU.mult))
                    go = stage(f"add{n}")
                    scale = spans["sel"][:, n:n + 1] if n < E else 1.0
                    go(); go.end(eng.scalar_tensor_tensor(spans["x"], bank[3][:, 0:D], scale, spans["x"], ALU.mult, ALU.add))
                layer_stats(eng, stage("stats2"))
                normalised(eng, stage("norm2"), spans["n"])
                go = stage("shift1")
                w1_ = spans["w"][:, 0:NK]
                go(); go.end(eng.tensor_copy(w1_, bank[0][:, 0:NK]))
                go(); go.end(eng.tensor_reduce(spans["one"][:, 0:1], w1_, X, ALU.max))
                go(); go.end(eng.tensor_scalar(w1_, w1_, spans["one"][:, 0:1], None, ALU.subtract))
                go = stage("weigh1")
                go(); go.end(eng.tensor_reduce(spans["one"][:, 0:1], w1_, X, ALU.add))
                go(); go.end(eng.reciprocal(spans["one"][:, 0:1], spans["one"][:, 0:1]))
                go(); go.end(eng.tensor_scalar(w1_, w1_, spans["one"][:, 0:1], None, ALU.mult))
                go = stage("add_att1")
                go(); go.end(eng.tensor_tensor(spans["x"], bank[0][:, 0:D], spans["x"], ALU.add))
                layer_stats(eng, go)
                normalised(eng, stage("norm3"), spans["n"])
                go = stage("shift2")
                go(); go.end(eng.tensor_tensor(spans["lg"], bank[1][:, 0:E], bs_rows[:], ALU.add))
                go(); go.end(eng.tensor_reduce(spans["one"][:, 0:1], spans["lg"], X, ALU.max))
                go(); go.end(eng.tensor_scalar(spans["lg"], spans["lg"], spans["one"][:, 0:1], None, ALU.subtract))
                go = stage("share")
                go(); go.end(eng.tensor_reduce(spans["one"][:, 0:1], spans["lg"], X, ALU.add))
                go(); go.end(eng.reciprocal(spans["one"][:, 0:1], spans["one"][:, 0:1]))
                go(); go.end(eng.tensor_scalar(spans["row"][:, D:ROW], spans["lg"], spans["one"][:, 0:1], None, ALU.mult))
                go(); go.end(eng.tensor_copy(spans["row"][:, 0:D], spans["n"]))
                go(); go.end(eng.tensor_tensor(spans["a"], spans["row"][:, D:ROW], spans["row"][:, D:ROW], ALU.is_equal))
                go(); go.end(eng.tensor_scalar(spans["a"], spans["a"], -1.5, 1.5, ALU.mult, ALU.add))
                go(); go.end(eng.tensor_scalar(spans["b"], spans["row"][:, D:ROW], 0.0, None, ALU.max))
                go(); go.end(eng.tensor_tensor(prob[:, :, bass.ds(i, 1)], spans["a"].unsqueeze(2), spans["b"].unsqueeze(2), ALU.add))
            if eng is nc.gpsimd:
                for n in (1, 2, 3):
                    layer_rstd(eng, stage(f"rstd{n}"))
            if eng is nc.tensor:
                go = stage("weights_T")
                for c in range(GC):
                    for g in range(G):
                        o = g * GK + c * CW
                        go(); go.end(eng.transpose(bank[5 + c][0:CW, g * P:(g + 1) * P], spans["w"][:, o:o + CW], ident))
                go = stage("attend")
                wT = spans["wT"].rearrange("p (c g t) -> p c g t", c=GC, g=G)
                for g in range(G):
                    for c in range(GC):
                        n, o = chunk_rows(c), c * D + g * GD
                        go(); go.end(eng.matmul(bank[0][:, g * GD:(g + 1) * GD], wT[0:n, c, g, :], spans["v8"][0:n, o:o + GD],
                                                start=(c == 0), stop=(c == GC - 1)))

                def turned(name, b, src, rows=P):
                    go = stage(name)
                    go(); go.end(eng.transpose(bank[b][0:rows, 0:P], src, ident))

                def product(name, to, lhsT, rhs):
                    go = stage(name)
                    go(); go.end(eng.matmul(to, lhsT, rhs, start=True, stop=True))

                turned("att_T", 1, spans["att"])
                product("project", bank[0][:, 0:D], spans["nT"], w_q[:, 2, :])
                turned("turn1", 0, spans["n"])
                product("route", bank[1][:, 0:E], spans["nT"], w_r[:, 0, :])
                for n in range(E + 1):
                    product(f"up{n}", bank[2][0:F0, 0:P], g_w1[:, n * F0:(n + 1) * F0] if n < E else w_s1[:], spans["nT"])
                    product(f"down{n}", bank[3][:, 0:D], spans["h"][0:F0, :], g_w2[:, n, :] if n < E else w_s2[:])
                turned("turn2", 0, spans["n"])
                product("query1", bank[1][:, 0:P], w_q[:, 1, :], spans["nT"])
                product("score1", bank[0][:, 0:NK], spans["q"], spans["k1"][:, 0:NK])
                turned("weights1_T", 1, spans["w"][:, 0:NK], NK)
                product("attend1", bank[0][:, 0:D], spans["wT"][0:NK, 0:P], spans["v1"][0:NK, :])
                turned("turn3", 0, spans["n"])
                product("route1", bank[1][:, 0:E], spans["nT"], w_r[:, 1, :])
            if eng is nc.scalar:
                def one(name, to, src, func=ACT.Copy, **more):
                    go = stage(name)
                    go(); go.end(eng.activation(to, src, func, **more))

                one("exp", spans["w"][:, 0:HK], spans["w"][:, 0:HK], ACT.Exp)
                go = stage("weights_copy")
                wT = spans["wT"].rearrange("p (c t) -> p c t", c=GC)
                for c in range(GC):
                    go(); go.end(eng.copy(wT[0:CW, c, :], bank[5 + c][0:CW, :]))
                one("att_copy", spans["nT"], bank[1][:, 0:P])
                one("turned1", spans["nT"], bank[0][:, 0:P])
                one("route_exp", spans["a"][:, 0:1], spans["a"][:, 0:1], ACT.Exp)
                for n in range(E + 1):
                    one(f"relu{n}", spans["h"][0:F0, :], bank[2][0:F0, 0:P], ACT.Relu)
                one("turned2", spans["nT"], bank[0][:, 0:P])
                one("queried1", spans["q"], bank[1][:, 0:P], ACT.Identity, bias=b_q[:, 1:2])
                one("exp1", spans["w"][:, 0:NK], spans["w"][:, 0:NK], ACT.Exp)
                one("weights1_copy", spans["wT"][0:NK, 0:P], bank[1][0:NK, 0:P])
                one("turned3", spans["nT"], bank[0][:, 0:P])
                one("exp2", spans["lg"], spans["lg"], ACT.Exp)
            if eng is nc.sync:
                go = stage("store")
                go()
                eng.dma_start(out.rearrange("b (p j) d -> p b j d", j=J)[:, bass.ds(i // J, 1), bass.ds(i % J, 1), :],
                              spans["x"].rearrange("p (a b d) -> p a b d", a=1, b=1)).then_inc(turn, 16)
                eng.dma_start(gather_rows.rearrange("(b p j) n -> p b j n", b=B, j=J)[:, bass.ds(i // J, 1), bass.ds(i % J, 1), :],
                              spans["row"].rearrange("p (a b d) -> p a b d", a=1, b=1)).then_inc(turn, 16)
        block = ctx.enter_context(nc.Block())

        @block.sync
        def _(sp):
            sp.dma_start(x[:, 0:J, :], tokens(a["x"], 0)).then_inc(ld_x[0], 16)
            sp.dma_start(w_q[:, 0, :], a["L0_xattn_Wq"]).then_inc(ld_q0, 16)
            sp.dma_start(x[:, J:2 * J, :], tokens(a["x"], 1)).then_inc(ld_x[1], 16)
            sp.dma_start(c16[:].bitcast(U16), a["c_bf16"]).then_inc(ld_c16, 16)
            sp.wait_ge(zeroed, 1)
            sp.dma_start(neg_head[0:H, :].bitcast(U16), a["c_neg"]).then_inc(ld_neg, 16)
            for b in range(2, B):
                sp.dma_start(x[:, b * J:(b + 1) * J, :], tokens(a["x"], b)).then_inc(ld_x[b], 16)
            for n, w in ((1, "L1_xattn_Wq"), (2, "L0_xattn_Wo")):
                sp.dma_start(w_q[:, n, :], a[w]).then_inc(ld_q, 16)
            sp.dma_start(b_q[:, 1:2], a["L1_xattn_bq"].rearrange("(d o) -> d o", o=1)).then_inc(ld_q, 16)
            sp.dma_start(bo_rows[:], a["L0_xattn_bo"].rearrange("(o d) -> o d", o=1).broadcast_to([P, D])).then_inc(ld_bo, 16)
            sp.dma_start(w_s1[:], a["L0_ffn_Ws1"]).then_inc(ld_ffn, 16)
            sp.dma_start(w_s2[:], a["L0_ffn_Ws2"]).then_inc(ld_ffn, 16)
            sp.dma_start(w_r[:, 0, :], a["L0_ffn_Wr"]).then_inc(ld_rt, 16)
            sp.dma_start(w_r[:, 1, :], a["L1_ffn_Ws"]).then_inc(ld_rt, 16)
            sp.dma_start(bs_rows[:], a["L1_ffn_bs"].rearrange("(o d) -> o d", o=1).broadcast_to([P, E])).then_inc(ld_rt, 16)
            sp.dma_start(tile_rows[:], a["c_rows"]).then_inc(ld_rc, 16)
            sp.dma_start(bit_steps[:], a["c_bits"]).then_inc(ld_rc, 16)
            sp.dma_start(b1_rows[:], a["L1_ffn_b1"].rearrange("e (c p) -> (e c) p", p=P)).then_inc(ld_b1, 16)
            sp.dma_start(b2_rows[:], a["L1_ffn_b2"].rearrange("(o e) d -> o e d", o=1).broadcast_to([P, E, D])).then_inc(ld_b2, 16)

            def stack_queries(b):
                for r, (part, split) in enumerate(((q_hi, q_hi_done), (q_hi, q_hi_done), (q_lo, q_lo_done), (q_lo, q_lo_done))):
                    if r % 2 == 0:
                        sp.wait_ge(split, b)
                    for g in range(G):
                        sp.dma_start(q_stack[r * GD:(r + 1) * GD, b, g, :],
                                     part[g * GD:(g + 1) * GD, b % 2, :]).then_inc(q_stack_done[b], 16)

            stack_queries(1)
            for ph in range(B + 3):
                if ph + 2 < B:
                    stack_queries(ph + 2)
                if ph == B - 1:
                    for e in range(E):
                        sp.dma_start(w1[:, e, :], a["L1_ffn_W1"][e]).then_inc(ld_w[e], 16)
                        sp.dma_start(w2[:, e, :, :], a["L1_ffn_W2"][e].rearrange("(c p) d -> p c d", p=P)).then_inc(ld_w[e], 16)
                b = ph - 3
                if 0 <= b:
                    sp.wait_ge(prob_done, last_unit(b))
                    sp.dma_start(gather_rows[b * T:(b + 1) * T, :].rearrange("(p j) n -> p j n", j=J),
                                 xrow[:, b % 2, :, :]).then_inc(rows_out[b], 16)
                b = ph - 2
                if 0 <= b < B:
                    sp.wait_ge(res3_done, last_unit(b))
                    sp.dma_start(tokens(out, b), res[:, b * J:(b + 1) * J, :]).then_inc(out_base, 16)
            sp.wait_ge(out_base, 16 * B)
            sp.wait_ge(flag_done, 1)
            with sp.If(sp.value_load(flag[0:1, 0:1], min_val=0, max_val=1) > 0):
                start_general(sp)
                with sp.Fori(0, NT) as i:
                    run_tile(sp, i)
                sp.wait_ge(turn, TURNS_ALL)

        @block.scalar
        def _(act):
            act.dma_start(ctx_in[:], a["ctx_768"].rearrange("b k c -> k b c")).then_inc(ld_ctx, 16)
            act.dma_start(c32[:], a["c_f32"]).then_inc(ld_c32, 16)
            act.dma_start(w_kv[0:DC, 0, :], a["L0_xattn_Wk"]).then_inc(ld_k, 16)
            act.dma_start(w_kv[DC:DC + 1, 0, :], a["L0_xattn_bk"].rearrange("(o d) -> o d", o=1)).then_inc(ld_k, 16)
            act.dma_start(b_q[:, 0:1], a["L0_xattn_bq"].rearrange("(d o) -> d o", o=1)).then_inc(ld_bq, 16)

            def copy_T(n, u, ps, j0=0, j1=J):
                cols = slice(j0 * P, j1 * P)
                act.wait_ge(xnT_ps_done[n], u + 1)
                nc.scalar.copy(xnT[:, n, cols], ps[:, cols]).then_inc(xnT_done[n], 1)

            act.wait_ge(ctxT_ps_done, 1)
            act.wait_ge(ones_set, 1)
            for o in range(0, WINDOW, NK):
                n = min(NK, WINDOW - o)
                ins = nc.scalar.copy(ctxT[0:DC, :, o:o + n],
                                     tail1_ps[1][0:DC, 0:B * NK].rearrange("p (b k) -> p b k", b=B)[:, :, 0:n])
            ins.then_inc(ctxT_done, 1)
            copy_T(0, 0, prep_ps)
            for u in range(2):
                act.wait_ge(k4_ps_done, u + 1)
                nc.scalar.activation(k_parts[:, 2 * u:2 * u + 2].rearrange("p g b k -> p g (b k)"), k4_ps[:, 2 * u:2 * u + 2, :], ACT.Copy,
                                     scale=float(HD) ** -0.5).then_inc(k_hi_done, 1)
            act.wait_ge(b_q4_done, 1)
            for u in range(2):
                act.wait_ge(q4_ps_done, u + 1)
                for g in (2 * u, 2 * u + 1):
                    ins = nc.scalar.activation(q_stack[:, 0, g, :], q4_ps[:, g, :], ACT.Identity, bias=b_q4[:, g:g + 1])
                ins.then_inc(q4_hi_done, 1)

            def q_high(b):
                act.wait_ge(q_ps_done, b)
                if b >= 3:
                    act.wait_ge(q_stack_done[b - 2], 256)
                nc.scalar.activation(q_hi[:, b % 2, :], prep_ps[:, :], ACT.Identity, bias=b_q[:, 0:1]).then_inc(q_hi_done, 1)

            copy_T(0, 1, prep_ps)
            q_high(1)
            for ph in range(B + 3):
                b = ph
                for s in range(SLOTS):
                    if b < B:
                        act.wait_ge(st_ps_done, b * CH + s + 1)
                        if b >= 2 and s == 0:
                            act.wait_ge(o_ps_done, b - 1)
                        n = chunk_rows(s // G)
                        nc.scalar.activation(pT[0:n, b % 2, s, :], ST_ps[s % 2][0:n, :], ACT.Exp).then_inc(exp_done, 1)
                    if b + 2 < B and s == 1:
                        copy_T(0, b + 2, prep_ps)
                    if b + 2 < B and s == 2:
                        q_high(b + 2)
                    if b == 0 and s == 3:
                        act.wait_ge(k1_ps_done, 1)
                        nc.scalar.copy(k1T[:].rearrange("p b k -> p (b k)"), tail2_ps[:, 0:B * NK]).then_inc(k1_done, 1)
                    if b == 0 and s == 5:
                        act.wait_ge(v1_ps_done, 1)
                        nc.scalar.copy(v1[:].rearrange("p b k -> p (b k)"), tail2_ps[0:NK, :]).then_inc(v1_done, 1)
                    if b == 0 and s == 7:
                        act.wait_ge(kT_ps_done, 1)
                        nc.scalar.activation(kT[:].rearrange("p b k -> p (b k)"), tail2_ps[:, 0:B * NK], ACT.Copy,
                                             scale=float(HD) ** -0.5).then_inc(kT_done, 1)
                    if b == 0 and s == 9:
                        act.wait_ge(b1_ps_done, 1)
                        nc.scalar.copy(b1[:], tail2_ps[:, 0:E * FC]).then_inc(b1_done, 1)
                    t = ph - 1
                    for u, j0, j1, ps, _ in units(t) if 0 <= t < B else ():
                        cols = slice(j0 * P, j1 * P)
                        if s == 8:
                            copy_T(1, u, ps[0], j0, j1)
                        if s == 9:
                            act.wait_ge(hid_ps_done, u + 1)
                            nc.scalar.activation(hid[:, cols], ps[1][0:F0, cols], ACT.Relu).then_inc(hid_done, 1)
                            act.wait_ge(hid_done, u + 1)
                            nc.scalar.activation(hid2[:, cols], hid[:, cols], ACT.Square).then_inc(hid2_done, 1)
                    t = ph - 2
                    for u, j0, j1, _, ps in units(t) if 0 <= t < B else ():
                        cols = slice(j0 * P, j1 * P)
                        if s == layer1_slot(t, 2):
                            copy_T(2, u, ps, j0, j1)
                        if s == layer1_slot(t, 3):
                            act.wait_ge(q1_ps_done, u + 1)
                            nc.scalar.activation(q1T[:, cols], ps[:, cols], ACT.Identity, bias=b_q[:, 1:2]).then_inc(q1_done, 1)
                        if s == layer1_slot(t, 5):
                            act.wait_ge(sub1_done, u + 1)
                            nc.scalar.activation(p1[:, j0:j1], p1[:, j0:j1], ACT.Exp).then_inc(exp1_done, 1)
                        if s == layer1_slot(t, 7):
                            act.wait_ge(p1T_ps_done, u + 1)
                            nc.scalar.copy(p1T[:, cols], ps[0:NK, cols]).then_inc(p1T_done, 1)
                    t = ph - 3
                    for u, j0, j1, _, ps in units(t) if 0 <= t < B else ():
                        if s == router1_slot(t, 0):
                            copy_T(3, u, ps, j0, j1)
                        if s == router1_slot(t, 1):
                            act.wait_ge(sub2_done, u + 1)
                            nc.scalar.activation(lg[:, t % 2, j0:j1], lg[:, t % 2, j0:j1], ACT.Exp).then_inc(exp2_done, 1)

            def experts(again):
                for e in range(E):
                    n = again * E + e
                    act.wait_ge(xinT_ps_done, n + 1)
                    nc.scalar.copy(xinT[:, e % 2, :], bank[e % 2][:, 0:CAP]).then_inc(xinT_done, 1)
                    if n >= 2:
                        act.wait_ge(y_ps_done, n - 1)
                    for c in range(FC):
                        act.wait_ge(h_ps_done, n * FC + c + 1)
                        nc.scalar.activation(hg[:, e % 2, c, :], bank[2 + c][:, 0:CAP], ACT.Gelu_apprx_tanh,
                                             bias=b1[:, e * FC + c:e * FC + c + 1]).then_inc(gelu_done, 1)

            act.wait_ge(b1_done, 1)
            experts(0)
            act.wait_ge(flag_done, 1)
            with act.If(act.value_load(flag[0:1, 0:1], min_val=0, max_val=1) > 0):
                with act.Fori(0, NT) as i:
                    find_nan(act, i)
                with act.Fori(0, NT) as i:
                    run_tile(act, i)
                experts(1)

        @block.tensor
        def _(pe):
            def transposes(n, b, ps, j0=0, j1=J):
                src = xrow[:, b % 2, :, 0:D] if n == 3 else xn[:, n]
                for j in range(j0, j1):
                    ins = pe.transpose(ps[:, j * P:(j + 1) * P], src[:, j, :], ident)
                ins.then_inc(xnT_ps_done[n], 1)

            def prep_T(b):
                pe.wait_ge(xn_done[0], b + 1)
                if b == 1:
                    pe.wait_ge(q4_lo_done, 2)
                if b >= 2:
                    pe.wait_ge(mT_done, b - 1)
                if b >= 3:
                    pe.wait_ge(v8_done, b - 2)
                transposes(0, b, prep_ps)

            def prep_q(b):
                pe.wait_ge(xnT_done[0], b + 1)
                pe.matmul(prep_ps[:, :], w_q[:, 0, :], xnT[:, 0, :], start=True, stop=True).then_inc(q_ps_done, 1)

            def scores(b, j, groups=range(G)):
                if j == 0 and groups[0] == 0:
                    if b >= 1:
                        pe.wait_ge(q_stack_done[b], 256)
                    pe.wait_ge(k_stack_done, b + 1)
                for g in groups:
                    u = (b * J + j) * G + g
                    if b == 0 and j == 0 and g % 2 == 0:
                        pe.wait_ge(q4_lo_done, g // 2 + 1)
                    if u >= 2:
                        pe.wait_ge(max_done, u - 1)
                    pe.matmul(S_ps[u % 2][:, 0:GK], q_stack[:, b, g, j * P:(j + 1) * P],
                              k_stack[:, b, g].rearrange("p h k -> p (h k)"), start=True, stop=True).then_inc(s_ps_done, 1)

            def maxima_T(b, j):
                pe.wait_ge(max_done, G * (b * J + j + 1))
                if j == 0:
                    if b == 0:
                        pe.wait_ge(q_lo_done, 1)
                    pe.wait_ge(v8_done, b)
                ins = pe.transpose(mT_ps[:, j * P:(j + 1) * P], mrow[:, b % 2, j, :], ident16)
                if j == J - 1:
                    ins.then_inc(mT_ps_done, 1)

            def values(b):
                for c in range(GC):
                    o = c * CW % NK
                    ins = pe.matmul(v_ps[:, c * D:(c + 1) * D], ctxT[:, b, o:o + CW], w_kv[:, 1, :], start=True, stop=True)
                ins.then_inc(v_ps_done, 1)

            def scores_T(b, s):
                if s == 0:
                    pe.wait_ge(mT_done, b + 1)
                if b * CH + s >= 2:
                    pe.wait_ge(exp_done, b * CH + s - 1)
                c, g = s // G, s % G
                n, o = chunk_rows(c), c * CW
                pe.matmul(ST_ps[s % 2][0:n, :], k_stack[:, b, g].rearrange("p h k -> p (h k)")[:, o:o + n], q_stack[:, b, g, :],
                          start=True, stop=False)
                pe.matmul(ST_ps[s % 2][0:n, :], neg_head[:, g * GK + o:g * GK + o + n], mT[:, b % 2, :], start=False,
                          stop=True).then_inc(st_ps_done, 1)

            def attend(b, c):
                pe.wait_ge(exp_done, b * CH + (c + 1) * G)
                if c == 0:
                    pe.wait_ge(v8_done, b + 1)
                    if b >= 1:
                        pe.wait_ge(res2_done, b)
                        pe.wait_ge(top0_done, b)
                n = chunk_rows(c)
                for to, of in ((O_ps, None), (den_ps, value_mask)):
                    for g in range(G):
                        lhsT = v8[0:n, b, c, g, :] if of is None else of[0:n, c, :]
                        ins = pe.matmul(to[g * GD:(g + 1) * GD, :], lhsT, pT[0:n, b % 2, c * G + g, :], start=(c == 0),
                                        stop=(c == GC - 1), tile_position=(0, g * GD))
                if c == GC - 1:
                    ins.then_inc(o_ps_done, 1)

            pe.wait_ge(ld_ctx, 16)
            pe.wait_ge(ld_c32, 16)
            for b in range(B):
                ins = pe.transpose(tail1_ps[1][0:DC, b * NK:(b + 1) * NK], ctx_in[:, b, :], ident[0:NK, 0:NK])
            ins.then_inc(ctxT_ps_done, 1)
            prep_T(0)
            pe.wait_ge(ctxT_done, 1)
            pe.wait_ge(w_k4_done, 1)
            for g in range(G):
                ins = pe.matmul(k4_ps[:, g, :], w_k4[:, g].rearrange("p r d -> p (r d)"), ctxT[:, :, 0:NK], start=True, stop=True)
                if g % 2:
                    ins.then_inc(k4_ps_done, 1)
            pe.wait_ge(xnT_done[0], 1)
            pe.wait_ge(w_q4_done, 1)
            for g in range(G):
                ins = pe.matmul(q4_ps[:, g, :], w_q4[:, g].rearrange("p r d -> p (r d)"), xnT[:, 0, :], start=True, stop=True)
                if g % 2:
                    ins.then_inc(q4_ps_done, 1)
            for j in range(J):
                scores(0, j)
                if j == 0:
                    prep_T(1)
                if j == 1:
                    prep_q(1)
                if j == 2:
                    pe.wait_ge(ld_c16, 16)
                if j >= 2:
                    maxima_T(0, j - 2)
            maxima_T(0, J - 2)
            pe.wait_ge(ld_neg, 16)

            for ph in range(B + 3):
                b = ph
                for s in range(SLOTS):
                    t = ph - 1
                    if b < B and s == 0:
                        maxima_T(b, J - 1)
                    if 0 <= t < B and s < GC - 1:
                        attend(t, s + 1)
                    if b < B:
                        scores_T(b, s)
                        if b + 2 < B and s == 1:
                            prep_T(b + 2)
                        if b + 2 < B and s == 2:
                            prep_q(b + 2)
                        if b + 1 < B:
                            if s >= 4:
                                scores(b + 1, (s - 4) // 2, range((s % 2) * 2, (s % 2) * 2 + 2))
                            if s in (6, 8, 10):
                                maxima_T(b + 1, s // 2 - 3)
                        if s == 3:
                            pe.wait_ge(q_lo_done, min(b + 2, B - 1))
                            if b == 0:
                                pe.wait_ge(ld_kv, 96)
                            values(b)
                    if b == 0 and s == 3:
                        pe.matmul(tail2_ps[:, 0:B * NK], w_kv[:, 2, :], ctxT[:, :, 0:NK], start=True, stop=True).then_inc(k1_ps_done, 1)
                    if b == 0 and s == 5:
                        pe.wait_ge(k1_done, 1)
                        for c in range(B):
                            ins = pe.matmul(tail2_ps[0:NK, c * D:(c + 1) * D], ctxT[:, c, 0:NK], w_kv[:, 3, :], start=True, stop=True)
                        ins.then_inc(v1_ps_done, 1)
                    if b == 0 and s == 7:
                        pe.wait_ge(v1_done, 1)
                        pe.matmul(tail2_ps[:, 0:B * NK], w_kv[:, 0, :], ctxT[:, :, 0:NK], start=True, stop=True).then_inc(kT_ps_done, 1)
                    if b == 0 and s == 9:
                        pe.wait_ge(kT_done, 1)
                        pe.wait_ge(ld_b1, 16)
                        pe.transpose(tail2_ps[:, 0:E * FC], b1_rows[:], ident[0:E * FC, 0:E * FC]).then_inc(b1_ps_done, 1)
                    for u, j0, j1, ps, _ in units(t) if 0 <= t < B else ():
                        cols = slice(j0 * P, j1 * P)
                        if s == 5:
                            pe.wait_ge(attT_done, u + 1)
                            if t == 0:
                                pe.wait_ge(ld_q, 48)
                            for j in range(j0, j1):
                                ins = pe.matmul(ps[1][:, j * P:(j + 1) * P], attT[:, j * P:(j + 1) * P], w_q[:, 2, :],
                                                start=True, stop=True)
                            ins.then_inc(wo_ps_done, 1)
                        if s == 8:
                            pe.wait_ge(xn_done[1], u + 1)
                            transposes(1, t, ps[0], j0, j1)
                        if s == 9:
                            pe.wait_ge(xnT_done[1], u + 1)
                            if t == 0:
                                pe.wait_ge(ld_ffn, 32)
                                pe.wait_ge(ld_rt, 48)
                            pe.matmul(ps[1][0:F0, cols], w_s1[:], xnT[:, 1, cols], start=True, stop=True).then_inc(hid_ps_done, 1)
                        if s == 9:
                            for j in range(j0, j1):
                                ins = pe.matmul(logits(ps[0])[:, j, :], xnT[:, 1, j * P:(j + 1) * P], w_r[:, 0, :], start=True, stop=True)
                            ins.then_inc(lg0_ps_done, 1)
                        if s == 11:
                            pe.wait_ge(hid2_done, u + 1)
                            for j in range(j0, j1):
                                ins = pe.matmul(ps[1][:, j * P:(j + 1) * P], hid2[:, j * P:(j + 1) * P], w_s2[:],
                                                start=True, stop=True)
                            ins.then_inc(ffn_ps_done, 1)
                    if b < B and s == 11:
                        attend(b, 0)
                    t = ph - 2
                    for u, j0, j1, _, ps in units(t) if 0 <= t < B else ():
                        cols = slice(j0 * P, j1 * P)
                        if s == layer1_slot(t, 2):
                            pe.wait_ge(xn_done[2], u + 1)
                            if t == 0:
                                pe.wait_ge(b1_done, 1)
                            elif t < B - 1:
                                pe.wait_ge(sub2_done, t)
                            transposes(2, t, ps, j0, j1)
                        if s == layer1_slot(t, 3):
                            pe.wait_ge(xnT_done[2], u + 1)
                            pe.matmul(ps[:, cols], w_q[:, 1, :], xnT[:, 2, cols], start=True, stop=True).then_inc(q1_ps_done, 1)
                        if s == layer1_slot(t, 4):
                            pe.wait_ge(q1_done, u + 1)
                            for j in range(j0, j1):
                                ins = pe.matmul(ps[:, j * NK:(j + 1) * NK], q1T[:, j * P:(j + 1) * P], k1T[:, t, :],
                                                start=True, stop=True)
                            ins.then_inc(s1_ps_done, 1)
                        if s == layer1_slot(t, 7):
                            pe.wait_ge(exp1_done, u + 1)
                            for j in range(j0, j1):
                                ins = pe.transpose(ps[0:NK, j * P:(j + 1) * P], p1[:, j, :], ident)
                            ins.then_inc(p1T_ps_done, 1)
                        if s == layer1_slot(t, 8):
                            pe.wait_ge(p1T_done, u + 1)
                            for j in range(j0, j1):
                                ins = pe.matmul(ps[:, j * P:(j + 1) * P], p1T[:, j * P:(j + 1) * P], v1[:, t, :],
                                                start=True, stop=True)
                            ins.then_inc(o1_ps_done, 1)
                    t = ph - 3
                    for u, j0, j1, _, ps in units(t) if 0 <= t < B else ():
                        if s == router1_slot(t, 0):
                            pe.wait_ge(xn_done[3], u + 1)
                            transposes(3, t, ps, j0, j1)
                        if s == router1_slot(t, 1):
                            pe.wait_ge(xnT_done[3], u + 1)
                            for j in range(j0, j1):
                                ins = pe.matmul(logits(ps)[:, j, :], xnT[:, 3, j * P:(j + 1) * P], w_r[:, 1, :], start=True, stop=True)
                            ins.then_inc(lg1_ps_done, 1)

            def threshold(again):
                pe.transpose(bank[7][:, 0:P], prob[:].rearrange("p e t -> p (e t)"), ident).then_inc(probT_ps_done, 1)
                for i in range(0 if again else SKIP, NSTEP):
                    pe.wait_ge(ge_done, i - SKIP + 1 + again * NSTEP)
                    pe.matmul(bank[6][:, 0:K], same16, count16[:], start=True, stop=True).then_inc(cnt_ps_done, 1)

            def indices(again):
                pe.wait_ge(pre_done, again + 1)
                pe.matmul(bank[6][:, 0:1], before, pre[:, P - 1:P], start=True, stop=True)
                pe.matmul(bank[6][:, 1:2], same16, pre[:, P - 1:P], start=True, stop=True).then_inc(base_ps_done, 1)
                for g in range(2):
                    pe.wait_ge(cumx_done, 2 * again + g + 1)
                    for h in range(SH):
                        oh = onehot[:, h * P:(h + 1) * P]
                        if g == 0:
                            pe.matmul(bank[4 + h][:, 0:E], oh, tile_rows[:], start=True, stop=True)
                        pe.matmul(bank[2 * h + g][:, :], oh, cumx[:, 4 * g:4 * g + 4, :].rearrange("p e t -> p (e t)"), start=True,
                                  stop=True).then_inc(idx_ps_done, 1)

            def rows_T(again, e):
                n = again * E + e
                pe.wait_ge(got[e], 16 * SH * (again + 1))
                if e >= 2:
                    pe.wait_ge(xinT_done, n - 1)
                else:
                    pe.wait_ge(idx_done, 2 * again + 2)
                for h in range(SH):
                    ins = pe.transpose(bank[e % 2][:, h * P:(h + 1) * P], xin[:, e, h, 0:D], ident)
                ins.then_inc(xinT_ps_done, 1)

            def experts(again):
                rows_T(again, 0)
                for e in range(E):
                    n = again * E + e
                    pe.wait_ge(xinT_done, n + 1)
                    pe.wait_ge(ld_w[e], 32)
                    for c in range(FC):
                        if n >= 1:
                            pe.wait_ge(gelu_done, (n - 1) * FC + c + 1)
                        pe.matmul(bank[2 + c][:, 0:CAP], w1[:, e, c * P:(c + 1) * P], xinT[:, e % 2, :], start=True,
                                  stop=True).then_inc(h_ps_done, 1)
                    if e + 1 < E:
                        rows_T(again, e + 1)
                    if n >= 2:
                        pe.wait_ge(y_done, n - 1)
                    for h in range(SH):
                        for c in range(FC):
                            if h == 0:
                                pe.wait_ge(gelu_done, n * FC + c + 1)
                            ins = pe.matmul(bank[6 + e % 2][:, h * P:(h + 1) * P], hg[:, e % 2, c, h * P:(h + 1) * P], w2[:, e, c, :],
                                            start=(c == 0), stop=(c == FC - 1))
                    ins.then_inc(y_ps_done, 1)

            pe.wait_ge(prob_done, UNITS)
            threshold(0)
            indices(0)
            experts(0)
            pe.wait_ge(suspect_done, 1)
            pe.matmul(bank[0][0:1, 0:1], ones16[:, 0:1], suspect16[:], start=True, stop=True).then_inc(flag_ps_done, 1)
            pe.wait_ge(flag_done, 1)
            with pe.If(pe.value_load(flag[0:1, 0:1], min_val=0, max_val=1) > 0):
                with pe.Fori(0, NT) as i:
                    find_nan(pe, i)
                count_nan(pe)
                with pe.Fori(0, NT) as i:
                    run_tile(pe, i)
                pe.wait_ge(turn, TURNS_ALL)
                threshold(1)
                pe.wait_ge(chosenT_done, 1)
                pe.transpose(bank[6][:, 0:P // 2].bitcast(BF16), chosenT[:], ident16)
                pe.transpose(bank[7][:, 0:P // 2].bitcast(BF16), passing[:, 0, :], ident16).then_inc(part_ps_done, 1)
                pe.wait_ge(eq_done, 1)
                pe.matmul(bank[6][:, 0:E * B], prefix, eqb[:], start=True, stop=True)
                pe.matmul(bank[7][:, 0:E * B], ones16, eqb[:], start=True, stop=True)
                pe.matmul(bank[7][:, E * B:E * B + E], ones16, gtb[:], start=True, stop=True).then_inc(rank_ps_done, 1)
                pe.wait_ge(chosen_done, 1)
                pe.transpose(bank[6][:, 0:P // 2].bitcast(BF16), chosen[:].rearrange("p e t -> p (e t)"), ident16).then_inc(chosenT_ps_done, 1)
                indices(1)
                experts(1)

        @block.vector
        def _(dve):
            count = [0]

            def settle(ins):
                count[0] += 1
                ins.then_inc(dve_chain, 1)
                dve.wait_ge(dve_chain, count[0])

            def ln_stats(n, src, j0=0, j1=J):
                for j in range(j0, j1):
                    ins = dve.bn_stats(stats[:, n, j, :], src[:, j, :])
                settle(ins)
                for j in range(j0, j1):
                    ins = dve.bn_aggr(mv[:, n, j, :], stats[:, n, j, :])
                ins.then_inc(var_done[n], 1)

            def ln_apply(n, u, src, dst, j0=0, j1=J):
                dve.wait_ge(rstd_done[n], u + 1)
                for j in range(j0, j1):
                    ins = dve.tensor_scalar(dst[:, j, :], src[:, j, :], mv[:, n, j, 0:1], rstd[:, n, j:j + 1],
                                            ALU.subtract, ALU.mult)
                ins.then_inc(xn_done[n], 1)

            def rtiles(b):
                return res[:, b * J:(b + 1) * J, :]


            def add_attention1(t):
                for u, j0, j1, _, ps in units(t):
                    dve.wait_ge(o1_ps_done, u + 1)
                    dve.wait_ge(r1_done, u + 1)
                    for j in range(j0, j1):
                        ins = dve.scalar_tensor_tensor(res[:, t * J + j, :], ps[:, j * P:(j + 1) * P],
                                                       r1[:, t % 2, j:j + 1], res[:, t * J + j, :], ALU.mult, ALU.add)
                    ins.then_inc(res3_done, 1)
                    dve.wait_ge(res3_done, u + 1)
                    ln_stats(3, rtiles(t), j0, j1)

            def ln3_apply(t):
                if t >= 2:
                    dve.wait_ge(rows_out[t - 2], 16)
                for u, j0, j1, _, _ in units(t):
                    ln_apply(3, u, rtiles(t), xrow[:, t % 2, :, 0:D], j0, j1)

            def ln0_stats(b):
                dve.wait_ge(ld_x[b], 16)
                ln_stats(0, x[:, b * J:(b + 1) * J, :])

            def ln0_apply(b):
                src = x[:, b * J:(b + 1) * J, :]
                if b >= 1:
                    dve.wait_ge(xnT_ps_done[0], b)
                ln_apply(0, b, src, xn[:, 0])

            def q_low(b):
                dve.wait_ge(q_hi_done, b)
                if b >= 3:
                    dve.wait_ge(q_stack_done[b - 2], 256)
                dve.scalar_tensor_tensor(q_lo[:, b % 2, :], prep_ps[:, :], b_q[:, 0:1], q_hi[:, b % 2, :], ALU.add,
                                         ALU.subtract).then_inc(q_lo_done, 1)

            def maxima(b, j, groups=range(G)):
                for g in groups:
                    u = (b * J + j) * G + g
                    dve.wait_ge(s_ps_done, u + 1)
                    dve.tensor_reduce(mrow[:, b % 2, j, g * GH:(g + 1) * GH], S_ps[u % 2][:, 0:GK].rearrange("p (h k) -> p h k", h=GH),
                                      X, ALU.max).then_inc(max_done, 1)

            def maxima_out(b):
                dve.wait_ge(mT_ps_done, b + 1)
                dve.tensor_copy(mT[0:H, b % 2, :], mT_ps).then_inc(mT_done, 1)
                dve.tensor_reduce(reach[:, b:b + 1], mrow[:, b % 2].rearrange("p j h -> p (j h)"), X, ALU.max,
                                  apply_absolute_value=True)

            def values_out(b):
                dve.wait_ge(v_ps_done, b + 1)
                for c in range(GC):
                    ins = dve.tensor_tensor(v8[0:CW, b, c], v_ps[:, c * D:(c + 1) * D].rearrange("p (g d) -> p g d", g=G),
                                            value_mask[0:CW, c, :].unsqueeze(1).broadcast_to([CW, G, GD]), ALU.mult)
                ins.then_inc(v8_done, 1)

            def normalise(b):
                dve.wait_ge(o_ps_done, b + 1)
                for _, j0, j1, _, _ in units(b):
                    cols = slice(j0 * P, j1 * P)
                    settle(dve.reciprocal(rden[:, cols], den_ps[:, cols]))
                    dve.tensor_tensor(attT[:, cols], O_ps[:, cols], rden[:, cols], ALU.mult).then_inc(attT_done, 1)

            with nc.allow_low_precision("a shift of the exponent that numerator and denominator share"):
                dve.memset(half_neg[:], -0.5).then_inc(half_set, 1)
                dve.memset(ctxT[DC:DC + 1, :, :], 1.0).then_inc(ones_set, 1)
                dve.memset(mT[:], 0.0)
                dve.memset(neg_head[:], 0.0).then_inc(zeroed, 1)
                ln0_stats(0)
                dve.wait_ge(ld_k, 32)
                dve.tensor_copy(w_k4[:], w_kv[:, 0, :].rearrange("p (g d) -> p g d", g=G).unsqueeze(2).broadcast_to([DC + 1, G, 4, GD])
                                ).then_inc(w_k4_done, 1)
                ln0_apply(0)
                dve.wait_ge(ld_q0, 16)
                dve.tensor_copy(w_q4[:], w_q[:, 0, :].rearrange("p (g d) -> p g d", g=G).unsqueeze(2).broadcast_to([P, G, 4, GD])
                                ).then_inc(w_q4_done, 1)
                ln0_stats(1)
                dve.wait_ge(ld_bq, 16)
                for g in range(G):
                    for r in range(4):
                        ins = dve.tensor_copy(b_q4[r * GD:(r + 1) * GD, g:g + 1], b_q[g * GD:(g + 1) * GD, 0:1])
                ins.then_inc(b_q4_done, 1)
                ln0_apply(1)
                for u in range(2):
                    dve.wait_ge(k_hi_done, u + 1)
                    for r in (1, 3):
                        part = k_parts[r * GD:(r + 1) * GD, 2 * u:2 * u + 2].rearrange("p g b k -> p g (b k)")
                        ins = dve.scalar_tensor_tensor(part, k4_ps[r * GD:(r + 1) * GD, 2 * u:2 * u + 2, :], float(HD) ** -0.5, part,
                                                       ALU.mult, ALU.subtract)
                    ins.then_inc(k_lo_done, 1)
                for u in range(2):
                    dve.wait_ge(q4_hi_done, u + 1)
                    for g in (2 * u, 2 * u + 1):
                        part = q_stack[2 * GD:, 0, g, :]
                        ins = dve.scalar_tensor_tensor(part, q4_ps[2 * GD:, g, :], b_q4[2 * GD:, g:g + 1], part, ALU.add, ALU.subtract)
                    ins.then_inc(q4_lo_done, 1)
                dve.wait_ge(ld_c32, 16)
                maxima(0, 0)
                ln0_stats(2)
                maxima(0, 1)
                q_low(1)
                maxima(0, 2)
                ln0_apply(2)
                maxima(0, 3)
                for ph in range(B + 3):
                    b = ph
                    for s in range(SLOTS):
                        if b < B and s == 0:
                            maxima_out(b)
                        if b + 1 < B and s >= 4:
                            maxima(b + 1, (s - 4) // 2, range((s % 2) * 2, (s % 2) * 2 + 2))
                        if b + 2 < B and s == 2:
                            q_low(b + 2)
                        if b < B and s == 4:
                            values_out(b)
                        if b + 3 < B and s == 3:
                            ln0_stats(b + 3)
                        if b + 3 < B and s == 10:
                            ln0_apply(b + 3)
                        t = ph - 2
                        for u, j0, j1, _, _ in units(t) if 0 <= t < B and s == 0 else ():
                            ln_apply(2, u, rtiles(t), xn[:, 2], j0, j1)
                        if ph == B + 1 and s == 0:
                            add_attention1(B - 2)
                            ln3_apply(B - 2)
                        t = ph - 3
                        for u, j0, j1, _, ps in units(t) if 0 <= t < B else ():
                            js = slice(j0, j1)
                            l, m = lg[:, t % 2, js], lm[:, t % 2, js]
                            m_rows = m.unsqueeze(2).broadcast_to([P, j1 - j0, E])
                            if s == router1_slot(t, 1):
                                dve.wait_ge(lg1_ps_done, u + 1)
                                settle(dve.tensor_tensor(l, logits(ps)[:, js], bs_rows[:].unsqueeze(1).broadcast_to([P, j1 - j0, E]), ALU.add))
                                settle(dve.tensor_reduce(m, l, X, ALU.max))
                                dve.tensor_tensor(l, l, m_rows, ALU.subtract).then_inc(sub2_done, 1)
                            if s == router1_slot(t, 3):
                                dve.wait_ge(exp2_done, u + 1)
                                settle(dve.tensor_reduce(m, l, X, ALU.add))
                                settle(dve.reciprocal(m, m))
                                settle(dve.tensor_tensor(xrow[:, t % 2, js, D:ROW], l, m_rows, ALU.mult))
                                dve.tensor_copy(prob[:, :, t * J + j0:t * J + j1].rearrange("p e j -> p j e"),
                                                xrow[:, t % 2, js, D:ROW]).then_inc(prob_done, 1)
                        t = ph - 2
                        for u, j0, j1, _, ps in units(t) if 0 <= t < B else ():
                            js = slice(j0, j1)
                            if s == layer1_slot(t, 4):
                                dve.wait_ge(s1_ps_done, u + 1)
                                sc = ps[:, 0:J * NK].rearrange("p (j k) -> p j k", j=J)[:, js]
                                settle(dve.tensor_reduce(m1[:, t % 2, js], sc, X, ALU.max))
                                dve.tensor_tensor(p1[:, js], sc, m1[:, t % 2, js].unsqueeze(2).broadcast_to([P, j1 - j0, NK]),
                                                  ALU.subtract).then_inc(sub1_done, 1)
                            if s == layer1_slot(t, 7):
                                dve.wait_ge(exp1_done, u + 1)
                                settle(dve.tensor_reduce(den1[:, t % 2, js], p1[:, js], X, ALU.add))
                                dve.reciprocal(r1[:, t % 2, js], den1[:, t % 2, js]).then_inc(r1_done, 1)
                        t = ph - 1
                        if 0 <= t < B and s == 2:
                            normalise(t)
                        for u, j0, j1, ps, _ in units(t) if 0 <= t < B else ():
                            added = ps[1][:, :].rearrange("p (j d) -> p j d", j=J)[:, j0:j1]
                            stream = rtiles(t)[:, j0:j1]
                            if s == 5:
                                dve.wait_ge(wo_ps_done, u + 1)
                                dve.wait_ge(res0_done, t + 1)
                                settle(dve.tensor_tensor(stream, added, stream, ALU.add))
                                ln_stats(1, rtiles(t), j0, j1)
                            if s == 7:
                                ln_apply(1, u, rtiles(t), xn[:, 1], j0, j1)
                            if s == (10 if t < B - 1 else 11):
                                dve.wait_ge(lg0_ps_done, u + 1)
                                for j in range(j0, j1):
                                    ins = dve.max(top0[:, t * J + j, :], logits(ps[0])[:, j, :])
                                ins.then_inc(top0_done, 1)
                            if s == 11:
                                dve.wait_ge(ffn_ps_done, u + 1)
                                dve.tensor_tensor(stream, added, stream, ALU.add).then_inc(res2_done, 1)
                                dve.wait_ge(res2_done, u + 1)
                                ln_stats(2, rtiles(t), j0, j1)
                        t = ph - 2
                        if 0 <= t < B and t != B - 2 and s == layer1_slot(t, 8):
                            add_attention1(t)
                        if 0 <= t < B and t != B - 2 and s == 10:
                            ln3_apply(t)

                def threshold(again):
                    bits = bit_steps[:].rearrange("p (i k) -> p i k", k=K)
                    dve.memset(count16[:], float(CAP))
                    settle(dve.memset(follow[:], 0.0 if again else FIRST))
                    first = 0 if again else SKIP
                    dve.tensor_tensor(cand[:].bitcast(I32), follow[:, 0, :].bitcast(I32), bits[:, first, :], ALU.bitwise_or)
                    dve.wait_ge(probT_ps_done, again + 1)
                    settle(dve.tensor_copy(probT[:], bank[7][:, 0:P]))
                    for i in range(first, NSTEP):
                        for k in range(1, K):
                            ins = dve.tensor_scalar(passing[:, k, :], probT[:], cand[:, k:k + 1], None, ALU.is_ge, ALU.add,
                                                    accum_out=count16[:, k:k + 1])
                        ins.then_inc(ge_done, 1)
                        settle(dve.tensor_tensor(follow[:].bitcast(I32), cand[:].bitcast(I32).unsqueeze(2).broadcast_to([P, K, K]),
                                                 bits[:, i + 1, :].unsqueeze(1).broadcast_to([P, K, K]), ALU.bitwise_or))
                        dve.wait_ge(cnt_ps_done, i - SKIP + 1 + again * NSTEP)
                        settle(dve.scalar_tensor_tensor(survivors[:], bank[6][:, 0:K].unsqueeze(2).broadcast_to([P, K, K]), CAP - 0.5,
                                                        follow[:], ALU.is_ge, ALU.mult))
                        settle(dve.tensor_reduce(cand[:], survivors[:].rearrange("p j k -> p k j"), X, ALU.max))

                def indices(again):
                    dve.tensor_tensor_scan(pre[:], ones16, chosenT[:], 0.0, ALU.mult, ALU.add).then_inc(pre_done, 1)
                    dve.wait_ge(base_ps_done, again + 1)
                    settle(dve.tensor_copy(base[:, 0:1], bank[6][:, 0:1]))
                    dve.tensor_scalar(base[:, 2:3], bank[6][:, 1:2], float(CAP), None, ALU.is_equal)
                    settle(dve.tensor_tensor(base[:, 1:2], pre[:, P - 1:P], base[:, 0:1], ALU.add))
                    dve.tensor_scalar(cum[:], pre[:], base[:, 0:1], None, ALU.add)
                    settle(dve.tensor_scalar(past[:], slots16, base[:, 1:2], None, ALU.is_ge))
                    dve.scalar_tensor_tensor(onehot[:], slots16, base[:, 0:1], past[:], ALU.is_ge, ALU.subtract)
                    for e in range(E):
                        ins = dve.tensor_scalar(cumx[:, e, :], cum[:], own[:, e:e + 1], None, ALU.mult)
                        if e % 4 == 3:
                            ins.then_inc(cumx_done, 1)
                    for g in range(2):
                        es = slice(4 * g, 4 * g + 4)
                        for h in range(SH):
                            dve.wait_ge(idx_ps_done, (2 * again + g) * SH + h + 1)
                            ins = dve.tensor_scalar(le[:, h, :, :], bank[2 * h + g][:, :].rearrange("p (e t) -> p e t", e=4),
                                                    slot_no[:, h:h + 1], None, ALU.is_le)
                        settle(ins)
                        settle(dve.tensor_reduce(pcount[:, :, es], le[:], X, ALU.add))
                        for h in range(SH):
                            ins = dve.scalar_tensor_tensor(idx[:, h, es], pcount[:, h, es], float(J), bank[4 + h][:, es],
                                                           ALU.mult, ALU.add)
                        ins.then_inc(idx_done, 1)

                def experts(again):
                    for e in range(E):
                        dve.wait_ge(y_ps_done, again * E + e + 1)
                        settle(dve.tensor_tensor(y[:, e], bank[6 + e % 2][:, 0:CAP].rearrange("p (h d) -> p h d", h=SH),
                                                 b2_rows[:, e, :].unsqueeze(1).broadcast_to([P, SH, D]), ALU.add))
                        dve.tensor_tensor(y[:, e], y[:, e], xin[:, e, :, D + e].unsqueeze(2).broadcast_to([P, SH, D]),
                                          ALU.mult).then_inc(y_done, 1)

                dve.wait_ge(ld_rc, 32)
                dve.wait_ge(prob_done, UNITS)
                threshold(0)
                settle(dve.tensor_scalar(chosenT[:], probT[:], cand[:, 0:1], None, ALU.is_ge))
                indices(0)

                settle(dve.tensor_reduce(suspect[:, 0:1], reach[:], X, ALU.max))
                settle(dve.tensor_scalar(suspect[:, 0:1], suspect[:, 0:1], 0.98 * CLAMP, None, ALU.is_gt))

                def any_false(ok, column):
                    settle(dve.tensor_reduce(suspect[:, column:column + 1], ok, X, ALU.min))
                    settle(dve.tensor_scalar(suspect[:, column:column + 1], suspect[:, column:column + 1], -1.0, 1.0, ALU.mult, ALU.add))

                settle(dve.tensor_reduce(suspect[:, 1:2], kT[:].rearrange("p b k -> p (b k)"), X, ALU.max, apply_absolute_value=True))
                settle(dve.tensor_reduce(suspect[:, 5:6], w_q[:, 0, :], X, ALU.max, apply_absolute_value=True))
                settle(dve.tensor_scalar(suspect[:, 5:6], suspect[:, 5:6], float(D), None, ALU.mult))
                settle(dve.tensor_tensor(suspect[:, 1:2], suspect[:, 1:2], suspect[:, 5:6], ALU.max))
                settle(dve.tensor_tensor(suspect[:, 1:2], suspect[:, 1:2], b_q[:, 0:1], ALU.max))
                settle(dve.tensor_scalar(suspect[:, 5:6], b_q[:, 0:1], -1.0, None, ALU.mult))
                settle(dve.tensor_tensor(suspect[:, 1:2], suspect[:, 1:2], suspect[:, 5:6], ALU.max))
                settle(dve.tensor_scalar(suspect[:, 1:2], suspect[:, 1:2], PART_MAX, None, ALU.is_gt))
                pr = prob[:].rearrange("p e t -> p (e t)")
                settle(dve.tensor_tensor(scratch, pr, pr, ALU.is_equal))
                any_false(scratch, 2)
                settle(dve.tensor_tensor(scratch[:, 0:NT], top0[:, :, 0], top0[:, :, 1], ALU.subtract))
                settle(dve.tensor_scalar(scratch[:, 0:NT], scratch[:, 0:NT], 16.0, None, ALU.is_lt))
                any_false(scratch[:, 0:NT], 3)
                settle(dve.tensor_scalar(suspect[:, 4:5], base[:, 2:3], -1.0, 1.0, ALU.mult, ALU.add))
                dve.tensor_reduce(suspect16[:], suspect[:, 0:5], X, ALU.max).then_inc(suspect_done, 1)
                dve.wait_ge(ld_b2, 16)
                experts(0)
                dve.wait_ge(flag_ps_done, 1)
                dve.tensor_scalar(flag[:], bank[0][0:1, 0:1], 0.5, None, ALU.is_gt).then_inc(flag_done, 1)
                dve.wait_ge(flag_done, 1)
                with dve.If(dve.value_load(flag[0:1, 0:1], min_val=0, max_val=1) > 0):
                    dve.wait_ge(y_ps_done, E)
                    start_general(dve)
                    with dve.Fori(0, NT) as i:
                        find_nan(dve, i)
                    count_nan(dve)
                    with dve.Fori(0, NT) as i:
                        run_tile(dve, i)
                    dve.wait_ge(turn, TURNS_ALL)
                    threshold(1)
                    eq = ge[:, 0]
                    gt = ge[:, 1]
                    settle(dve.tensor_scalar(chosenT[:], probT[:], cand[:, 0:1], None, ALU.is_equal))
                    dve.tensor_scalar(passing[:, 0, :], probT[:], cand[:, 0:1], None, ALU.is_gt).then_inc(chosenT_done, 1)
                    dve.wait_ge(part_ps_done, 1)
                    settle(dve.tensor_copy(eq.rearrange("p e t -> p (e t)"), bank[6][:, 0:P // 2].bitcast(BF16)))
                    settle(dve.tensor_copy(gt.rearrange("p e t -> p (e t)"), bank[7][:, 0:P // 2].bitcast(BF16)))
                    settle(dve.tensor_reduce(eqb[:].rearrange("p (e b) -> p e b", e=E), eq.rearrange("p e (b j) -> p e b j", b=B), X, ALU.add))
                    dve.tensor_reduce(gtb[:], gt, X, ALU.add).then_inc(eq_done, 1)
                    dve.wait_ge(rank_ps_done, 1)
                    settle(dve.tensor_scalar(need[:], bank[7][:, E * B:E * B + E], -1.0, float(CAP), ALU.mult, ALU.add))
                    eb = eqb[:].rearrange("p (e b) -> p e b", e=E)
                    total = bank[7][:, 0:E * B].rearrange("p (e b) -> p e b", e=E)
                    rk = rank[:].rearrange("p e (b j) -> p e b j", b=B)
                    settle(dve.tensor_tensor(rk[:, :, :, 0], bank[6][:, 0:E * B].rearrange("p (e b) -> p e b", e=E), eb, ALU.subtract))
                    for later in range(1, B):
                        for b in range(later):
                            settle(dve.tensor_tensor(rk[:, :, later, 0], rk[:, :, later, 0], total[:, :, b], ALU.add))
                    for j in range(1, J):
                        settle(dve.tensor_tensor(rk[:, :, :, j], rk[:, :, :, j - 1],
                                                 eq.rearrange("p e (b j) -> p e b j", b=B)[:, :, :, j - 1], ALU.add))
                    settle(dve.tensor_tensor(rank[:], rank[:], need[:].unsqueeze(2).broadcast_to([P, E, NT]), ALU.is_lt))
                    settle(dve.tensor_tensor(rank[:], rank[:], eq, ALU.mult))
                    dve.tensor_tensor(chosen[:], rank[:], gt, ALU.add).then_inc(chosen_done, 1)
                    dve.wait_ge(chosenT_ps_done, 1)
                    settle(dve.tensor_copy(chosenT[:], bank[6][:, 0:P // 2].bitcast(BF16)))
                    indices(1)
                    experts(1)

        @block.gpsimd
        def _(pool):
            count = [0]

            def settle(ins):
                count[0] += 1
                ins.then_inc(pool_chain, 1)
                pool.wait_ge(pool_chain, count[0])

            def ln_rstd(n, u, j0=0, j1=J):
                js = slice(j0, j1)
                pool.wait_ge(var_done[n], u + 1)
                settle(nc.gpsimd.tensor_scalar(ve[:, n, js], mv[:, n, js, 1], EPS, None, ALU.add))
                nc.gpsimd.tensor_tensor(rstd[:, n, js], ve[:, n, js], half_neg[:, js], ALU.pow).then_inc(rstd_done[n], 1)

            def ln_rstds(n, t):
                for u, j0, j1, _, _ in units(t) if 0 <= t < B else ():
                    ln_rstd(n, u, j0, j1)

            def stack_keys(b):
                nc.gpsimd.tensor_tensor(k_stack[:, b], k_parts[:, :, b, :].unsqueeze(2).broadcast_to([P, G, GH, NK]),
                                        part_mask.unsqueeze(1).unsqueeze(3).broadcast_to([P, G, GH, NK]), ALU.mult).then_inc(k_stack_done, 1)

            def residual(b):
                nc.gpsimd.tensor_tensor(res[:, b * J:(b + 1) * J, :], x[:, b * J:(b + 1) * J, :],
                                        bo_rows[:].unsqueeze(1).broadcast_to([P, J, D]), ALU.add).then_inc(res0_done, 1)

            pool.wait_ge(half_set, 1)
            ln_rstd(0, 0)
            ln_rstd(0, 1)
            pool.wait_ge(k_lo_done, 2)
            pool.wait_ge(ld_c32, 16)
            stack_keys(0)
            for n, (w, bias) in enumerate((("L0_xattn_Wv", "L0_xattn_bv"), ("L1_xattn_Wk", "L1_xattn_bk"), ("L1_xattn_Wv", "L1_xattn_bv"))):
                pool.dma_start(w_kv[0:DC, n + 1, :], a[w]).then_inc(ld_kv, 16)
                pool.dma_start(w_kv[DC:DC + 1, n + 1, :], a[bias].rearrange("(o d) -> o d", o=1)).then_inc(ld_kv, 16)
            ln_rstd(0, 2)
            stack_keys(1)
            pool.wait_ge(ld_bo, 16)
            residual(0)
            for ph in range(B + 2):
                if ph + 1 < B:
                    residual(ph + 1)
                    if ph >= 1:
                        stack_keys(ph + 1)
                ln_rstds(1, ph - 1)
                if ph + 3 < B:
                    ln_rstd(0, ph + 3)
                if ph == B:
                    ln_rstds(2, ph - 1)
                    ln_rstds(3, ph - 2)
                else:
                    ln_rstds(3, ph - 2)
                    ln_rstds(2, ph - 1)
            flat = out.rearrange("b t d -> (b t) d")

            def experts(again):
                for e in range(E):
                    pool.wait_ge(idx_done, 2 * again + e // 4 + 1)
                    for h in range(SH):
                        nc.gpsimd.indirect_dma_start(xin[:, e, h, :], None, gather_rows, bass.IndirectOffsetOnAxis(idx[:, h, e:e + 1], 0),
                                                     bounds_check=B * T - 1, oob_is_err=False).then_inc(got[e], 16)
                for e in range(E):
                    n = again * E + e
                    pool.wait_ge(y_done, n + 1)
                    if n >= 1:
                        pool.wait_ge(out_add, 16 * SH * n)
                    for h in range(SH):
                        nc.gpsimd.indirect_dma_start(flat, bass.IndirectOffsetOnAxis(idx[:, h, e:e + 1], 0), y[:, e, h, :], None,
                                                     bounds_check=B * T - 1, oob_is_err=True, compute_op=ALU.add).then_inc(out_add, 16)
                pool.wait_ge(out_add, 16 * SH * E * (again + 1))

            for b in range(B):
                pool.wait_ge(rows_out[b], 16)
            pool.wait_ge(out_base, 16 * B)
            pool.wait_ge(o_ps_done, B)
            experts(0)
            pool.wait_ge(flag_done, 1)
            with pool.If(pool.value_load(flag[0:1, 0:1], min_val=0, max_val=1) > 0):
                start_general(pool)
                with pool.Fori(0, NT) as i:
                    find_nan(pool, i)
                with pool.Fori(0, NT) as i:
                    run_tile(pool, i)
                experts(1)


_INS = ["x", "ctx_768", "L0_xattn_Wq", "L0_xattn_bq", "L0_xattn_Wk", "L0_xattn_bk", "L0_xattn_Wv", "L0_xattn_bv",
        "L0_xattn_Wo", "L0_xattn_bo", "L0_ffn_Ws1", "L0_ffn_Ws2", "L0_ffn_W1", "L0_ffn_W2", "L0_ffn_Wr",
        "L1_xattn_Wq", "L1_xattn_bq", "L1_xattn_Wk", "L1_xattn_bk", "L1_xattn_Wv", "L1_xattn_bv",
        "L1_ffn_Ws", "L1_ffn_bs", "L1_ffn_W1", "L1_ffn_b1", "L1_ffn_W2", "L1_ffn_b2"]


def kernel(**inputs):
    import concourse.bacc as bacc
    from concourse.bass_utils import run_bass_kernel_spmd

    nc = bacc.Bacc("TRN2", target_bir_lowering=False, num_devices=1)
    arrays, args = {}, {}
    for name, v in [(n, np.ascontiguousarray(inputs[n])) for n in _INS] + list(constants().items()):
        arrays[f"in_{name}"] = v
        args[name] = nc.dram_tensor(f"in_{name}", v.shape, mybir.dt.from_np(v.dtype), kind="ExternalInput").ap()
    out = nc.dram_tensor("out_0", (B, T, D), F32, kind="ExternalOutput").ap()
    program(nc, args, out)
    r = run_bass_kernel_spmd(nc, [arrays], core_ids=[0])
    return r.results[0]["out_0"]
```
